# Optimizing a Trainium2 kernel written in Bass

```python
import numpy as np
import jax
import jax.numpy as jnp

def _softmax(x, axis=-1):
    return jax.nn.softmax(x, axis=axis)

def _gelu(x):
    return jax.nn.gelu(x, approximate=True)

def _silu(x):
    return jax.nn.silu(x)

def _sigmoid(x):
    return jax.nn.sigmoid(x)

def _layernorm(x, axis=-1, eps=1e-05):
    m = jnp.mean(x, axis=axis, keepdims=True)
    v = jnp.var(x, axis=axis, keepdims=True)
    return (x - m) / jnp.sqrt(v + eps)

def _scatter_add(tgt, idx, src, axis=0):
    return tgt.at[idx].add(src)

def _segment_sum(src, seg, n):
    return jax.ops.segment_sum(src, seg, n)
kernel_name = 'mk_adaln_d1_jaxref_r4_8b40f5'

def setup_inputs(seed: int=0):
    np.random.seed(seed)
    _w = jnp.asarray

    def _L0_attn_setup():
        import jax, jax.numpy as jnp
        import numpy as np
        EPS = 1e-08

        def unit_projection(x):
            f = jnp.fft.fft(x)
            f = f / (jnp.abs(f) + EPS)
            return jnp.fft.ifft(f).real

        def bind(a, b):
            return jnp.fft.ifft(jnp.fft.fft(a) * jnp.fft.fft(b)).real

        def unbind(s, a):
            return jnp.fft.ifft(jnp.fft.fft(s) * jnp.conj(jnp.fft.fft(a))).real
        key = jax.random.key(seed)
        B, S, D = (4, 1024, 256)
        ks = jax.random.split(key, 7)
        scale = 1.0 / np.sqrt(D)
        x = jax.random.normal(ks[0], (B, S, D), dtype=jnp.float32)
        Wq = jax.random.uniform(ks[1], (D, D), jnp.float32, -scale, scale)
        bq = jax.random.uniform(ks[2], (D,), jnp.float32, -scale, scale)
        Wk = jax.random.uniform(ks[3], (D, D), jnp.float32, -scale, scale)
        bk = jax.random.uniform(ks[4], (D,), jnp.float32, -scale, scale)
        Wv = jax.random.uniform(ks[5], (D, D), jnp.float32, -scale, scale)
        bv = jax.random.uniform(ks[6], (D,), jnp.float32, -scale, scale)
        return {'x': x, 'Wq': Wq, 'bq': bq, 'Wk': Wk, 'bk': bk, 'Wv': Wv, 'bv': bv}
    _L0_attn_in = _L0_attn_setup()

    def _L0_ffn_setup():
        import jax, jax.numpy as jnp
        import numpy as np
        ALPHA = 1.702
        LIMIT = 9.0
        TOP_K = 2

        def swiglu(x):
            g, v = (x[..., 0::2], x[..., 1::2])
            g = jnp.clip(g, None, LIMIT)
            v = jnp.clip(v, -LIMIT, LIMIT)
            return g * jax.nn.sigmoid(ALPHA * g) * (v + 1)
        key = jax.random.key(seed)
        ks = jax.random.split(key, 6)
        B, L, D = (2, 512, 256)
        E, F = (8, 512)
        s_gate = 1.0 / np.sqrt(D)
        s1 = 1.0 / np.sqrt(D)
        s2 = 1.0 / np.sqrt(F)
        return {'x': jax.random.normal(ks[0], (B, L, D), dtype=jnp.float32), 'gate_w': jax.random.normal(ks[1], (D, E), dtype=jnp.float32) * s_gate, 'dense_1_w': jax.random.normal(ks[2], (E, 2 * F, D), dtype=jnp.float32) * s1, 'dense_1_b': jnp.zeros((E, 2 * F), dtype=jnp.float32), 'dense_2_w': jax.random.normal(ks[3], (E, D, F), dtype=jnp.float32) * s2, 'dense_2_b': jnp.zeros((E, D), dtype=jnp.float32)}
    _L0_ffn_in = _L0_ffn_setup()
    _L0_c = _w((lambda *s: np.random.randn(*s).astype(np.float32) * 0.05)(4, 256))
    _L0_wmod = _w((lambda *s: np.random.randn(*s).astype(np.float32) * 0.05)(256, 6 * 256) * 256 ** (-0.5))
    _d = {'L0_attn_x': _L0_attn_in['x'], 'L0_attn_Wq': _L0_attn_in['Wq'], 'L0_attn_bq': _L0_attn_in['bq'], 'L0_attn_Wk': _L0_attn_in['Wk'], 'L0_attn_bk': _L0_attn_in['bk'], 'L0_attn_Wv': _L0_attn_in['Wv'], 'L0_attn_bv': _L0_attn_in['bv'], 'L0_ffn_gate_w': _L0_ffn_in['gate_w'], 'L0_ffn_dense_1_w': _L0_ffn_in['dense_1_w'], 'L0_ffn_dense_1_b': _L0_ffn_in['dense_1_b'], 'L0_ffn_dense_2_w': _L0_ffn_in['dense_2_w'], 'L0_ffn_dense_2_b': _L0_ffn_in['dense_2_b'], 'L0_c': _L0_c, 'L0_wmod': _L0_wmod}
    _x0 = _d['L0_attn_x']
    _d['L0_attn_x'] = jax.random.normal(jax.random.fold_in(jax.random.key(seed), 1), (4, 1024, 256), dtype=_x0.dtype)
    del _x0
    return _d

def reference(L0_attn_x, L0_attn_Wq, L0_attn_bq, L0_attn_Wk, L0_attn_bk, L0_attn_Wv, L0_attn_bv, L0_ffn_gate_w, L0_ffn_dense_1_w, L0_ffn_dense_1_b, L0_ffn_dense_2_w, L0_ffn_dense_2_b, L0_c, L0_wmod):

    def _L0_attn_ref(x, Wq, bq, Wk, bk, Wv, bv):
        import jax, jax.numpy as jnp
        import numpy as np
        EPS = 1e-08

        def unit_projection(x):
            f = jnp.fft.fft(x)
            f = f / (jnp.abs(f) + EPS)
            return jnp.fft.ifft(f).real

        def bind(a, b):
            return jnp.fft.ifft(jnp.fft.fft(a) * jnp.fft.fft(b)).real

        def unbind(s, a):
            return jnp.fft.ifft(jnp.fft.fft(s) * jnp.conj(jnp.fft.fft(a))).real
        query = unit_projection(jnp.einsum('bsd,ed->bse', x, Wq) + bq)
        keys = unit_projection(jnp.einsum('bsd,ed->bse', x, Wk) + bk)
        values = unit_projection(jnp.einsum('bsd,ed->bse', x, Wv) + bv)
        x_k = bind(keys, values)
        s = jnp.cumsum(x_k, axis=1)
        out = unbind(s, query)
        return out

    def _L0_ffn_ref(x, gate_w, dense_1_w, dense_1_b, dense_2_w, dense_2_b):
        import jax, jax.numpy as jnp
        import numpy as np
        ALPHA = 1.702
        LIMIT = 9.0
        TOP_K = 2

        def swiglu(x):
            g, v = (x[..., 0::2], x[..., 1::2])
            g = jnp.clip(g, None, LIMIT)
            v = jnp.clip(v, -LIMIT, LIMIT)
            return g * jax.nn.sigmoid(ALPHA * g) * (v + 1)
        B, L, D = x.shape
        xf = x.reshape(B * L, D)
        gate = xf @ gate_w
        weights, sel = jax.lax.top_k(gate, k=TOP_K)
        weights = jax.nn.softmax(weights, axis=-1)
        h = jnp.einsum('ecd,td->tec', dense_1_w, xf) + dense_1_b[None]
        h = swiglu(h)
        y = jnp.einsum('edf,tef->ted', dense_2_w, h) + dense_2_b[None]
        y_sel = jnp.take_along_axis(y, sel[:, :, None], axis=1)
        out = jnp.einsum('tkd,tk->td', y_sel, weights)
        return out.reshape(B, L, D)
    x = L0_attn_x
    mod = (_silu(L0_c) @ L0_wmod).reshape(L0_c.shape[0], 6, 1, -1)
    sa, ca, ga, sb, cb, gb = (mod[:, 0], mod[:, 1], mod[:, 2], mod[:, 3], mod[:, 4], mod[:, 5])
    ga = (2 * (ga >= 0) - 1) * jnp.maximum(jnp.abs(ga), 0.25)
    gb = (2 * (gb >= 0) - 1) * jnp.maximum(jnp.abs(gb), 0.25)
    h = _layernorm(x, axis=-1) * (1 + ca) + sa
    x = x + ga * _L0_attn_ref(h, L0_attn_Wq, L0_attn_bq, L0_attn_Wk, L0_attn_bk, L0_attn_Wv, L0_attn_bv)
    h = _layernorm(x, axis=-1) * (1 + cb) + sb
    x = x + gb * _L0_ffn_ref(h, L0_ffn_gate_w, L0_ffn_dense_1_w, L0_ffn_dense_1_b, L0_ffn_dense_2_w, L0_ffn_dense_2_b)
    return x

_drawn_inputs = setup_inputs


def setup_inputs(seed=0):
    import zlib

    import numpy as np

    out = dict(_drawn_inputs(seed))
    spreads = {'L0_ffn_dense_1_b': (0.0, 0.431), 'L0_ffn_dense_2_b': (0.0, 0.512)}
    factors = {}
    for name, (base, spread) in spreads.items():
        noise = np.random.default_rng([zlib.crc32(name.encode()), seed]).standard_normal(out[name].shape)
        drawn = base * np.exp(spread * noise) if base else spread * noise
        out[name] = jnp.asarray(drawn.astype(out[name].dtype))
    for name, factor in factors.items():
        out[name] = (out[name] * factor).astype(out[name].dtype)
    return out
```

```python
from contextlib import ExitStack

import numpy as np

import concourse.bass as bass
from concourse import mybir

ALU = mybir.AluOpType
ACT = mybir.ActivationFunctionType
F32 = mybir.dt.float32
BF16 = mybir.dt.bfloat16
I32 = mybir.dt.int32
U32 = mybir.dt.uint32
AX_X = mybir.AxisListType.X

P = 128
BATCH, SEQ, D = 4, 1024, 256
TOKENS = BATCH * SEQ
KD = D // P
EXPERTS, HID = 8, 512
KF = HID // P
TOP_K = 2
BLK = 512
NBLK = TOKENS // BLK
TPB = BLK // P
TILES = TOKENS // P
PAIRS = TOKENS * TOP_K
PCOLS = PAIRS // P
MOE_TILES = PAIRS // P + EXPERTS - 1
EPS_UNIT, EPS_LN = 1e-8, 1e-5
ALPHA, LIMIT = 1.702, 9.0
KEY, VAL, QRY = 0, 1, 2
RE, IM = 0, 1


def psum_plan():
    items = []
    for t in range(-1, NBLK + 1):
        if t + 1 < NBLK:
            items += [("z", t + 1, i) for i in range(6)] + [("ny", t + 1, 0)]
        if 0 <= t < NBLK:
            items.append(("pre", t, 0))
        if t >= 1:
            items.append(("gate", t - 1, 0))
        if 0 <= t < NBLK:
            items.append(("row", t, 0))
    return {item: n for n, item in enumerate(items)}, items


def adaln_moe_kernel(nc, x, wqkv, bqkv, gate_w, w1, b1, w2, b2, c_t, wmod, dft, idft, ident, tri, iota, out):
    place, order = psum_plan()
    ROT = 4
    x_scratch = nc.dram_tensor("x_scratch", (TOKENS, D), F32).ap()
    h_scratch = nc.dram_tensor("h_scratch", (TOKENS, D), F32).ap()
    y_scratch = nc.dram_tensor("y_scratch", (PAIRS, D), F32).ap()

    x_blk = x.rearrange("(t j p) d -> t p j d", p=P, j=TPB)
    xs_blk = x_scratch.rearrange("(t j p) d -> t p j d", p=P, j=TPB)
    hs_blk = h_scratch.rearrange("(t j p) d -> t p j d", p=P, j=TPB)
    y_blk = y_scratch.rearrange("(k t j p) d -> k t p j d", p=P, j=TPB, k=TOP_K)
    out_blk = out.rearrange("(t j p) d -> t p j d", p=P, j=TPB)

    with ExitStack() as ctx:
        def sb(name, shape, dt=F32):
            return ctx.enter_context(nc.sbuf_tensor(name, shape, dt))

        def sem(name):
            return ctx.enter_context(nc.semaphore(name))

        def sems(name, n):
            return [sem(f"{name}{i}") for i in range(n)]

        w1_sb = sb("w1_sb", [P, EXPERTS * KD * 2 * HID])
        ident_sb = sb("ident_sb", [P, P])
        iota_all = sb("iota_all", [P, P + 1])
        iota_sb = iota_all[:, 0:P]
        pcol = iota_all[:, P:P + 1]
        gb_bc = sb("gb_bc", [P, BATCH, D])
        gates = sb("gates", [P, TILES, EXPERTS])

        REGION = 35200
        region = sb("region", [P, REGION])
        cursor = [0]

        def carve(n):
            cursor[0] += n
            assert cursor[0] <= REGION, cursor
            return region[:, cursor[0] - n:cursor[0]]

        XS = 4
        x_sb = carve(XS * TPB * D).rearrange("p (s j d) -> p s j d", s=XS, j=TPB)
        n_sb = carve(TPB * D).rearrange("p (j d) -> p j d", j=TPB)
        h_t = carve(KD * BLK).rearrange("p (k n) -> p k n", k=KD)
        z_flat = carve(2 * 6 * BLK)
        z = z_flat.rearrange("p (s c r n) -> p s c r n", s=2, c=3, r=2)
        sq = carve(6 * BLK).rearrange("p (c r n) -> p c r n", c=3, r=2)
        m_flat = carve(2 * 3 * BLK)
        mag = m_flat.rearrange("p (s c n) -> p s c n", s=2, c=3)
        den = carve(BLK)
        rec = carve(BLK)
        uk = carve(2 * BLK).rearrange("p (r n) -> p r n", r=2)
        p_flat = carve(4 * BLK)
        prod = p_flat.rearrange("p (a r n) -> p a r n", a=2, r=2)
        s_flat = carve(4 * BLK)
        s_run = s_flat.rearrange("p (s r n) -> p s r n", s=2, r=2)
        x2 = carve(TPB * D).rearrange("p (j d) -> p j d", j=TPB)
        h2 = carve(TPB * D).rearrange("p (j d) -> p j d", j=TPB)
        mod_bc = carve(BATCH * 3 * D).rearrange("p (b m d) -> p b m d", b=BATCH, m=3)
        NF = 2 * P + 1
        w_spec = carve(3 * KD * NF).rearrange("p (c k f) -> p c k f", c=3, k=KD)
        idft_sb = carve(2 * D).rearrange("p (r d) -> p r d", r=2)
        idft_ga = carve(2 * 2 * D).rearrange("p (s r d) -> p s r d", s=2, r=2)
        gate_sb = carve(KD * EXPERTS).rearrange("p (k e) -> p k e", k=KD)
        tri_sb = carve(2 * P).rearrange("p (a n) -> p a n", a=2)
        bias_f = carve(9)
        sca_t = carve(4 * BATCH).rearrange("p (w k b) -> p w k b", w=2, k=KD)
        stats = carve(2 * TPB * 6).rearrange("p (w j s) -> p w j s", w=2, j=TPB)
        mv = carve(2 * TPB * 2).rearrange("p (w j s) -> p w j s", w=2, j=TPB)
        mv1 = carve(2 * TPB * 2).rearrange("p (s j a) -> p s j a", s=2, j=TPB)
        rstd = carve(3 * TPB).rearrange("p (w j) -> p w j", w=3)
        ny = carve(3 * TPB).rearrange("p (j c) -> p j c", j=TPB)
        ny_abs = carve(3 * TPB).rearrange("p (j c) -> p j c", j=TPB)
        ny_unit = carve(3 * TPB).rearrange("p (j c) -> p j c", j=TPB)
        ny_kv = carve(TPB)
        ny_tot = carve(2 * (TPB + 1)).rearrange("p (s j) -> p s j", s=2)
        ny_pre = carve(TPB)
        ny_g = carve(TPB)
        wmod_sb = z_flat[:, 0:KD * 6 * D].rearrange("p (k n) -> p k n", k=KD)
        mod_tmp = s_flat[:, 0:BATCH * D].rearrange("p (b d) -> p b d", b=BATCH)
        wraw = m_flat[:, 0:3 * KD * D].rearrange("p (c k d) -> p c k d", c=3, k=KD)
        silu_rep = p_flat[:, 0:KD * BATCH * P].rearrange("p (k b m) -> p k b m", k=KD, b=BATCH)
        dft_sb = uk[:, :, :].rearrange("p r n -> p (r n)")[:, 0:KD * NF].rearrange("p (k f) -> p k f", k=KD)
        alt_rep = den[:, 0:P]
        bq_sb = rec[:, 0:KD * 3].rearrange("p (k c) -> p k c", k=KD)
        c_sb = rec[:, 16:16 + KD * BATCH].rearrange("p (k b) -> p k b", k=KD)
        c_sig = rec[:, 32:32 + KD * BATCH].rearrange("p (k b) -> p k b", k=KD)
        c_silu = rec[:, 48:48 + KD * BATCH].rearrange("p (k b) -> p k b", k=KD)

        cursor[0] = 0
        w2_sb = carve(EXPERTS * KF * D)
        b1_bc = carve(EXPERTS * 2 * HID)
        b2_bc = carve(EXPERTS * D)
        route_lo = cursor[0]
        NX = 3
        xg = carve(2 * D).rearrange("p (s d) -> p s d", s=2)
        xg_t = carve(2 * D).rearrange("p (s d) -> p s d", s=2)
        gv = carve(2 * 2 * HID).rearrange("p (s a f) -> p s a f", s=2, a=2)
        sig = carve(HID)
        hid_t = carve(2 * HID).rearrange("p (s f) -> p s f", s=2)
        y_sb = carve(2 * D).rearrange("p (s d) -> p s d", s=2)
        gather_idx = carve(MOE_TILES).bitcast(I32)
        scatter_idx = carve(MOE_TILES).bitcast(I32)
        tile_expert = carve(MOE_TILES).bitcast(I32)
        gather_now = carve(2).bitcast(I32)
        scatter_now = carve(2).bitcast(I32)
        pair_w = carve(PCOLS).rearrange("p (k t) -> p k t", k=TOP_K)
        cursor[0] = EXPERTS * KF * D
        best = carve(TILES * 8).rearrange("p (t e) -> p t e", e=8)
        best_i = carve(TILES * 8).bitcast(U32).rearrange("p (t e) -> p t e", e=8)
        pick = carve(PCOLS)
        onehot = carve(PCOLS * EXPERTS).rearrange("p (c e) -> p c e", e=EXPERTS)
        onehot_b = carve(PCOLS * EXPERTS // 2).bitcast(BF16)
        rank = carve(PCOLS * EXPERTS)
        tot = carve(PCOLS * EXPERTS).rearrange("p (c e) -> p c e", e=EXPERTS)
        cum = carve(EXPERTS * (PCOLS + 1)).rearrange("p (e c) -> p e c", e=EXPERTS)
        small = carve(16 * EXPERTS).rearrange("p (a e) -> p a e", e=EXPERTS)
        slot = carve(PCOLS)
        slot_i = carve(2 * PCOLS).bitcast(I32).rearrange("p (a c) -> p a c", a=2)
        slot_hl = carve(2 * PCOLS).rearrange("p (a c) -> p a c", a=2)
        tri_b = carve(P).bitcast(BF16).rearrange("p (a n) -> p a n", a=2)
        pw_tmp = carve(2 * TILES).rearrange("p (a t) -> p a t", a=2)
        lo_hot = carve(2 * P // 2).bitcast(BF16).rearrange("p (s n) -> p s n", s=2)
        hi_hot = carve(2 * MOE_TILES).bitcast(BF16).rearrange("p (s a n) -> p s a n", s=2, a=2)
        te_cmp = carve(MOE_TILES * EXPERTS).rearrange("p (i e) -> p i e", e=EXPERTS)
        perm = carve(4 * MOE_TILES).rearrange("p (a i) -> p a i", a=4)
        strict_f = carve(P)
        assert cursor[0] <= route_lo, (cursor, route_lo)
        cursor[0] = 0
        d_y = carve(2 * 2 * TPB * D).rearrange("p (s k j d) -> p s k j d", s=2, k=2, j=TPB)
        d_x = carve(2 * TPB * D).rearrange("p (s j d) -> p s j d", s=2, j=TPB)

        ps = ctx.enter_context(nc.psum_tensor("ps", [P, 8, 512], F32))
        TP, OUT, ROT0 = 0, 2, 4

        def rot(item):
            return ps[:, ROT0 + place[item] % ROT, :]

        const_in, wmod_in, wraw_in, w1_in, w2_in, bias_in = (sem(n) for n in (
            "const_in", "wmod_in", "wraw_in", "w1_in", "w2_in", "bias_in"))
        x_in = sems("x_in", XS)
        x2_out, h2_out = sem("x2_out"), sem("h2_out")
        (sig_done, silu_done, rep_done, pe_setup, act_setup, mod_mm, mod_copied, mod_ready, ga_ready,
         ln1_stats, ln1_agg, ln1_var, ln1_std, ln1_rstd, n_ready, tp_done, ht_ready, z_mm, z_ready, sq_ready,
         mag_ready, root_ready, eps_ready, den_ready, all_ready, rec_ready, rkv_ready, rq_ready, uk_ready,
         prod_ready, scan_ready, uq_ready, x1_ready, g_ready, nymm, ny_read, ny_absd, ny_rec, ny_unitd, ny_kvd,
         pre_mm, tot_read, ny_sum, ny_done, row_mm, row_ready, idft_done, x2_ready, ln2_stats,
         ln2_agg, ln2_var, ln2_std, ln2_rstd, h2_mid, h2_ready, tp2_done, h2t_ready, gate_mm, gate_ready) = (
            sem(n) for n in (
                "sig_done silu_done rep_done pe_setup act_setup mod_mm mod_copied mod_ready ga_ready "
                "ln1_stats ln1_agg ln1_var ln1_std ln1_rstd n_ready tp_done ht_ready z_mm z_ready sq_ready "
                "mag_ready root_ready eps_ready den_ready all_ready rec_ready rkv_ready rq_ready uk_ready "
                "prod_ready scan_ready uq_ready x1_ready g_ready nymm ny_read ny_absd ny_rec ny_unitd ny_kvd "
                "pre_mm tot_read ny_sum ny_done row_mm row_ready idft_done x2_ready ln2_stats "
                "ln2_agg ln2_var ln2_std ln2_rstd h2_mid h2_ready tp2_done h2t_ready gate_mm gate_ready").split())
        (route, cast_done, rank_mm, w_exp, hi_made, perm_mm, tiles_ready, w_sub) = (
            sem(n) for n in "route cast_done rank_mm w_exp hi_made perm_mm tiles_ready w_sub".split())
        gathered = sems("gathered", 2)
        scattered = sems("scattered", 2)
        gather_set, scatter_set, pool_turn = sem("gather_set"), sem("scatter_set"), sem("pool_turn")
        (xg_tp, xgt_ready, up_done, gv_ready, clip_done, sig_ready, glu_ready, hid_ready, hid_tp, hidt_ready,
         down_done, y_ready) = (sem(n) for n in (
            "xg_tp xgt_ready up_done gv_ready clip_done sig_ready glu_ready hid_ready hid_tp hidt_ready "
            "down_done y_ready").split())
        d_in, d_out = sems("d_in", 2), sems("d_out", 2)
        d_w1, d_w2, d_gb, d_ready = (sem(n) for n in "d_w1 d_w2 d_gb d_ready".split())

        block = ctx.enter_context(nc.Block())

        def bank_free(e, item):
            n = place[item] - ROT
            if n >= 0:
                kind, t, i = order[n]
                s, v = {"z": (z_ready, 6 * t + i + 1), "ny": (ny_read, t + 1), "pre": (ny_sum, 2 * t + 2),
                        "gate": (gate_ready, t + 1), "row": (row_ready, t + 1)}[kind]
                e.wait_ge(s, v)

        @block.sync
        def _(sp):
            sp.dma_start(c_sb, c_t).then_inc(const_in, 16)
            sp.dma_start(dft_sb, dft[:, :, 0:NF]).then_inc(const_in, 16)
            sp.dma_start(alt_rep, tri[:, 3, :]).then_inc(const_in, 16)
            sp.dma_start(bq_sb, bqkv).then_inc(const_in, 16)
            sp.dma_start(ident_sb[:], ident).then_inc(const_in, 16)
            sp.dma_start(iota_all[:], iota).then_inc(const_in, 16)
            sp.dma_start(idft_sb, idft).then_inc(const_in, 16)
            sp.dma_start(gate_sb, gate_w).then_inc(const_in, 16)
            sp.dma_start(tri_sb, tri[:, 0:2, :]).then_inc(const_in, 16)
            sp.dma_start(wraw, wqkv).then_inc(wraw_in, 16)
            sp.dma_start(wmod_sb, wmod).then_inc(wmod_in, 16)
            for t in range(XS):
                sp.dma_start(x_sb[:, t], x_blk[t]).then_inc(x_in[t], 16)
            sp.dma_start(w1_sb[:], w1).then_inc(w1_in, 16)
            for t in range(NBLK):
                sp.wait_ge(x2_ready, t + 1)
                sp.dma_start(xs_blk[t], x2).then_inc(x2_out, 16)
                if t + XS < NBLK:
                    sp.dma_start(x_sb[:, (t + XS) % XS], x_blk[t + XS]).then_inc(x_in[t % XS], 16)
                sp.wait_ge(h2_ready, TPB * (t + 1))
                sp.dma_start(hs_blk[t], h2).then_inc(h2_out, 16)
            sp.wait_ge(gate_ready, NBLK)
            sp.wait_ge(x2_out, 16 * NBLK)
            sp.wait_ge(h2_out, 16 * NBLK)
            sp.dma_start(w2_sb, w2).then_inc(w2_in, 16)
            sp.wait_ge(tiles_ready, 4)
            sp.dma_start(b1_bc, b1.partition_broadcast(P)).then_inc(bias_in, 16)
            sp.dma_start(b2_bc, b2.partition_broadcast(P)).then_inc(bias_in, 16)
            for t in range(NBLK):
                s = t % 2
                if t == 0:
                    sp.wait_ge(y_ready, MOE_TILES + 1)
                    for i in range(2):
                        sp.wait_ge(scattered[i], 16 * ((MOE_TILES + 1 - i) // 2))
                if t >= 2:
                    sp.wait_ge(d_out[s], 16 * (t // 2))
                for k in range(TOP_K):
                    sp.dma_start(d_y[:, s, k], y_blk[k, t]).then_inc(d_in[s], 16)
                sp.dma_start(d_x[:, s], xs_blk[t]).then_inc(d_in[s], 16)
                if t >= 1:
                    sp.wait_ge(d_ready, t)
                    sp.dma_start(out_blk[t - 1], d_x[:, 1 - s]).then_inc(d_out[1 - s], 16)
            sp.wait_ge(d_ready, NBLK)
            sp.dma_start(out_blk[NBLK - 1], d_x[:, (NBLK - 1) % 2]).then_inc(d_out[(NBLK - 1) % 2], 16)
            for i in range(2):
                sp.wait_ge(d_out[i], 16 * (NBLK // 2))

        @block.tensor
        def _(pe):
            def transform_weights():
                pe.wait_ge(const_in, 144)
                pe.wait_ge(wraw_in, 16)
                for c in range(3):
                    for kd in range(KD):
                        for ke in range(KD):
                            mm = pe.matmul(ps[:, c * KD + kd, 0:NF], wraw[:, c, ke, kd * P:(kd + 1) * P],
                                           dft_sb[:, ke, :], start=(ke == 0), stop=(ke == KD - 1))
                        mm.then_inc(pe_setup, 1)
                for r in range(3):
                    for ke in range(KD):
                        lhs = dft_sb[:, ke, r * P:(r + 1) * P] if r < 2 else alt_rep
                        mm = pe.matmul(ps[:, 6, 3 * r:3 * r + 3], lhs, bq_sb[:, ke, :],
                                       start=(ke == 0), stop=(ke == KD - 1))
                mm.then_inc(pe_setup, 1)
                pe.wait_ge(wmod_in, 16)
                pe.wait_ge(silu_done, 1)
                for w in range(2):
                    for kd in range(KD):
                        for ke in range(KD):
                            at = w * D + kd * P
                            mm = pe.matmul(ps[:, 7, (w * KD + kd) * BATCH:(w * KD + kd + 1) * BATCH],
                                           wmod_sb[:, ke, at:at + P], c_silu[:, ke, :],
                                           start=(ke == 0), stop=(ke == KD - 1))
                mm.then_inc(pe_setup, 1)

            def broadcast_modulation():
                pe.wait_ge(rep_done, 1)
                for b in range(BATCH):
                    for half in range(2):
                        n = 2 * b + half
                        pe.wait_ge(act_setup, n + 1)
                        for ke in range(KD):
                            mm = pe.matmul(ps[:, n, :], silu_rep[:, ke, b, :],
                                           wmod_sb[:, ke, (2 + 2 * half) * D:(4 + 2 * half) * D],
                                           start=(ke == 0), stop=(ke == KD - 1))
                        mm.then_inc(mod_mm, 1)
                pe.wait_ge(mod_copied, 2 * BATCH)

            def transpose_rows(src, t, done):
                for k in range(KD):
                    for j in range(TPB):
                        mm = pe.transpose(ps[:, TP + k, j * P:(j + 1) * P], src[:, j, k * P:(k + 1) * P],
                                          ident_sb[:])
                    mm.then_inc(done, 1)

            def project(t):
                pe.wait_ge(n_ready, TPB * (t + 1))
                if t >= 1:
                    pe.wait_ge(ht_ready, KD * t)
                if t >= 3:
                    pe.wait_ge(h2t_ready, KD * (t - 2))
                transpose_rows(n_sb, t, tp_done)
                pe.wait_ge(ht_ready, KD * (t + 1))
                for i in range(6):
                    c, r = i // 2, i % 2
                    bank_free(pe, ("z", t, i))
                    for k in range(KD):
                        mm = pe.matmul(rot(("z", t, i)), w_spec[:, c, k, r * P:(r + 1) * P], h_t[:, k, :],
                                       start=(k == 0), stop=(k == KD - 1))
                    mm.then_inc(z_mm, 1)
                bank_free(pe, ("ny", t, 0))
                for j in range(TPB):
                    for k in range(KD):
                        mm = pe.matmul(rot(("ny", t, 0))[:, 3 * j:3 * j + 3], h_t[:, k, j * P:(j + 1) * P],
                                       w_spec[:, :, k, 2 * P], start=(k == 0), stop=(k == KD - 1))
                mm.then_inc(nymm, 1)

            def nyquist_sums(t):
                pe.wait_ge(ny_kvd, t + 1)
                bank_free(pe, ("pre", t, 0))
                pe.matmul(rot(("pre", t, 0))[:, 0:TPB], tri_sb[:, 0, :], ny_kv, start=True, stop=True)
                pe.matmul(rot(("pre", t, 0))[:, TPB:2 * TPB], tri_sb[:, 1, :], ny_kv, start=True,
                          stop=True).then_inc(pre_mm, 1)

            def gate(t):
                pe.wait_ge(h2_ready, TPB * (t + 1))
                pe.wait_ge(ht_ready, KD * min(t + 3, NBLK))
                transpose_rows(h2, t, tp2_done)
                pe.wait_ge(h2t_ready, KD * (t + 1))
                bank_free(pe, ("gate", t, 0))
                for j in range(TPB):
                    for k in range(KD):
                        mm = pe.matmul(rot(("gate", t, 0))[:, j * EXPERTS:(j + 1) * EXPERTS],
                                       h_t[:, k, j * P:(j + 1) * P], gate_sb[:, k, :],
                                       start=(k == 0), stop=(k == KD - 1))
                mm.then_inc(gate_mm, 1)

            def nyquist_row(t):
                pe.wait_ge(ny_done, t + 1)
                bank_free(pe, ("row", t, 0))
                for j in range(TPB):
                    mm = pe.transpose(rot(("row", t, 0))[0:1, j * P:(j + 1) * P], ny_g[:, j:j + 1], ident_sb[:])
                mm.then_inc(row_mm, 1)

            def inverse(t):
                pe.wait_ge(row_ready, t + 1)
                pe.wait_ge(g_ready, 2 * (t + 1))
                pe.wait_ge(ga_ready, t // 2 + 1)
                if t >= 1:
                    pe.wait_ge(x2_ready, t)
                for j in range(TPB):
                    for r in range(2):
                        mm = pe.matmul(ps[:, OUT + j // 2, (j % 2) * D:(j % 2 + 1) * D],
                                       prod[:, 0, r, j * P:(j + 1) * P], idft_ga[:, (t // 2) % 2, r, :],
                                       start=(r == 0), stop=(r == 1))
                mm.then_inc(idft_done, 1)

            transform_weights()
            broadcast_modulation()
            for t in range(-1, NBLK + 1):
                if t + 1 < NBLK:
                    project(t + 1)
                if 0 <= t < NBLK:
                    nyquist_sums(t)
                if t >= 1:
                    gate(t - 1)
                if 0 <= t < NBLK:
                    nyquist_row(t)
                    inverse(t)

            pe.wait_ge(cast_done, 1)
            pe.matmul(ps[:, 0, :], tri_b[:, 0, :], onehot_b, start=True, stop=True)
            pe.matmul(ps[:, 1, :], tri_b[:, 1, :], onehot_b, start=True, stop=True).then_inc(rank_mm, 1)
            for c in range(PCOLS):
                pe.wait_ge(hi_made, 2 * (c + 1))
                pe.matmul(ps[:, 2, 0:2 * MOE_TILES], lo_hot[:, c % 2, :],
                          hi_hot[:, c % 2].rearrange("p a n -> p (a n)"),
                          start=(c == 0), stop=(c == PCOLS - 1)).then_inc(perm_mm, 1)

            XT, HT, YB, GV = 0, 1, 2, 4

            def rows_in(i, s, wait):
                pe.wait_ge(gathered[s], wait)
                for k in range(KD):
                    mm = pe.transpose(ps[:, XT, k * P:(k + 1) * P], xg[:, s, k * P:(k + 1) * P], ident_sb[:])
                mm.then_inc(xg_tp, 1)

            def up(i, s):
                e = pe.value_load(tile_expert[0:1, bass.ds(i, 1)], min_val=0, max_val=EXPERTS - 1)
                pe.wait_ge(xgt_ready, i + 1)
                for a in range(2):
                    for k in range(KD):
                        mm = pe.matmul(ps[:, GV + 2 * s + a, :], xg_t[:, s, k * P:(k + 1) * P],
                                       w1_sb[:, bass.ds(e * (KD * 2 * HID) + (k * 2 + a) * HID, HID)],
                                       start=(k == 0), stop=(k == KD - 1))
                mm.then_inc(up_done, 1)

            def down(i, s):
                e = pe.value_load(tile_expert[0:1, bass.ds(i, 1)], min_val=0, max_val=EXPERTS - 1)
                pe.wait_ge(hid_ready, i + 1)
                for k in range(KF):
                    mm = pe.transpose(ps[:, HT, k * P:(k + 1) * P], gv[:, s, 0, k * P:(k + 1) * P], ident_sb[:])
                mm.then_inc(hid_tp, 1)
                pe.wait_ge(hidt_ready, i + 1)
                pe.wait_ge(y_ready, i + 1)
                for k in range(KF):
                    mm = pe.matmul(ps[:, YB, 0:D], hid_t[:, s, k * P:(k + 1) * P],
                                   w2_sb[:, bass.ds(e * (KF * D) + k * D, D)],
                                   start=(k == 0), stop=(k == KF - 1))
                mm.then_inc(down_done, 1)

            pe.sem_inc(down_done, 1)
            pe.wait_ge(w1_in, 16)
            pe.wait_ge(w2_in, 16)
            pe.wait_ge(tiles_ready, 4)
            rows_in(0, 0, 16)
            up(0, 0)
            with pe.Fori(0, (MOE_TILES - 1) // 2) as n:
                for s in range(2):
                    i = 2 * n + s
                    rows_in(i + 1, 1 - s, 16 * (n + 1 + s))
                    pe.wait_ge(gv_ready, i + 1)
                    up(i + 1, 1 - s)
                    down(i, s)
            down(MOE_TILES - 1, 0)

        @block.scalar
        def _(act):
            act.wait_ge(const_in, 144)
            nc.scalar.activation(c_sig, c_sb, ACT.Sigmoid).then_inc(sig_done, 1)
            for n in range(6):
                act.wait_ge(pe_setup, n + 1)
                nc.scalar.activation(w_spec[:, n // KD, n % KD, :], ps[:, n, 0:NF], ACT.Copy).then_inc(act_setup, 1)
            act.wait_ge(pe_setup, 7)
            nc.scalar.activation(bias_f, ps[:, 6, 0:9], ACT.Copy).then_inc(act_setup, 1)
            act.wait_ge(pe_setup, 8)
            nc.scalar.activation(sca_t.rearrange("p w k b -> p (w k b)"), ps[:, 7, 0:4 * BATCH],
                                 ACT.Copy).then_inc(act_setup, 1)
            for b in range(BATCH):
                act.wait_ge(mod_mm, 2 * b + 1)
                nc.scalar.activation(mod_bc[:, b, 0:2, :], ps[:, 2 * b, :].rearrange("p (m d) -> p m d", m=2),
                                     ACT.Copy).then_inc(mod_copied, 1)
                act.wait_ge(mod_mm, 2 * b + 2)
                nc.scalar.activation(mod_bc[:, b, 2, :], ps[:, 2 * b + 1, 0:D], ACT.Copy)
                nc.scalar.activation(gb_bc[:, b, :], ps[:, 2 * b + 1, D:2 * D], ACT.Copy).then_inc(mod_copied, 1)

            def project(t):
                act.wait_ge(ln1_var, t + 1)
                nc.scalar.activation(rstd[:, t % 2, :], rstd[:, t % 2, :], ACT.Sqrt).then_inc(ln1_std, 1)

            def spectra(t):
                b = t // 2
                if t == 0:
                    act.wait_ge(mod_ready, 1)
                for k in range(KD):
                    act.wait_ge(tp_done, KD * t + k + 1)
                    if k == 0 and t >= 1:
                        act.wait_ge(nymm, t)
                    if k == 0 and t >= 3:
                        act.wait_ge(gate_mm, t - 2)
                    nc.scalar.activation(h_t[:, k, :], ps[:, TP + k, :], ACT.Identity,
                                         bias=sca_t[:, 0, k, b:b + 1],
                                         scale=sca_t[:, 1, k, b:b + 1]).then_inc(ht_ready, 1)

            def evacuate(t):
                if t >= 2:
                    act.wait_ge(uq_ready, t - 1)
                    act.wait_ge(prod_ready, 2 * (t - 1))
                for i in range(6):
                    c, r = i // 2, i % 2
                    act.wait_ge(z_mm, 6 * t + i + 1)
                    nc.scalar.activation(z[:, t % 2, c, r, :], rot(("z", t, i)), ACT.Identity,
                                         bias=bias_f[:, 3 * r + c:3 * r + c + 1]).then_inc(z_ready, 1)
                if t >= 1:
                    act.wait_ge(mag_ready, t)
                for c in range(3):
                    act.wait_ge(z_ready, 6 * t + 2 * c + 2)
                    nc.scalar.activation(sq[:, c], z[:, t % 2, c], ACT.Square).then_inc(sq_ready, 1)

            def std2(t):
                act.wait_ge(ln2_var, t + 1)
                nc.scalar.activation(rstd[:, 2, :], rstd[:, 2, :], ACT.Sqrt).then_inc(ln2_std, 1)

            def roots(t):
                act.wait_ge(mag_ready, t + 1)
                nc.scalar.activation(mag[:, t % 2], mag[:, t % 2], ACT.Sqrt).then_inc(root_ready, 1)

            def gate(t):
                for k in range(KD):
                    act.wait_ge(tp2_done, KD * t + k + 1)
                    if k == 0:
                        act.wait_ge(nymm, min(t + 3, NBLK))
                    nc.scalar.activation(h_t[:, k, :], ps[:, TP + k, :], ACT.Copy).then_inc(h2t_ready, 1)
                act.wait_ge(gate_mm, t + 1)
                nc.scalar.activation(gates[:, t * TPB:(t + 1) * TPB, :],
                                     rot(("gate", t, 0))[:, 0:TPB * EXPERTS].rearrange("p (j e) -> p j e", j=TPB),
                                     ACT.Copy).then_inc(gate_ready, 1)

            def nyquist_row(t):
                act.wait_ge(row_mm, t + 1)
                act.wait_ge(g_ready, 2 * (t + 1))
                nc.scalar.activation(prod[0:1, 0, IM, :], rot(("row", t, 0))[0:1, :], ACT.Copy).then_inc(row_ready, 1)

            project(0)
            project(1)
            for t in range(-1, NBLK + 1):
                if t + 1 < NBLK:
                    spectra(t + 1)
                if t >= 1:
                    std2(t - 1)
                if t >= 0 and t + 2 < NBLK:
                    project(t + 2)
                if t + 1 < NBLK:
                    evacuate(t + 1)
                if t >= 1:
                    gate(t - 1)
                if 0 <= t < NBLK:
                    nyquist_row(t)
                if t + 1 < NBLK:
                    roots(t + 1)

            act.wait_ge(w_sub, 1)
            nc.scalar.activation(pw_tmp[:, 1, :], pw_tmp[:, 0, :], ACT.Exp).then_inc(w_exp, 1)

            def rows_in(i, s):
                act.wait_ge(xg_tp, i + 1)
                nc.scalar.activation(xg_t[:, s, :], ps[:, 0, 0:D], ACT.Copy).then_inc(xgt_ready, 1)

            def hidden(i, s):
                act.wait_ge(clip_done, i + 1)
                nc.scalar.activation(sig[:], gv[:, s, 0, :], ACT.Sigmoid, scale=ALPHA).then_inc(sig_ready, 1)
                act.wait_ge(hid_tp, i + 1)
                act.wait_ge(down_done, i + 1)
                nc.scalar.activation(hid_t[:, s, :], ps[:, 1, :], ACT.Copy).then_inc(hidt_ready, 1)

            rows_in(0, 0)
            with act.Fori(0, (MOE_TILES - 1) // 2) as n:
                for s in range(2):
                    i = 2 * n + s
                    rows_in(i + 1, 1 - s)
                    hidden(i, s)
            hidden(MOE_TILES - 1, 0)

            for t in range(NBLK):
                act.wait_ge(d_in[t % 2], 48 * (t // 2 + 1))
                for j in range(TPB):
                    nc.scalar.activation(d_y[:, t % 2, 0, j, :], d_y[:, t % 2, 0, j, :], ACT.Copy,
                                         scale=pair_w[:, 0, t * TPB + j:t * TPB + j + 1]).then_inc(d_w1, 1)

        @block.vector
        def _(dve):
            V = nc.vector
            dve.wait_ge(sig_done, 1)
            V.tensor_tensor(c_silu, c_sb, c_sig, ALU.mult).then_inc(silu_done, 1)
            dve.wait_ge(silu_done, 1)
            V.tensor_copy(silu_rep, c_silu.unsqueeze(3).to_broadcast([P, KD, BATCH, P])).then_inc(rep_done, 1)
            dve.wait_ge(act_setup, 8)
            V.tensor_scalar(sca_t[:, 1], sca_t[:, 1], 1.0, None, ALU.add).then_inc(mod_ready, 1)

            def clamp_gain(g, n):
                V.tensor_scalar(mod_tmp, g, 0.0, 2.0, ALU.is_ge, ALU.mult).then_inc(mod_ready, 1)
                dve.wait_ge(mod_ready, n + 1)
                V.scalar_tensor_tensor(out=g, in0=g, scalar=-1.0, in1=g, op0=ALU.mult,
                                       op1=ALU.max).then_inc(mod_ready, 1)
                dve.wait_ge(mod_ready, n + 2)
                V.tensor_scalar(g, g, 0.25, None, ALU.max).then_inc(mod_ready, 1)
                dve.wait_ge(mod_ready, n + 3)
                V.scalar_tensor_tensor(out=g, in0=mod_tmp, scalar=-1.0, in1=g, op0=ALU.add,
                                       op1=ALU.mult).then_inc(mod_ready, 1)
                dve.wait_ge(mod_ready, n + 4)

            def modulation():
                dve.wait_ge(mod_copied, 2 * BATCH)
                clamp_gain(mod_bc[:, :, 0, :], 1)
                clamp_gain(gb_bc[:, :, :], 5)
                V.tensor_scalar(mod_bc[:, :, 2, :], mod_bc[:, :, 2, :], 1.0, None, ALU.add).then_inc(mod_ready, 1)

            def moments(src, w, t, s_stats, s_agg, s_var, mvt, sd):
                for j in range(TPB):
                    V.bn_stats(stats[:, w, j, :], src[:, j, :]).then_inc(s_stats, 1)
                dve.wait_ge(s_stats, TPB * (t + 1))
                for j in range(TPB):
                    V.bn_aggr(mvt[:, j, :], stats[:, w, j, :]).then_inc(s_agg, 1)
                dve.wait_ge(s_agg, TPB * (t + 1))
                V.tensor_scalar(sd, mvt[:, :, 1], EPS_LN, None, ALU.add).then_inc(s_var, 1)

            def ln1_moments(t):
                dve.wait_ge(x_in[t % XS], 16 * (t // XS + 1))
                moments(x_sb[:, t % XS], 0, t, ln1_stats, ln1_agg, ln1_var, mv1[:, t % 2], rstd[:, t % 2, :])

            def ln1_rows(t):
                dve.wait_ge(ln1_std, t + 1)
                V.reciprocal(rstd[:, t % 2, :], rstd[:, t % 2, :]).then_inc(ln1_rstd, 1)
                dve.wait_ge(ln1_rstd, t + 1)
                if t >= 1:
                    dve.wait_ge(tp_done, KD * t)
                for j in range(TPB):
                    V.tensor_scalar(n_sb[:, j, :], x_sb[:, t % XS, j, :], mv1[:, t % 2, j, 0:1],
                                    rstd[:, t % 2, j:j + 1], ALU.subtract, ALU.mult).then_inc(n_ready, 1)

            def magnitudes(t):
                dve.wait_ge(sq_ready, 3 * (t + 1))
                V.tensor_tensor(mag[:, t % 2], sq[:, :, RE, :], sq[:, :, IM, :], ALU.add).then_inc(mag_ready, 1)

            def nyquist_units(t):
                dve.wait_ge(nymm, t + 1)
                V.tensor_tensor(ny, rot(("ny", t, 0))[:, 0:3 * TPB].rearrange("p (j c) -> p j c", j=TPB),
                                bias_f[:, 6:9].unsqueeze(1).to_broadcast([P, TPB, 3]), ALU.add).then_inc(ny_read, 1)
                dve.wait_ge(ny_read, t + 1)
                V.scalar_tensor_tensor(out=ny_abs, in0=ny, scalar=-1.0, in1=ny, op0=ALU.mult,
                                       op1=ALU.max).then_inc(ny_absd, 1)
                dve.wait_ge(ny_absd, 2 * t + 1)
                V.tensor_scalar(ny_abs, ny_abs, EPS_UNIT, None, ALU.add).then_inc(ny_absd, 1)
                dve.wait_ge(ny_absd, 2 * t + 2)
                V.reciprocal(ny_abs, ny_abs).then_inc(ny_rec, 1)
                dve.wait_ge(ny_rec, t + 1)
                V.tensor_tensor(ny_unit, ny, ny_abs, ALU.mult).then_inc(ny_unitd, 1)
                dve.wait_ge(ny_unitd, t + 1)
                V.tensor_tensor(ny_kv, ny_unit[:, :, KEY], ny_unit[:, :, VAL], ALU.mult).then_inc(ny_kvd, 1)

            def nyquist_apply(t):
                dve.wait_ge(pre_mm, t + 1)
                if t % 2 == 0:
                    V.memset(ny_tot[:, 0, 0:1], 0.0).then_inc(tot_read, 1)
                else:
                    V.tensor_copy(ny_tot[:, 1, 0:1], ny_tot[:, 0, TPB:TPB + 1]).then_inc(tot_read, 1)
                V.tensor_copy(ny_pre, rot(("pre", t, 0))[:, 0:TPB]).then_inc(ny_sum, 1)
                dve.wait_ge(tot_read, 2 * t + 1)
                s = t % 2
                V.tensor_tensor_scan(ny_tot[:, s, 1:TPB + 1], rot(("pre", t, 0))[:, TPB:2 * TPB],
                                     ny_unit[:, :, QRY], ny_tot[:, s, 0:1], ALU.add, ALU.bypass).then_inc(tot_read, 1)
                dve.wait_ge(tot_read, 2 * t + 2)
                dve.wait_ge(ny_sum, 2 * t + 1)
                V.tensor_tensor(ny_pre, ny_pre, ny_tot[:, s, 0:TPB], ALU.add).then_inc(ny_sum, 1)
                dve.wait_ge(ny_sum, 2 * t + 2)
                V.tensor_tensor(ny_g, ny_pre, ny_unit[:, :, QRY], ALU.mult).then_inc(ny_done, 1)

            def bind(t):
                s = t % 2
                dve.wait_ge(root_ready, t + 1)
                V.tensor_scalar(mag[:, s], mag[:, s], EPS_UNIT, None, ALU.add).then_inc(eps_ready, 1)
                dve.wait_ge(eps_ready, t + 1)
                V.tensor_tensor(den, mag[:, s, KEY, :], mag[:, s, VAL, :], ALU.mult).then_inc(den_ready, 1)
                dve.wait_ge(den_ready, t + 1)
                V.tensor_tensor(rec, den, mag[:, s, QRY, :], ALU.mult).then_inc(all_ready, 1)
                dve.wait_ge(all_ready, t + 1)
                V.reciprocal(rec, rec).then_inc(rec_ready, 1)
                dve.wait_ge(rec_ready, t + 1)
                V.tensor_tensor(mag[:, s, KEY, :], rec, mag[:, s, QRY, :], ALU.mult).then_inc(rkv_ready, 1)
                dve.wait_ge(rkv_ready, t + 1)
                V.tensor_tensor(mag[:, s, QRY, :], rec, den, ALU.mult).then_inc(rq_ready, 1)
                V.tensor_tensor(uk, z[:, s, KEY], mag[:, s, KEY, :].unsqueeze(1).to_broadcast([P, 2, BLK]),
                                ALU.mult).then_inc(uk_ready, 1)
                dve.wait_ge(uk_ready, t + 1)
                if t >= 1:
                    dve.wait_ge(idft_done, t)
                for a in range(2):
                    V.tensor_tensor(prod[:, a], z[:, s, VAL], uk[:, a, :].unsqueeze(1).to_broadcast([P, 2, BLK]),
                                    ALU.mult).then_inc(prod_ready, 1)
                dve.wait_ge(prod_ready, 2 * t + 2)
                if t >= 2:
                    dve.wait_ge(x1_ready, 2 * (t - 1))
                first = t % 2 == 0
                V.tensor_tensor_scan(s_run[:, s, RE, :], prod[:, 0, RE, :], prod[:, 1, IM, :],
                                     0.0 if first else s_run[:, 1 - s, RE, BLK - 1:BLK],
                                     ALU.add, ALU.subtract).then_inc(scan_ready, 1)
                V.tensor_tensor_scan(s_run[:, s, IM, :], prod[:, 0, IM, :], prod[:, 1, RE, :],
                                     0.0 if first else s_run[:, 1 - s, IM, BLK - 1:BLK],
                                     ALU.add, ALU.add).then_inc(scan_ready, 1)

            def unbind(t):
                dve.wait_ge(x1_ready, 2 * (t + 1))
                V.tensor_tensor(prod[:, 0, RE, :], prod[:, 0, RE, :], prod[:, 1, IM, :], ALU.add).then_inc(g_ready, 1)
                V.tensor_tensor(prod[:, 0, IM, :], prod[:, 1, RE, :], prod[:, 0, IM, :], ALU.subtract).then_inc(g_ready, 1)

            def residual(t):
                dve.wait_ge(idft_done, t + 1)
                if t >= 1:
                    dve.wait_ge(x2_out, 16 * t)
                V.tensor_tensor(x2, ps[:, OUT:OUT + 2, :].rearrange("p a (j d) -> p (a j) d", d=D),
                                x_sb[:, t % XS], ALU.add).then_inc(x2_ready, 1)
                dve.wait_ge(x2_ready, t + 1)
                moments(x2, 1, t, ln2_stats, ln2_agg, ln2_var, mv[:, 1], rstd[:, 2, :])

            def ln2_rows(t):
                b = t // 2
                dve.wait_ge(ln2_std, t + 1)
                V.reciprocal(rstd[:, 2, :], rstd[:, 2, :]).then_inc(ln2_rstd, 1)
                if t >= 1:
                    dve.wait_ge(h2_out, 16 * t)
                    dve.wait_ge(tp2_done, KD * t)
                for j in range(TPB):
                    V.scalar_tensor_tensor(out=h2[:, j, :], in0=x2[:, j, :], scalar=mv[:, 1, j, 0:1],
                                           in1=mod_bc[:, b, 2, :], op0=ALU.subtract, op1=ALU.mult).then_inc(h2_mid, 1)
                dve.wait_ge(ln2_rstd, t + 1)
                for j in range(TPB):
                    dve.wait_ge(h2_mid, TPB * t + j + 1)
                    V.scalar_tensor_tensor(out=h2[:, j, :], in0=h2[:, j, :], scalar=rstd[:, 2, j:j + 1],
                                           in1=mod_bc[:, b, 1, :], op0=ALU.mult, op1=ALU.add).then_inc(h2_ready, 1)

            ln1_moments(0)
            ln1_moments(1)
            ln1_rows(0)
            modulation()
            for t in range(-1, NBLK + 1):
                if t >= 1:
                    residual(t - 1)
                if t >= 0 and t + 2 < NBLK:
                    ln1_moments(t + 2)
                if 0 <= t < NBLK:
                    nyquist_units(t)
                    bind(t)
                if t >= 1:
                    if t == 1:
                        dve.wait_ge(mod_ready, 10)
                    ln2_rows(t - 1)
                if 0 <= t < NBLK:
                    nyquist_apply(t)
                    unbind(t)
                if t == -1:
                    ln1_rows(1)
                elif t + 2 < NBLK:
                    ln1_rows(t + 2)
                if t + 1 < NBLK:
                    magnitudes(t + 1)

            steps = [0]

            def step(ins):
                steps[0] += 1
                ins.then_inc(route, 1)
                dve.wait_ge(route, steps[0])

            dve.wait_ge(gate_ready, NBLK)
            dve.wait_ge(idft_done, NBLK)
            dve.wait_ge(x2_out, 16 * NBLK)
            dve.wait_ge(h2_out, 16 * NBLK)
            dve.wait_ge(tp2_done, KD * NBLK)
            for t in range(TILES):
                ins = V.max(best[:, t, :], gates[:, t, :])
            step(ins)
            for t in range(TILES):
                ins = V.max_index(best_i[:, t, :], best[:, t, :], gates[:, t, :])
            step(ins)
            V.tensor_tensor(pw_tmp[:, 0, :], best[:, :, 1], best[:, :, 0], ALU.subtract).then_inc(w_sub, 1)
            step(V.tensor_copy(pick[:].rearrange("p (k t) -> p k t", k=TOP_K),
                               best_i[:, :, 0:TOP_K].rearrange("p t k -> p k t")))
            step(V.tensor_tensor(onehot, pick[:].unsqueeze(2).to_broadcast([P, PCOLS, EXPERTS]),
                                 iota_sb[:, 0:EXPERTS].unsqueeze(1).to_broadcast([P, PCOLS, EXPERTS]), ALU.is_equal))
            step(V.tensor_scalar(strict_f, iota_sb, pcol, None, ALU.is_gt))
            step(V.tensor_copy(tri_b[:, 0, :], strict_f))
            step(V.memset(tri_b[:, 1, :], 1.0))
            V.tensor_copy(onehot_b, onehot.rearrange("p c e -> p (c e)")).then_inc(cast_done, 1)
            dve.wait_ge(rank_mm, 1)
            step(V.tensor_copy(rank, ps[:, 0, :]))
            step(V.tensor_copy(tot.rearrange("p c e -> p (c e)"), ps[:, 1, :]))
            step(V.memset(cum[:, :, 0:1], 0.0))
            for e in range(EXPERTS):
                ins = V.tensor_tensor_scan(cum[:, e, 1:PCOLS + 1], tot[:, :, e], tot[:, :, e], 0.0,
                                           ALU.add, ALU.bypass)
            step(ins)
            step(V.tensor_scalar(small[:, 0, :].bitcast(I32), cum[:, :, PCOLS], float(P - 1), None, ALU.add))
            step(V.tensor_scalar(small[:, 1, :].bitcast(I32), small[:, 0, :].bitcast(I32), 7, None,
                                 ALU.logical_shift_right))
            step(V.tensor_copy(small[:, 2, :], small[:, 1, :].bitcast(I32)))
            step(V.tensor_tensor_scan(small[:, 3, :], small[:, 2, :], small[:, 2, :], 0.0, ALU.add, ALU.bypass))
            step(V.tensor_tensor(small[:, 4, :], small[:, 3, :], small[:, 2, :], ALU.subtract))
            step(V.tensor_scalar(small[:, 5, :], small[:, 4, :], float(P), None, ALU.mult))
            rank_v = rank.rearrange("p (c e) -> p c e", e=EXPERTS)
            step(V.tensor_tensor(rank_v, rank_v, cum[:, :, 0:PCOLS].rearrange("p e c -> p c e"), ALU.add))
            step(V.tensor_tensor(rank_v, rank_v, small[:, 5, :].unsqueeze(1).to_broadcast([P, PCOLS, EXPERTS]),
                                 ALU.add))
            step(V.tensor_tensor(rank_v, rank_v, onehot, ALU.mult))
            step(V.tensor_reduce(slot, rank_v, AX_X, ALU.add))
            step(V.tensor_copy(slot_i[:, 0, :], slot))
            step(V.tensor_scalar(slot_i[:, 1, :], slot_i[:, 0, :], 7, None, ALU.logical_shift_right))
            step(V.tensor_copy(slot_hl[:, 1, :], slot_i[:, 1, :]))
            step(V.scalar_tensor_tensor(out=slot_hl[:, 0, :], in0=slot_hl[:, 1, :], scalar=-float(P), in1=slot,
                                        op0=ALU.mult, op1=ALU.add))
            step(V.tensor_scalar(small[:, 6, 0:1], pcol, 1.0, None, ALU.add))
            for c in range(PCOLS):
                if c >= 2:
                    dve.wait_ge(perm_mm, c - 1)
                V.tensor_scalar(lo_hot[:, c % 2, :], iota_sb, slot_hl[:, 0, c:c + 1], None, ALU.is_equal)
                V.tensor_scalar(hi_hot[:, c % 2, 0, :], iota_sb[:, 0:MOE_TILES], slot_hl[:, 1, c:c + 1],
                                small[:, 6, 0:1], ALU.is_equal, ALU.mult).then_inc(hi_made, 1)
                V.tensor_scalar(hi_hot[:, c % 2, 1, :], iota_sb[:, 0:MOE_TILES], slot_hl[:, 1, c:c + 1],
                                float(c), ALU.is_equal, ALU.mult).then_inc(hi_made, 1)
            step(V.tensor_tensor(te_cmp, iota_sb[:, 0:MOE_TILES].unsqueeze(2).to_broadcast([P, MOE_TILES, EXPERTS]),
                                 small[:, 3, :].unsqueeze(1).to_broadcast([P, MOE_TILES, EXPERTS]), ALU.is_ge))
            step(V.tensor_reduce(perm[:, 3, :], te_cmp, AX_X, ALU.add))
            V.tensor_scalar(tile_expert, perm[:, 3, :], float(EXPERTS - 1), None, ALU.min).then_inc(tiles_ready, 1)
            dve.wait_ge(w_exp, 1)
            step(V.tensor_scalar(pw_tmp[:, 0, :], pw_tmp[:, 1, :], 1.0, None, ALU.add))
            step(V.reciprocal(pair_w[:, 0, :], pw_tmp[:, 0, :]))
            V.tensor_tensor(pair_w[:, 1, :], pair_w[:, 0, :], pw_tmp[:, 1, :], ALU.mult).then_inc(tiles_ready, 1)
            dve.wait_ge(perm_mm, PCOLS)
            step(V.tensor_copy(perm[:, 1, :], ps[:, 2, 0:MOE_TILES]))
            step(V.scalar_tensor_tensor(out=perm[:, 0, :], in0=ps[:, 2, MOE_TILES:2 * MOE_TILES], scalar=float(P),
                                        in1=perm[:, 1, :], op0=ALU.mult, op1=ALU.add))
            step(V.tensor_scalar(perm[:, 1, :], perm[:, 0, :], 0.0, float(PAIRS + 1), ALU.is_equal, ALU.mult))
            V.scalar_tensor_tensor(out=scatter_idx, in0=perm[:, 0, :], scalar=-1.0, in1=perm[:, 1, :],
                                   op0=ALU.add, op1=ALU.add).then_inc(tiles_ready, 1)
            step(V.tensor_scalar(perm[:, 2, :], perm[:, 0, :], float(TOKENS + 1), -float(TOKENS), ALU.is_ge, ALU.mult))
            step(V.scalar_tensor_tensor(out=perm[:, 1, :], in0=perm[:, 0, :], scalar=-1.0, in1=perm[:, 2, :],
                                        op0=ALU.add, op1=ALU.add))
            V.tensor_scalar(gather_idx, perm[:, 1, :], 0.0, None, ALU.max).then_inc(tiles_ready, 1)

            dve.wait_ge(tiles_ready, 4)
            dve.wait_ge(bias_in, 32)
            dve.sem_inc(gv_ready, 1)
            dve.sem_inc(y_ready, 1)

            def gated(i, s):
                e = dve.value_load(tile_expert[0:1, bass.ds(i, 1)], min_val=0, max_val=EXPERTS - 1)
                dve.wait_ge(up_done, i + 1)
                V.tensor_tensor(gv[:, s].rearrange("p a f -> p (a f)"),
                                ps[:, 4 + 2 * s:6 + 2 * s, :].rearrange("p a f -> p (a f)"),
                                b1_bc[:, bass.ds(e * (2 * HID), 2 * HID)], ALU.add).then_inc(gv_ready, 1)
                dve.wait_ge(gv_ready, i + 2)
                V.tensor_scalar(gv[:, s, 0, :], gv[:, s, 0, :], LIMIT, None, ALU.min).then_inc(clip_done, 1)
                V.tensor_scalar(gv[:, s, 1, :], gv[:, s, 1, :], LIMIT, -LIMIT, ALU.min, ALU.max).then_inc(glu_ready, 1)
                dve.wait_ge(sig_ready, i + 1)
                V.tensor_tensor(gv[:, s, 0, :], gv[:, s, 0, :], sig[:], ALU.mult).then_inc(glu_ready, 1)
                dve.wait_ge(glu_ready, 2 * (i + 1))
                V.scalar_tensor_tensor(out=gv[:, s, 0, :], in0=gv[:, s, 1, :], scalar=1.0, in1=gv[:, s, 0, :],
                                       op0=ALU.add, op1=ALU.mult).then_inc(hid_ready, 1)
                return e

            def rows_out(i, s, e, wait):
                dve.wait_ge(down_done, i + 2)
                if wait is not None:
                    dve.wait_ge(scattered[s], wait)
                V.tensor_tensor(y_sb[:, s, :], ps[:, 2, 0:D], b2_bc[:, bass.ds(e * D, D)], ALU.add).then_inc(y_ready, 1)

            for s in range(2):
                e = gated(s, s)
                rows_out(s, s, e, None)
            with dve.Fori(1, (MOE_TILES - 1) // 2) as n:
                for s in range(2):
                    e = gated(2 * n + s, s)
                    rows_out(2 * n + s, s, e, 16 * n)
            e = gated(MOE_TILES - 1, 0)
            rows_out(MOE_TILES - 1, 0, e, 16 * (MOE_TILES // 2))

            for t in range(NBLK):
                s = t % 2
                for j in range(TPB):
                    n = t * TPB + j
                    dve.wait_ge(d_w1, n + 1)
                    V.scalar_tensor_tensor(out=d_y[:, s, 0, j, :], in0=d_y[:, s, 1, j, :],
                                           scalar=pair_w[:, 1, n:n + 1], in1=d_y[:, s, 0, j, :],
                                           op0=ALU.mult, op1=ALU.add).then_inc(d_w2, 1)
                dve.wait_ge(d_w2, TPB * (t + 1))
                V.tensor_tensor(d_y[:, s, 0], d_y[:, s, 0], gb_bc[:, t // 2, :].unsqueeze(1).to_broadcast([P, TPB, D]),
                                ALU.mult).then_inc(d_gb, 1)
                dve.wait_ge(d_gb, t + 1)
                V.tensor_tensor(d_x[:, s], d_y[:, s, 0], d_x[:, s], ALU.add).then_inc(d_ready, 1)

        @block.gpsimd
        def _(pool):
            G = nc.gpsimd
            pool.wait_ge(mod_ready, 10)
            for t in range(NBLK):
                s, b = t % 2, t // 2
                if s == 0:
                    if b >= 2:
                        pool.wait_ge(idft_done, 2 * (b - 1))
                    for r in range(2):
                        ins = G.tensor_tensor(idft_ga[:, b % 2, r, :], idft_sb[:, r, :], mod_bc[:, b, 0, :], ALU.mult)
                    ins.then_inc(ga_ready, 1)
                pool.wait_ge(rq_ready, t + 1)
                for r in range(2):
                    ins = G.tensor_tensor(z[:, s, QRY, r, :], z[:, s, QRY, r, :], mag[:, s, QRY, :], ALU.mult)
                ins.then_inc(uq_ready, 1)
                pool.wait_ge(uq_ready, t + 1)
                pool.wait_ge(scan_ready, 2 * (t + 1))
                for a in range(2):
                    for r in range(2):
                        ins = G.tensor_tensor(prod[:, a, r, :], s_run[:, s, a, :], z[:, s, QRY, r, :], ALU.mult)
                    ins.then_inc(x1_ready, 1)

            def wait_turn(signal, value):
                pool.wait_ge(signal, value)
                pool.sem_inc(pool_turn, 1)

            def gather(i, s):
                G.tensor_copy(gather_now[:, s:s + 1], gather_idx[:, bass.ds(i, 1)]).then_inc(gather_set, 1)
                wait_turn(gather_set, i + 1)
                G.indirect_dma_start(out=xg[:, s, :], out_offset=None, in_=h_scratch,
                                     in_offset=bass.IndirectOffsetOnAxis(ap=gather_now[:, s:s + 1], axis=0)
                                     ).then_inc(gathered[s], 16)

            def scatter(i, s):
                wait_turn(y_ready, i + 2)
                G.tensor_copy(scatter_now[:, s:s + 1], scatter_idx[:, bass.ds(i, 1)]).then_inc(scatter_set, 1)
                wait_turn(scatter_set, i + 1)
                G.indirect_dma_start(out=y_scratch,
                                     out_offset=bass.IndirectOffsetOnAxis(ap=scatter_now[:, s:s + 1], axis=0),
                                     in_=y_sb[:, s, :], in_offset=None, bounds_check=PAIRS - 1,
                                     oob_is_err=False).then_inc(scattered[s], 16)

            pool.wait_ge(tiles_ready, 4)
            gather(0, 0)
            gather(1, 1)
            with pool.Fori(0, (MOE_TILES - 1) // 2 - 1) as n:
                for s in range(2):
                    i = 2 * n + s
                    wait_turn(xg_tp, i + 1)
                    gather(i + 2, s)
                    scatter(i, s)
            last = MOE_TILES - 3
            pool.wait_ge(xg_tp, last + 1)
            gather(last + 2, 0)
            for i in range(last, MOE_TILES):
                scatter(i, i % 2)


def constants():
    f32 = np.float32
    e, k = np.arange(D), np.arange(P)
    turn = 2.0 * np.pi * ((e[:, None] * k[None, :]) % D) / D
    alt = np.where(e % 2 == 0, 1.0, -1.0)
    dft = np.concatenate([np.cos(turn), -np.sin(turn), alt[:, None]], axis=1).astype(f32)
    inv_re = np.cos(turn).T * np.where(k == 0, 1.0, 2.0)[:, None] / D
    inv_im = -np.sin(turn).T * 2.0 / D
    inv_im[0] = alt / D
    idft = np.stack([inv_re, inv_im], axis=1).astype(f32)
    i = np.arange(P)
    tri = np.zeros((P, 4, P), f32)
    tri[:, 0] = i[:, None] <= i[None, :]
    tri[:, 1] = 1.0
    tri[:, 3] = alt[:P, None]
    iota = np.concatenate([np.broadcast_to(i, (P, P)), i[:, None]], axis=1).astype(f32)
    return {"dft": dft.reshape(KD, P, -1).transpose(1, 0, 2), "idft": idft, "ident": np.eye(P, dtype=f32),
            "tri": tri, "iota": iota}


def kernel(L0_attn_x, L0_attn_Wq, L0_attn_bq, L0_attn_Wk, L0_attn_bk, L0_attn_Wv, L0_attn_bv, L0_ffn_gate_w,
           L0_ffn_dense_1_w, L0_ffn_dense_1_b, L0_ffn_dense_2_w, L0_ffn_dense_2_b, L0_c, L0_wmod):
    import concourse.bacc as bacc
    from concourse.bass_utils import run_bass_kernel_spmd

    def rows(a):
        a = np.asarray(a)
        return a.reshape(-1, P, a.shape[-1]).transpose(1, 0, 2)

    w1 = np.asarray(L0_ffn_dense_1_w).reshape(EXPERTS, HID, 2, KD, P)
    w2 = np.asarray(L0_ffn_dense_2_w).reshape(EXPERTS, D, KF, P)
    arrays = {
        "x": np.asarray(L0_attn_x).reshape(TOKENS, D),
        "wqkv": np.stack([rows(w) for w in (L0_attn_Wk, L0_attn_Wv, L0_attn_Wq)], axis=1),
        "bqkv": np.stack([np.asarray(b).reshape(KD, P).T for b in (L0_attn_bk, L0_attn_bv, L0_attn_bq)], axis=2),
        "gate_w": rows(L0_ffn_gate_w),
        "w1": w1.transpose(4, 0, 3, 2, 1).reshape(P, -1),
        "b1": np.asarray(L0_ffn_dense_1_b).reshape(EXPERTS, HID, 2).transpose(0, 2, 1).reshape(-1),
        "w2": w2.transpose(3, 0, 2, 1).reshape(P, -1),
        "b2": np.asarray(L0_ffn_dense_2_b).reshape(-1),
        "c_t": rows(np.asarray(L0_c).T),
        "wmod": rows(L0_wmod),
        **constants(),
    }
    nc = bacc.Bacc("TRN2", target_bir_lowering=False, num_devices=1)
    feed, args = {}, {}
    for name, a in arrays.items():
        a = np.ascontiguousarray(a)
        feed[f"in_{name}"] = a
        args[name] = nc.dram_tensor(f"in_{name}", a.shape, mybir.dt.from_np(a.dtype), kind="ExternalInput").ap()
    out = nc.dram_tensor("out_rows", (TOKENS, D), F32, kind="ExternalOutput").ap()
    adaln_moe_kernel(nc, **args, out=out)
    r = run_bass_kernel_spmd(nc, [feed], core_ids=[0])
    return r.results[0]["out_rows"].reshape(BATCH, SEQ, D)
```

```python
from contextlib import ExitStack

import numpy as np

import concourse.bass as bass
from concourse import mybir

ALU = mybir.AluOpType
ACT = mybir.ActivationFunctionType
F32 = mybir.dt.float32
BF16 = mybir.dt.bfloat16
FP16 = mybir.dt.float16
I32 = mybir.dt.int32
U32 = mybir.dt.uint32
AX_X = mybir.AxisListType.X

P = 128
BATCH, SEQ, D = 4, 1024, 256
TOKENS = BATCH * SEQ
KD = D // P
EXPERTS, HID = 8, 512
KF = HID // P
TOP_K = 2
BLK = 512
NBLK = TOKENS // BLK
TPB = BLK // P
TILES = TOKENS // P
PAIRS = TOKENS * TOP_K
PCOLS = PAIRS // P
MOE_TILES = PAIRS // P + EXPERTS - 1
LOOP_END = MOE_TILES - 3
EPS_UNIT, EPS_LN = 1e-8, 1e-5
ALPHA, LIMIT = 1.702, 9.0
KEY, VAL, QRY = 0, 1, 2
SX, SW, SH = 8.0, 64.0, 16.0
HI, LO = 0, 1
SPLIT = ((HI, HI), (LO, HI), (HI, LO))
WCH = 1024
RE, IM = 0, 1


def psum_plan():
    items = []
    for t in range(-1, NBLK + 1):
        if t + 1 < NBLK:
            items += [("z", t + 1, i) for i in range(6)] + [("ny", t + 1, 0)]
        if 0 <= t < NBLK:
            items.append(("pre", t, 0))
        if t >= 1:
            items.append(("gate", t - 1, 0))
        if 0 <= t < NBLK:
            items.append(("row", t, 0))
    return {item: n for n, item in enumerate(items)}, items


def adaln_moe_kernel(nc, x, wqkv, bqkv, gate_w, w1, b1, w2, b2, c_t, wmod, dft, idft, ident, tri, iota, out):
    place, order = psum_plan()
    ROT = 4
    x_scratch = nc.dram_tensor("x_scratch", (TOKENS, D), F32).ap()
    h_scratch = nc.dram_tensor("h_scratch", (TOKENS, 2 * D), FP16).ap()
    y_scratch = nc.dram_tensor("y_scratch", (PAIRS, D), F32).ap()

    x_blk = x.rearrange("(t j p) d -> t p j d", p=P, j=TPB)
    xs_blk = x_scratch.rearrange("(t j p) d -> t p j d", p=P, j=TPB)
    hs_blk = h_scratch.rearrange("(t j p) d -> t p j d", p=P, j=TPB)
    y_blk = y_scratch.rearrange("(k t j p) d -> k t p j d", p=P, j=TPB, k=TOP_K)
    out_blk = out.rearrange("(t j p) d -> t p j d", p=P, j=TPB)

    with ExitStack() as ctx:
        def sb(name, shape, dt=F32):
            return ctx.enter_context(nc.sbuf_tensor(name, shape, dt))

        def sem(name):
            return ctx.enter_context(nc.semaphore(name))

        def sems(name, n):
            return [sem(f"{name}{i}") for i in range(n)]

        w1_sb = sb("w1_sb", [P, 2, EXPERTS * KD * 2 * HID], FP16)
        w_stage = sb("w_stage", [P, 2, WCH])
        ident_sb = sb("ident_sb", [P, P])
        ident_h = sb("ident_h", [P, P], FP16)
        gb_bc = sb("gb_bc", [P, BATCH, D])
        gates = sb("gates", [P, TILES, EXPERTS])

        REGION = 33296
        region = sb("region", [P, REGION])
        cursor = [0]

        def carve(n):
            cursor[0] += n
            assert cursor[0] <= REGION, cursor
            return region[:, cursor[0] - n:cursor[0]]

        XS = 4
        x_sb = carve(XS * TPB * D).rearrange("p (s j d) -> p s j d", s=XS, j=TPB)
        n_sb = carve(TPB * D).rearrange("p (j d) -> p j d", j=TPB)
        h_t = carve(KD * BLK).rearrange("p (k n) -> p k n", k=KD)
        z_flat = carve(2 * 6 * BLK)
        z = z_flat.rearrange("p (s c r n) -> p s c r n", s=2, c=3, r=2)
        sq = carve(6 * BLK).rearrange("p (c r n) -> p c r n", c=3, r=2)
        m_flat = carve(2 * 3 * BLK)
        mag = m_flat.rearrange("p (s c n) -> p s c n", s=2, c=3)
        den = carve(BLK)
        rec = carve(BLK)
        uk = carve(2 * BLK).rearrange("p (r n) -> p r n", r=2)
        p_flat = carve(4 * BLK)
        prod = p_flat.rearrange("p (a r n) -> p a r n", a=2, r=2)
        s_flat = carve(4 * BLK)
        s_run = s_flat.rearrange("p (s r n) -> p s r n", s=2, r=2)
        x2 = carve(TPB * D).rearrange("p (j d) -> p j d", j=TPB)
        h2_parts = carve(TPB * D).bitcast(FP16).rearrange("p (j a d) -> p j a d", j=TPB, a=2)
        mod_bc = carve(BATCH * 3 * D).rearrange("p (b m d) -> p b m d", b=BATCH, m=3)
        NF = 2 * P + 1
        w_spec = carve(3 * KD * NF).rearrange("p (c k f) -> p c k f", c=3, k=KD)
        idft_sb = carve(2 * D).rearrange("p (r d) -> p r d", r=2)
        idft_ga = carve(2 * 2 * D).rearrange("p (s r d) -> p s r d", s=2, r=2)
        gate_h = carve(KD * EXPERTS).bitcast(FP16).rearrange("p (a k e) -> p a k e", a=2, k=KD)
        tri_sb = carve(2 * P).rearrange("p (a n) -> p a n", a=2)
        bias_f = carve(9)
        sca_t = carve(4 * BATCH).rearrange("p (w k b) -> p w k b", w=2, k=KD)
        stats = carve(2 * TPB * 6).rearrange("p (w j s) -> p w j s", w=2, j=TPB)
        mv = carve(2 * TPB * 2).rearrange("p (w j s) -> p w j s", w=2, j=TPB)
        mv1 = carve(2 * TPB * 2).rearrange("p (s j a) -> p s j a", s=2, j=TPB)
        rstd = carve(3 * TPB).rearrange("p (w j) -> p w j", w=3)
        ny = carve(3 * TPB).rearrange("p (j c) -> p j c", j=TPB)
        ny_abs = carve(3 * TPB).rearrange("p (j c) -> p j c", j=TPB)
        ny_unit = carve(3 * TPB).rearrange("p (j c) -> p j c", j=TPB)
        ny_kv = carve(TPB)
        ny_tot = carve(2 * (TPB + 1)).rearrange("p (s j) -> p s j", s=2)
        ny_pre = carve(TPB)
        ny_g = carve(TPB)
        wmod_sb = z_flat[:, 0:KD * 6 * D].rearrange("p (k n) -> p k n", k=KD)
        mod_tmp = s_flat[:, 0:BATCH * D].rearrange("p (b d) -> p b d", b=BATCH)
        wraw = m_flat[:, 0:3 * KD * D].rearrange("p (c k d) -> p c k d", c=3, k=KD)
        silu_rep = p_flat[:, 0:KD * BATCH * P].rearrange("p (k b m) -> p k b m", k=KD, b=BATCH)
        dft_sb = uk[:, :, :].rearrange("p r n -> p (r n)")[:, 0:KD * NF].rearrange("p (k f) -> p k f", k=KD)
        alt_rep = den[:, 0:P]
        bq_sb = rec[:, 0:KD * 3].rearrange("p (k c) -> p k c", k=KD)
        c_sb = rec[:, 16:16 + KD * BATCH].rearrange("p (k b) -> p k b", k=KD)
        c_sig = rec[:, 32:32 + KD * BATCH].rearrange("p (k b) -> p k b", k=KD)
        c_silu = rec[:, 48:48 + KD * BATCH].rearrange("p (k b) -> p k b", k=KD)
        gate_sb = rec[:, 64:64 + KD * EXPERTS].rearrange("p (k e) -> p k e", k=KD)

        cursor[0] = 0
        w2_sb = carve(EXPERTS * KF * D).bitcast(FP16).rearrange("p (a n) -> p a n", a=2)
        b1_bc = carve(EXPERTS * 2 * HID)
        b2_bc = carve(EXPERTS * D)
        route_lo = cursor[0]
        xg = carve(2 * D).bitcast(FP16).rearrange("p (s d) -> p s d", s=2)
        xg_t = carve(2 * D).bitcast(FP16).rearrange("p (s n) -> p s n", s=2)
        gv = carve(2 * 2 * HID).rearrange("p (s a f) -> p s a f", s=2, a=2)
        sig = w_stage[:, 0, 0:2 * HID].rearrange("p (s f) -> p s f", s=2)
        hid = carve(2 * HID).bitcast(FP16).rearrange("p (s a f) -> p s a f", s=2, a=2)
        hid_t = carve(2 * HID).bitcast(FP16).rearrange("p (s n) -> p s n", s=2)
        y_sb = w_stage[:, 1, 0:2 * D].rearrange("p (s d) -> p s d", s=2)
        gather_idx = carve(MOE_TILES).bitcast(I32)
        scatter_idx = carve(MOE_TILES).bitcast(I32)
        tile_expert = carve(MOE_TILES).bitcast(I32)
        gather_now = carve(2).bitcast(I32)
        scatter_now = carve(2).bitcast(I32)
        pair_w = carve(PCOLS).rearrange("p (k t) -> p k t", k=TOP_K)
        x2_lo = cursor[0]
        cursor[0] = EXPERTS * KF * D
        best = carve(TILES * 8).rearrange("p (t e) -> p t e", e=8)
        best_i = carve(TILES * 8).bitcast(U32).rearrange("p (t e) -> p t e", e=8)
        pick = carve(PCOLS)
        onehot = carve(PCOLS * EXPERTS).rearrange("p (c e) -> p c e", e=EXPERTS)
        onehot_b = carve(PCOLS * EXPERTS // 2).bitcast(BF16)
        rank = carve(PCOLS * EXPERTS)
        tot = carve(PCOLS * EXPERTS).rearrange("p (c e) -> p c e", e=EXPERTS)
        cum = carve(EXPERTS * (PCOLS + 1)).rearrange("p (e c) -> p e c", e=EXPERTS)
        small = carve(16 * EXPERTS).rearrange("p (a e) -> p a e", e=EXPERTS)
        slot = carve(PCOLS)
        slot_i = carve(2 * PCOLS).bitcast(I32).rearrange("p (a c) -> p a c", a=2)
        slot_hl = carve(2 * PCOLS).rearrange("p (a c) -> p a c", a=2)
        tri_b = carve(P).bitcast(BF16).rearrange("p (a n) -> p a n", a=2)
        pw_tmp = carve(2 * TILES).rearrange("p (a t) -> p a t", a=2)
        lo_hot = carve(2 * P // 2).bitcast(BF16).rearrange("p (s n) -> p s n", s=2)
        hi_hot = carve(2 * MOE_TILES).bitcast(BF16).rearrange("p (s a n) -> p s a n", s=2, a=2)
        te_cmp = carve(MOE_TILES * EXPERTS).rearrange("p (i e) -> p i e", e=EXPERTS)
        perm = carve(4 * MOE_TILES).rearrange("p (a i) -> p a i", a=4)
        strict_f = carve(P)
        iota_all = carve(P + 1)
        iota_sb = iota_all[:, 0:P]
        pcol = iota_all[:, P:P + 1]
        assert cursor[0] <= route_lo, (cursor, route_lo)
        cursor[0] = 0
        d_y = carve(2 * 2 * TPB * D).rearrange("p (s k j d) -> p s k j d", s=2, k=2, j=TPB)
        assert cursor[0] <= EXPERTS * KF * D
        cursor[0] = x2_lo
        d_x = carve(TILES * D).rearrange("p (t j d) -> p t j d", t=NBLK, j=TPB)

        ps = ctx.enter_context(nc.psum_tensor("ps", [P, 8, 512], F32))
        TP, OUT, ROT0 = 0, 2, 4

        def rot(item):
            return ps[:, ROT0 + place[item] % ROT, :]

        const_in, wmod_in, wraw_in, w1_in, w2_in, bias_in = (sem(n) for n in (
            "const_in", "wmod_in", "wraw_in", "w1_in", "w2_in", "bias_in"))
        x_in = sems("x_in", XS)
        x2_out, h2_out = sem("x2_out"), sem("h2_out")
        (sig_done, silu_done, rep_done, pe_setup, act_setup, mod_mm, mod_copied, mod_ready, ga_ready,
         ln1_stats, ln1_agg, ln1_var, ln1_std, ln1_rstd, n_ready, tp_done, ht_ready, z_mm, z_ready, sq_ready,
         mag_ready, root_ready, eps_ready, den_ready, all_ready, rec_ready, rkv_ready, rq_ready, uk_ready,
         prod_ready, scan_ready, uq_ready, x1_ready, g_ready, nymm, ny_read, ny_absd, ny_rec, ny_unitd, ny_kvd,
         pre_mm, tot_read, ny_sum, ny_done, row_mm, row_ready, idft_done, x2_ready, ln2_stats,
         ln2_agg, ln2_var, ln2_std, ln2_rstd, h2_mid, h2_ready, tp2_done, h2t_ready, gate_mm, gate_ready) = (
            sem(n) for n in (
                "sig_done silu_done rep_done pe_setup act_setup mod_mm mod_copied mod_ready ga_ready "
                "ln1_stats ln1_agg ln1_var ln1_std ln1_rstd n_ready tp_done ht_ready z_mm z_ready sq_ready "
                "mag_ready root_ready eps_ready den_ready all_ready rec_ready rkv_ready rq_ready uk_ready "
                "prod_ready scan_ready uq_ready x1_ready g_ready nymm ny_read ny_absd ny_rec ny_unitd ny_kvd "
                "pre_mm tot_read ny_sum ny_done row_mm row_ready idft_done x2_ready ln2_stats "
                "ln2_agg ln2_var ln2_std ln2_rstd h2_mid h2_ready tp2_done h2t_ready gate_mm gate_ready").split())
        (route, cast_done, rank_mm, w_exp, hi_made, perm_mm, tiles_ready, w_sub) = (
            sem(n) for n in "route cast_done rank_mm w_exp hi_made perm_mm tiles_ready w_sub".split())
        w_in = sems("w_in", 2)
        iota_in = sem("iota_in")
        w_scaled, w_hi, w_lo, gate_split, h2_hi, h2_lo, hid_hi, x2_in = (sem(n) for n in (
            "w_scaled w_hi w_lo gate_split h2_hi h2_lo hid_hi x2_in").split())
        gathered = sems("gathered", 2)
        scattered = sems("scattered", 2)
        gather_set, scatter_set, pool_turn = sem("gather_set"), sem("scatter_set"), sem("pool_turn")
        (gsig_ready, vclip_done, xg_tp, xgt_ready, up_done, gv_ready, clip_done, sig_ready, glu_ready, hid_ready, hid_tp, hidt_ready,
         down_done, y_ready) = (sem(n) for n in (
            "gsig_ready vclip_done xg_tp xgt_ready up_done gv_ready clip_done sig_ready glu_ready hid_ready hid_tp hidt_ready "
            "down_done y_ready").split())
        d_in, d_out = sems("d_in", 2), sems("d_out", 2)
        d_w1, d_w2, d_gb, d_ready = (sem(n) for n in "d_w1 d_w2 d_gb d_ready".split())

        block = ctx.enter_context(nc.Block())

        def bank_free(e, item):
            n = place[item] - ROT
            if n >= 0:
                kind, t, i = order[n]
                s, v = {"z": (z_ready, 6 * t + i + 1), "ny": (ny_read, t + 1), "pre": (ny_sum, 2 * t + 2),
                        "gate": (gate_ready, t + 1), "row": (row_ready, t + 1)}[kind]
                e.wait_ge(s, v)

        W1_CHUNKS = EXPERTS * KD * 2 * HID // WCH
        W_CHUNKS = W1_CHUNKS + EXPERTS * KF * D // WCH

        def load_weights(sp, n):
            if n >= 2:
                sp.wait_ge(w_hi, n - 1)
                sp.wait_ge(w_lo, n - 1)
            src = w1[:, n * WCH:(n + 1) * WCH] if n < W1_CHUNKS else w2[:, (n - W1_CHUNKS) * WCH:
                                                                         (n - W1_CHUNKS + 1) * WCH]
            sp.dma_start(w_stage[:, n % 2, :], src).then_inc(w_in[n % 2], 16)

        def parts_of(n):
            if n < W1_CHUNKS:
                return [w1_sb[:, a, n * WCH:(n + 1) * WCH] for a in (HI, LO)]
            return [w2_sb[:, a, (n - W1_CHUNKS) * WCH:(n - W1_CHUNKS + 1) * WCH] for a in (HI, LO)]

        @block.sync
        def _(sp):
            sp.dma_start(c_sb, c_t).then_inc(const_in, 16)
            sp.dma_start(dft_sb, dft[:, :, 0:NF]).then_inc(const_in, 16)
            sp.dma_start(alt_rep, tri[:, 3, :]).then_inc(const_in, 16)
            sp.dma_start(bq_sb, bqkv).then_inc(const_in, 16)
            sp.dma_start(ident_sb[:], ident).then_inc(const_in, 16)
            sp.dma_start(idft_sb, idft).then_inc(const_in, 16)
            sp.dma_start(gate_sb, gate_w).then_inc(const_in, 16)
            sp.dma_start(tri_sb, tri[:, 0:2, :]).then_inc(const_in, 16)
            sp.dma_start(wraw, wqkv).then_inc(wraw_in, 16)
            sp.dma_start(wmod_sb, wmod).then_inc(wmod_in, 16)
            for t in range(XS):
                sp.dma_start(x_sb[:, t], x_blk[t]).then_inc(x_in[t], 16)
            for n in range(2):
                load_weights(sp, n)
            for t in range(NBLK):
                sp.wait_ge(x2_ready, t + 1)
                sp.dma_start(xs_blk[t], x2).then_inc(x2_out, 16)
                if t + XS < NBLK:
                    sp.dma_start(x_sb[:, (t + XS) % XS], x_blk[t + XS]).then_inc(x_in[t % XS], 16)
                for n in (2 * t + 2, 2 * t + 3):
                    load_weights(sp, n)
                sp.wait_ge(h2_lo, t + 1)
                sp.dma_start(hs_blk[t], h2_parts.rearrange("p j a d -> p j (a d)")).then_inc(h2_out, 16)
            sp.wait_ge(gate_ready, NBLK)
            sp.wait_ge(x2_out, 16 * NBLK)
            sp.wait_ge(h2_out, 16 * NBLK)
            sp.wait_ge(tp2_done, KD * NBLK)
            sp.wait_ge(idft_done, NBLK)
            sp.dma_start(iota_all, iota).then_inc(iota_in, 16)
            for n in range(2 * NBLK + 2, W_CHUNKS):
                load_weights(sp, n)
            sp.wait_ge(tiles_ready, 4)
            sp.dma_start(b1_bc, b1.partition_broadcast(P)).then_inc(bias_in, 16)
            sp.dma_start(b2_bc, b2.partition_broadcast(P)).then_inc(bias_in, 16)
            sp.dma_start(d_x, x_scratch.rearrange("(t j p) d -> p t j d", p=P, j=TPB)).then_inc(x2_in, 16)
            for t in range(NBLK):
                s = t % 2
                if t == 0:
                    sp.wait_ge(y_ready, MOE_TILES)
                    for i in range(2):
                        sp.wait_ge(scattered[i], 16 * ((MOE_TILES + 1 - i) // 2))
                if t >= 2:
                    sp.wait_ge(d_ready, t - 1)
                for k in range(TOP_K):
                    sp.dma_start(d_y[:, s, k], y_blk[k, t]).then_inc(d_in[s], 16)
                if t >= 1:
                    sp.wait_ge(d_ready, t)
                    sp.dma_start(out_blk[t - 1], d_x[:, t - 1]).then_inc(d_out[1 - s], 16)
            sp.wait_ge(d_ready, NBLK)
            sp.dma_start(out_blk[NBLK - 1], d_x[:, NBLK - 1]).then_inc(d_out[(NBLK - 1) % 2], 16)
            for i in range(2):
                sp.wait_ge(d_out[i], 16 * (NBLK // 2))

        @block.tensor
        def _(pe):
            def transform_weights():
                pe.wait_ge(const_in, 128)
                pe.wait_ge(wraw_in, 16)
                for c in range(3):
                    for kd in range(KD):
                        for ke in range(KD):
                            mm = pe.matmul(ps[:, c * KD + kd, 0:NF], wraw[:, c, ke, kd * P:(kd + 1) * P],
                                           dft_sb[:, ke, :], start=(ke == 0), stop=(ke == KD - 1))
                        mm.then_inc(pe_setup, 1)
                for r in range(3):
                    for ke in range(KD):
                        lhs = dft_sb[:, ke, r * P:(r + 1) * P] if r < 2 else alt_rep
                        mm = pe.matmul(ps[:, 6, 3 * r:3 * r + 3], lhs, bq_sb[:, ke, :],
                                       start=(ke == 0), stop=(ke == KD - 1))
                mm.then_inc(pe_setup, 1)
                pe.wait_ge(wmod_in, 16)
                pe.wait_ge(silu_done, 1)
                for w in range(2):
                    for kd in range(KD):
                        for ke in range(KD):
                            at = w * D + kd * P
                            mm = pe.matmul(ps[:, 7, (w * KD + kd) * BATCH:(w * KD + kd + 1) * BATCH],
                                           wmod_sb[:, ke, at:at + P], c_silu[:, ke, :],
                                           start=(ke == 0), stop=(ke == KD - 1))
                mm.then_inc(pe_setup, 1)

            def broadcast_modulation():
                pe.wait_ge(rep_done, 1)
                for b in range(BATCH):
                    for half in range(2):
                        n = 2 * b + half
                        pe.wait_ge(act_setup, n + 1)
                        for ke in range(KD):
                            mm = pe.matmul(ps[:, n, :], silu_rep[:, ke, b, :],
                                           wmod_sb[:, ke, (2 + 2 * half) * D:(4 + 2 * half) * D],
                                           start=(ke == 0), stop=(ke == KD - 1))
                        mm.then_inc(mod_mm, 1)
                pe.wait_ge(mod_copied, 2 * BATCH)

            def transpose_rows(src, t, done):
                for k in range(KD):
                    for j in range(TPB):
                        mm = pe.transpose(ps[:, TP + k, j * P:(j + 1) * P], src[:, j, k * P:(k + 1) * P],
                                          ident_sb[:])
                    mm.then_inc(done, 1)

            def project(t):
                pe.wait_ge(n_ready, TPB * (t + 1))
                if t >= 1:
                    pe.wait_ge(ht_ready, KD * t)
                if t >= 3:
                    pe.wait_ge(h2t_ready, KD * (t - 2))
                transpose_rows(n_sb, t, tp_done)
                pe.wait_ge(ht_ready, KD * (t + 1))
                for i in range(6):
                    c, r = i // 2, i % 2
                    bank_free(pe, ("z", t, i))
                    for k in range(KD):
                        mm = pe.matmul(rot(("z", t, i)), w_spec[:, c, k, r * P:(r + 1) * P], h_t[:, k, :],
                                       start=(k == 0), stop=(k == KD - 1))
                    mm.then_inc(z_mm, 1)
                bank_free(pe, ("ny", t, 0))
                for j in range(TPB):
                    for k in range(KD):
                        mm = pe.matmul(rot(("ny", t, 0))[:, 3 * j:3 * j + 3], h_t[:, k, j * P:(j + 1) * P],
                                       w_spec[:, :, k, 2 * P], start=(k == 0), stop=(k == KD - 1))
                mm.then_inc(nymm, 1)

            def nyquist_sums(t):
                pe.wait_ge(ny_kvd, t + 1)
                bank_free(pe, ("pre", t, 0))
                pe.matmul(rot(("pre", t, 0))[:, 0:TPB], tri_sb[:, 0, :], ny_kv, start=True, stop=True)
                pe.matmul(rot(("pre", t, 0))[:, TPB:2 * TPB], tri_sb[:, 1, :], ny_kv, start=True,
                          stop=True).then_inc(pre_mm, 1)

            def gate(t):
                pe.wait_ge(h2_lo, t + 1)
                pe.wait_ge(ht_ready, KD * min(t + 3, NBLK))
                for k in range(KD):
                    bank = ps[:, TP + k, :].bitcast(FP16)
                    for a in (HI, LO):
                        for j in range(TPB):
                            mm = pe.transpose(bank[:, a * BLK + j * P:a * BLK + (j + 1) * P],
                                              h2_parts[:, j, a, k * P:(k + 1) * P], ident_h[:])
                    mm.then_inc(tp2_done, 1)
                pe.wait_ge(h2t_ready, KD * (t + 1))
                bank_free(pe, ("gate", t, 0))
                for j in range(TPB):
                    n = 0
                    for k in range(KD):
                        cols = h_t[:, k, :].bitcast(FP16)
                        for xa, wa in SPLIT:
                            mm = pe.matmul(rot(("gate", t, 0))[:, j * EXPERTS:(j + 1) * EXPERTS],
                                           cols[:, xa * BLK + j * P:xa * BLK + (j + 1) * P], gate_h[:, wa, k, :],
                                           start=(n == 0), stop=(n == 3 * KD - 1))
                            n += 1
                mm.then_inc(gate_mm, 1)

            def nyquist_row(t):
                pe.wait_ge(ny_done, t + 1)
                bank_free(pe, ("row", t, 0))
                for j in range(TPB):
                    mm = pe.transpose(rot(("row", t, 0))[0:1, j * P:(j + 1) * P], ny_g[:, j:j + 1], ident_sb[:])
                mm.then_inc(row_mm, 1)

            def inverse(t):
                pe.wait_ge(row_ready, t + 1)
                pe.wait_ge(g_ready, 2 * (t + 1))
                pe.wait_ge(ga_ready, t // 2 + 1)
                if t >= 1:
                    pe.wait_ge(x2_ready, t)
                for j in range(TPB):
                    for r in range(2):
                        mm = pe.matmul(ps[:, OUT + j // 2, (j % 2) * D:(j % 2 + 1) * D],
                                       prod[:, 0, r, j * P:(j + 1) * P], idft_ga[:, (t // 2) % 2, r, :],
                                       start=(r == 0), stop=(r == 1))
                mm.then_inc(idft_done, 1)

            transform_weights()
            broadcast_modulation()
            for t in range(-1, NBLK + 1):
                if t + 1 < NBLK:
                    project(t + 1)
                if 0 <= t < NBLK:
                    nyquist_sums(t)
                if t >= 1:
                    gate(t - 1)
                if 0 <= t < NBLK:
                    nyquist_row(t)
                    inverse(t)

            pe.wait_ge(cast_done, 1)
            pe.matmul(ps[:, 0, :], tri_b[:, 0, :], onehot_b, start=True, stop=True)
            pe.matmul(ps[:, 1, :], tri_b[:, 1, :], onehot_b, start=True, stop=True).then_inc(rank_mm, 1)
            for c in range(PCOLS):
                pe.wait_ge(hi_made, 2 * (c + 1))
                pe.matmul(ps[:, 2, 0:2 * MOE_TILES], lo_hot[:, c % 2, :],
                          hi_hot[:, c % 2].rearrange("p a n -> p (a n)"),
                          start=(c == 0), stop=(c == PCOLS - 1)).then_inc(perm_mm, 1)

            XT, HT, YB, GV = 0, 1, 2, 4

            def expert(i):
                return pe.value_load(tile_expert[0:1, bass.ds(i, 1)], min_val=0, max_val=EXPERTS - 1)

            def rows_in(s, wait):
                pe.wait_ge(gathered[s], wait)
                for q in range(2 * KD):
                    mm = pe.transpose(ps[:, XT, :].bitcast(FP16)[:, q * P:(q + 1) * P],
                                      xg[:, s, q * P:(q + 1) * P], ident_h[:])
                mm.then_inc(xg_tp, 1)

            def up(i, s):
                e = expert(i)
                pe.wait_ge(xgt_ready, i + 1)
                for a in range(2):
                    n = 0
                    for k in range(KD):
                        for xa, wa in SPLIT:
                            mm = pe.matmul(ps[:, GV + 2 * s + a, :],
                                           xg_t[:, s, (xa * KD + k) * P:(xa * KD + k + 1) * P],
                                           w1_sb[:, wa, bass.ds(e * (KD * 2 * HID) + (k * 2 + a) * HID, HID)],
                                           start=(n == 0), stop=(n == 3 * KD - 1))
                            n += 1
                mm.then_inc(up_done, 1)

            def down(i, s):
                e = expert(i)
                pe.wait_ge(hid_ready, i + 1)
                for q in range(2 * KF):
                    mm = pe.transpose(ps[:, HT, :].bitcast(FP16)[:, q * P:(q + 1) * P],
                                      hid[:, s, q // KF, (q % KF) * P:(q % KF + 1) * P], ident_h[:])
                mm.then_inc(hid_tp, 1)
                pe.wait_ge(hidt_ready, i + 1)
                n = 0
                for k in range(KF):
                    for xa, wa in SPLIT:
                        mm = pe.matmul(ps[:, YB + s, 0:D], hid_t[:, s, (xa * KF + k) * P:(xa * KF + k + 1) * P],
                                       w2_sb[:, wa, bass.ds(e * (KF * D) + k * D, D)],
                                       start=(n == 0), stop=(n == 3 * KF - 1))
                        n += 1
                mm.then_inc(down_done, 1)

            def turn(i, s, wait):
                if wait is not None:
                    rows_in(s, wait)
                    pe.wait_ge(gv_ready, i + 1)
                    up(i + 2, s)
                if not isinstance(i, int) or i >= 2:
                    pe.wait_ge(y_ready, i - 1)
                down(i, s)

            pe.wait_ge(w_hi, W_CHUNKS)
            pe.wait_ge(w_lo, W_CHUNKS)
            pe.wait_ge(tiles_ready, 4)
            for s in range(2):
                rows_in(s, 16)
                up(s, s)
            for s in range(2):
                turn(s, s, 32)
            with pe.Fori(1, LOOP_END // 2) as n:
                for s in range(2):
                    turn(2 * n + s, s, 16 * (n + 2))
            turn(LOOP_END, 0, 16 * (LOOP_END // 2 + 2))
            turn(LOOP_END + 1, 1, None)
            turn(LOOP_END + 2, 0, None)

        @block.scalar
        def _(act):
            act.wait_ge(const_in, 128)
            nc.scalar.activation(c_sig, c_sb, ACT.Sigmoid).then_inc(sig_done, 1)
            for n in range(6):
                act.wait_ge(pe_setup, n + 1)
                nc.scalar.activation(w_spec[:, n // KD, n % KD, :], ps[:, n, 0:NF], ACT.Copy).then_inc(act_setup, 1)
            act.wait_ge(pe_setup, 7)
            nc.scalar.activation(bias_f, ps[:, 6, 0:9], ACT.Copy).then_inc(act_setup, 1)
            act.wait_ge(pe_setup, 8)
            nc.scalar.activation(sca_t.rearrange("p w k b -> p (w k b)"), ps[:, 7, 0:4 * BATCH],
                                 ACT.Copy).then_inc(act_setup, 1)
            for b in range(BATCH):
                act.wait_ge(mod_mm, 2 * b + 1)
                nc.scalar.activation(mod_bc[:, b, 0:2, :], ps[:, 2 * b, :].rearrange("p (m d) -> p m d", m=2),
                                     ACT.Copy).then_inc(mod_copied, 1)
                act.wait_ge(mod_mm, 2 * b + 2)
                nc.scalar.activation(mod_bc[:, b, 2, :], ps[:, 2 * b + 1, 0:D], ACT.Copy)
                nc.scalar.activation(gb_bc[:, b, :], ps[:, 2 * b + 1, D:2 * D], ACT.Copy).then_inc(mod_copied, 1)

            def project(t):
                act.wait_ge(ln1_var, t + 1)
                nc.scalar.activation(rstd[:, t % 2, :], rstd[:, t % 2, :], ACT.Sqrt).then_inc(ln1_std, 1)

            def spectra(t):
                b = t // 2
                if t == 0:
                    act.wait_ge(mod_ready, 1)
                for k in range(KD):
                    act.wait_ge(tp_done, KD * t + k + 1)
                    if k == 0 and t >= 1:
                        act.wait_ge(nymm, t)
                    if k == 0 and t >= 3:
                        act.wait_ge(gate_mm, t - 2)
                    nc.scalar.activation(h_t[:, k, :], ps[:, TP + k, :], ACT.Identity,
                                         bias=sca_t[:, 0, k, b:b + 1],
                                         scale=sca_t[:, 1, k, b:b + 1]).then_inc(ht_ready, 1)

            def evacuate(t):
                if t >= 2:
                    act.wait_ge(uq_ready, t - 1)
                    act.wait_ge(prod_ready, 2 * (t - 1))
                for i in range(6):
                    c, r = i // 2, i % 2
                    act.wait_ge(z_mm, 6 * t + i + 1)
                    nc.scalar.activation(z[:, t % 2, c, r, :], rot(("z", t, i)), ACT.Identity,
                                         bias=bias_f[:, 3 * r + c:3 * r + c + 1]).then_inc(z_ready, 1)
                if t >= 1:
                    act.wait_ge(mag_ready, t)
                for c in range(3):
                    act.wait_ge(z_ready, 6 * t + 2 * c + 2)
                    nc.scalar.activation(sq[:, c], z[:, t % 2, c], ACT.Square).then_inc(sq_ready, 1)

            def std2(t):
                act.wait_ge(ln2_var, t + 1)
                nc.scalar.activation(rstd[:, 2, :], rstd[:, 2, :], ACT.Sqrt).then_inc(ln2_std, 1)

            def roots(t):
                act.wait_ge(mag_ready, t + 1)
                nc.scalar.activation(mag[:, t % 2], mag[:, t % 2], ACT.Sqrt).then_inc(root_ready, 1)

            def gate(t):
                for k in range(KD):
                    act.wait_ge(tp2_done, KD * t + k + 1)
                    if k == 0:
                        act.wait_ge(nymm, min(t + 3, NBLK))
                    nc.scalar.activation(h_t[:, k, :].bitcast(FP16), ps[:, TP + k, :].bitcast(FP16),
                                         ACT.Copy).then_inc(h2t_ready, 1)
                act.wait_ge(gate_mm, t + 1)
                nc.scalar.activation(gates[:, t * TPB:(t + 1) * TPB, :],
                                     rot(("gate", t, 0))[:, 0:TPB * EXPERTS].rearrange("p (j e) -> p j e", j=TPB),
                                     ACT.Copy, scale=1.0 / (SX * SW)).then_inc(gate_ready, 1)

            def split_rows(t):
                act.wait_ge(h2_ready, TPB * (t + 1))
                if t >= 1:
                    act.wait_ge(h2_out, 16 * t)
                    act.wait_ge(tp2_done, KD * t)
                nc.scalar.activation(h2_parts[:, :, HI, :], x2, ACT.Copy).then_inc(h2_hi, 1)

            def split_weights(n):
                act.wait_ge(w_in[n % 2], 16 * (n // 2 + 1))
                nc.scalar.activation(w_stage[:, n % 2, :], w_stage[:, n % 2, :], ACT.Copy,
                                     scale=SW).then_inc(w_scaled, 1)
                act.wait_ge(w_scaled, n + 1)
                nc.scalar.activation(parts_of(n)[HI], w_stage[:, n % 2, :], ACT.Copy).then_inc(w_hi, 1)

            def nyquist_row(t):
                act.wait_ge(row_mm, t + 1)
                act.wait_ge(g_ready, 2 * (t + 1))
                nc.scalar.activation(prod[0:1, 0, IM, :], rot(("row", t, 0))[0:1, :], ACT.Copy).then_inc(row_ready, 1)

            project(0)
            project(1)
            for t in range(-1, NBLK + 1):
                if t + 1 < NBLK:
                    spectra(t + 1)
                if t + 1 < NBLK:
                    evacuate(t + 1)
                if t >= 1:
                    std2(t - 1)
                if t >= 0 and t + 2 < NBLK:
                    project(t + 2)
                if t >= 1:
                    split_rows(t - 1)
                if 0 <= t < NBLK:
                    split_weights(2 * t)
                if t >= 1:
                    gate(t - 1)
                if 0 <= t < NBLK:
                    split_weights(2 * t + 1)
                    nyquist_row(t)
                if t + 1 < NBLK:
                    roots(t + 1)

            for n in range(2 * NBLK, W_CHUNKS):
                split_weights(n)
            act.wait_ge(w_sub, 1)
            nc.scalar.activation(pw_tmp[:, 1, :], pw_tmp[:, 0, :], ACT.Exp).then_inc(w_exp, 1)

            def rows_in(i, s):
                act.wait_ge(xg_tp, i + 1)
                nc.scalar.activation(xg_t[:, s, :], ps[:, 0, :].bitcast(FP16)[:, 0:2 * D], ACT.Copy).then_inc(xgt_ready, 1)

            def sigmoid(i, s):
                act.wait_ge(clip_done, i + 1)
                nc.scalar.activation(sig[:, s, :], gv[:, s, 0, :], ACT.Sigmoid, scale=ALPHA).then_inc(sig_ready, 1)

            def turn(i, s, more_rows, more_gates):
                act.wait_ge(glu_ready, i + 1)
                if not isinstance(i, int) or i >= 2:
                    act.wait_ge(hid_tp, i - 1)
                nc.scalar.activation(hid[:, s, HI, :], gv[:, s, 0, :], ACT.Copy, scale=SH).then_inc(hid_hi, 1)
                if more_rows:
                    rows_in(i + 2, s)
                if more_gates:
                    sigmoid(i + 1, 1 - s)
                act.wait_ge(hid_tp, i + 1)
                if not isinstance(i, int) or i >= 2:
                    act.wait_ge(down_done, i - 1)
                nc.scalar.activation(hid_t[:, s, :], ps[:, 1, :].bitcast(FP16), ACT.Copy).then_inc(hidt_ready, 1)

            rows_in(0, 0)
            rows_in(1, 1)
            sigmoid(0, 0)
            for s in range(2):
                turn(s, s, True, True)
            with act.Fori(1, LOOP_END // 2) as n:
                for s in range(2):
                    turn(2 * n + s, s, True, True)
            turn(LOOP_END, 0, True, True)
            turn(LOOP_END + 1, 1, False, True)
            turn(LOOP_END + 2, 0, False, False)

            for t in range(NBLK):
                act.wait_ge(d_in[t % 2], 32 * (t // 2 + 1))
                for j in range(TPB):
                    nc.scalar.activation(d_y[:, t % 2, 0, j, :], d_y[:, t % 2, 0, j, :], ACT.Copy,
                                         scale=pair_w[:, 0, t * TPB + j:t * TPB + j + 1]).then_inc(d_w1, 1)

        @block.vector
        def _(dve):
            V = nc.vector
            dve.wait_ge(sig_done, 1)
            V.tensor_tensor(c_silu, c_sb, c_sig, ALU.mult).then_inc(silu_done, 1)
            dve.wait_ge(silu_done, 1)
            V.tensor_copy(silu_rep, c_silu.unsqueeze(3).to_broadcast([P, KD, BATCH, P])).then_inc(rep_done, 1)
            V.tensor_copy(ident_h[:], ident_sb[:]).then_inc(gate_split, 1)
            V.tensor_scalar(gate_sb, gate_sb, SW, None, ALU.mult).then_inc(gate_split, 1)
            dve.wait_ge(gate_split, 2)
            V.tensor_copy(gate_h[:, HI], gate_sb).then_inc(gate_split, 1)
            dve.wait_ge(gate_split, 3)
            V.tensor_tensor(gate_h[:, LO], gate_sb, gate_h[:, HI], ALU.subtract).then_inc(gate_split, 1)
            dve.wait_ge(act_setup, 8)
            V.tensor_scalar(sca_t[:, 1], sca_t[:, 1], 1.0, None, ALU.add).then_inc(mod_ready, 1)

            def clamp_gain(g, n):
                V.tensor_scalar(mod_tmp, g, 0.0, 2.0, ALU.is_ge, ALU.mult).then_inc(mod_ready, 1)
                dve.wait_ge(mod_ready, n + 1)
                V.scalar_tensor_tensor(out=g, in0=g, scalar=-1.0, in1=g, op0=ALU.mult,
                                       op1=ALU.max).then_inc(mod_ready, 1)
                dve.wait_ge(mod_ready, n + 2)
                V.tensor_scalar(g, g, 0.25, None, ALU.max).then_inc(mod_ready, 1)
                dve.wait_ge(mod_ready, n + 3)
                V.scalar_tensor_tensor(out=g, in0=mod_tmp, scalar=-1.0, in1=g, op0=ALU.add,
                                       op1=ALU.mult).then_inc(mod_ready, 1)
                dve.wait_ge(mod_ready, n + 4)

            def modulation():
                dve.wait_ge(mod_copied, 2 * BATCH)
                clamp_gain(mod_bc[:, :, 0, :], 1)
                clamp_gain(gb_bc[:, :, :], 5)
                V.tensor_scalar(mod_bc[:, :, 2, :], mod_bc[:, :, 2, :], 1.0, SX, ALU.add, ALU.mult).then_inc(mod_ready, 1)
                V.tensor_scalar(mod_bc[:, :, 1, :], mod_bc[:, :, 1, :], SX, None, ALU.mult).then_inc(mod_ready, 1)

            def moments(src, w, t, s_stats, s_agg, s_var, mvt, sd):
                for j in range(TPB):
                    V.bn_stats(stats[:, w, j, :], src[:, j, :]).then_inc(s_stats, 1)
                dve.wait_ge(s_stats, TPB * (t + 1))
                for j in range(TPB):
                    V.bn_aggr(mvt[:, j, :], stats[:, w, j, :]).then_inc(s_agg, 1)
                dve.wait_ge(s_agg, TPB * (t + 1))
                V.tensor_scalar(sd, mvt[:, :, 1], EPS_LN, None, ALU.add).then_inc(s_var, 1)

            def ln1_moments(t):
                dve.wait_ge(x_in[t % XS], 16 * (t // XS + 1))
                moments(x_sb[:, t % XS], 0, t, ln1_stats, ln1_agg, ln1_var, mv1[:, t % 2], rstd[:, t % 2, :])

            def ln1_rows(t):
                dve.wait_ge(ln1_std, t + 1)
                V.reciprocal(rstd[:, t % 2, :], rstd[:, t % 2, :]).then_inc(ln1_rstd, 1)
                dve.wait_ge(ln1_rstd, t + 1)
                if t >= 1:
                    dve.wait_ge(tp_done, KD * t)
                for j in range(TPB):
                    V.tensor_scalar(n_sb[:, j, :], x_sb[:, t % XS, j, :], mv1[:, t % 2, j, 0:1],
                                    rstd[:, t % 2, j:j + 1], ALU.subtract, ALU.mult).then_inc(n_ready, 1)

            def magnitudes(t):
                dve.wait_ge(sq_ready, 3 * (t + 1))
                V.tensor_tensor(mag[:, t % 2], sq[:, :, RE, :], sq[:, :, IM, :], ALU.add).then_inc(mag_ready, 1)

            def nyquist_units(t):
                dve.wait_ge(nymm, t + 1)
                V.tensor_tensor(ny, rot(("ny", t, 0))[:, 0:3 * TPB].rearrange("p (j c) -> p j c", j=TPB),
                                bias_f[:, 6:9].unsqueeze(1).to_broadcast([P, TPB, 3]), ALU.add).then_inc(ny_read, 1)
                dve.wait_ge(ny_read, t + 1)
                V.scalar_tensor_tensor(out=ny_abs, in0=ny, scalar=-1.0, in1=ny, op0=ALU.mult,
                                       op1=ALU.max).then_inc(ny_absd, 1)
                dve.wait_ge(ny_absd, 2 * t + 1)
                V.tensor_scalar(ny_abs, ny_abs, EPS_UNIT, None, ALU.add).then_inc(ny_absd, 1)
                dve.wait_ge(ny_absd, 2 * t + 2)
                V.reciprocal(ny_abs, ny_abs).then_inc(ny_rec, 1)
                dve.wait_ge(ny_rec, t + 1)
                V.tensor_tensor(ny_unit, ny, ny_abs, ALU.mult).then_inc(ny_unitd, 1)
                dve.wait_ge(ny_unitd, t + 1)
                V.tensor_tensor(ny_kv, ny_unit[:, :, KEY], ny_unit[:, :, VAL], ALU.mult).then_inc(ny_kvd, 1)

            def nyquist_apply(t):
                dve.wait_ge(pre_mm, t + 1)
                if t % 2 == 0:
                    V.memset(ny_tot[:, 0, 0:1], 0.0).then_inc(tot_read, 1)
                else:
                    V.tensor_copy(ny_tot[:, 1, 0:1], ny_tot[:, 0, TPB:TPB + 1]).then_inc(tot_read, 1)
                V.tensor_copy(ny_pre, rot(("pre", t, 0))[:, 0:TPB]).then_inc(ny_sum, 1)
                dve.wait_ge(tot_read, 2 * t + 1)
                s = t % 2
                V.tensor_tensor_scan(ny_tot[:, s, 1:TPB + 1], rot(("pre", t, 0))[:, TPB:2 * TPB],
                                     ny_unit[:, :, QRY], ny_tot[:, s, 0:1], ALU.add, ALU.bypass).then_inc(tot_read, 1)
                dve.wait_ge(tot_read, 2 * t + 2)
                dve.wait_ge(ny_sum, 2 * t + 1)
                V.tensor_tensor(ny_pre, ny_pre, ny_tot[:, s, 0:TPB], ALU.add).then_inc(ny_sum, 1)
                dve.wait_ge(ny_sum, 2 * t + 2)
                V.tensor_tensor(ny_g, ny_pre, ny_unit[:, :, QRY], ALU.mult).then_inc(ny_done, 1)

            def bind(t):
                s = t % 2
                dve.wait_ge(root_ready, t + 1)
                V.tensor_scalar(mag[:, s], mag[:, s], EPS_UNIT, None, ALU.add).then_inc(eps_ready, 1)
                dve.wait_ge(eps_ready, t + 1)
                V.tensor_tensor(den, mag[:, s, KEY, :], mag[:, s, VAL, :], ALU.mult).then_inc(den_ready, 1)
                dve.wait_ge(den_ready, t + 1)
                V.tensor_tensor(rec, den, mag[:, s, QRY, :], ALU.mult).then_inc(all_ready, 1)
                dve.wait_ge(all_ready, t + 1)
                V.reciprocal(rec, rec).then_inc(rec_ready, 1)
                dve.wait_ge(rec_ready, t + 1)
                V.tensor_tensor(mag[:, s, KEY, :], rec, mag[:, s, QRY, :], ALU.mult).then_inc(rkv_ready, 1)
                dve.wait_ge(rkv_ready, t + 1)
                V.tensor_tensor(mag[:, s, QRY, :], rec, den, ALU.mult).then_inc(rq_ready, 1)
                V.tensor_tensor(uk, z[:, s, KEY], mag[:, s, KEY, :].unsqueeze(1).to_broadcast([P, 2, BLK]),
                                ALU.mult).then_inc(uk_ready, 1)
                dve.wait_ge(uk_ready, t + 1)
                if t >= 1:
                    dve.wait_ge(idft_done, t)
                for a in range(2):
                    V.tensor_tensor(prod[:, a], z[:, s, VAL], uk[:, a, :].unsqueeze(1).to_broadcast([P, 2, BLK]),
                                    ALU.mult).then_inc(prod_ready, 1)
                dve.wait_ge(prod_ready, 2 * t + 2)
                if t >= 2:
                    dve.wait_ge(x1_ready, 2 * (t - 1))
                first = t % 2 == 0
                V.tensor_tensor_scan(s_run[:, s, RE, :], prod[:, 0, RE, :], prod[:, 1, IM, :],
                                     0.0 if first else s_run[:, 1 - s, RE, BLK - 1:BLK],
                                     ALU.add, ALU.subtract).then_inc(scan_ready, 1)
                V.tensor_tensor_scan(s_run[:, s, IM, :], prod[:, 0, IM, :], prod[:, 1, RE, :],
                                     0.0 if first else s_run[:, 1 - s, IM, BLK - 1:BLK],
                                     ALU.add, ALU.add).then_inc(scan_ready, 1)

            def unbind(t):
                dve.wait_ge(x1_ready, 2 * (t + 1))
                V.tensor_tensor(prod[:, 0, RE, :], prod[:, 0, RE, :], prod[:, 1, IM, :], ALU.add).then_inc(g_ready, 1)
                V.tensor_tensor(prod[:, 0, IM, :], prod[:, 1, RE, :], prod[:, 0, IM, :], ALU.subtract).then_inc(g_ready, 1)

            def residual(t):
                dve.wait_ge(idft_done, t + 1)
                if t >= 1:
                    dve.wait_ge(h2_lo, t)
                V.tensor_tensor(x2, ps[:, OUT:OUT + 2, :].rearrange("p a (j d) -> p (a j) d", d=D),
                                x_sb[:, t % XS], ALU.add).then_inc(x2_ready, 1)
                dve.wait_ge(x2_ready, t + 1)
                moments(x2, 1, t, ln2_stats, ln2_agg, ln2_var, mv[:, 1], rstd[:, 2, :])

            def ln2_rows(t):
                b = t // 2
                dve.wait_ge(ln2_std, t + 1)
                V.reciprocal(rstd[:, 2, :], rstd[:, 2, :]).then_inc(ln2_rstd, 1)
                dve.wait_ge(x2_out, 16 * (t + 1))
                for j in range(TPB):
                    V.scalar_tensor_tensor(out=x2[:, j, :], in0=x2[:, j, :], scalar=mv[:, 1, j, 0:1],
                                           in1=mod_bc[:, b, 2, :], op0=ALU.subtract, op1=ALU.mult).then_inc(h2_mid, 1)
                dve.wait_ge(ln2_rstd, t + 1)
                for j in range(TPB):
                    dve.wait_ge(h2_mid, TPB * t + j + 1)
                    V.scalar_tensor_tensor(out=x2[:, j, :], in0=x2[:, j, :], scalar=rstd[:, 2, j:j + 1],
                                           in1=mod_bc[:, b, 1, :], op0=ALU.mult, op1=ALU.add).then_inc(h2_ready, 1)

            ln1_moments(0)
            ln1_moments(1)
            ln1_rows(0)
            modulation()
            for t in range(-1, NBLK + 1):
                if 0 <= t < NBLK:
                    nyquist_units(t)
                    bind(t)
                if t >= 1:
                    residual(t - 1)
                if t >= 0 and t + 2 < NBLK:
                    ln1_moments(t + 2)
                if t >= 1:
                    if t == 1:
                        dve.wait_ge(mod_ready, 11)
                    ln2_rows(t - 1)
                if 0 <= t < NBLK:
                    nyquist_apply(t)
                    unbind(t)
                if t == -1:
                    ln1_rows(1)
                elif t + 2 < NBLK:
                    ln1_rows(t + 2)
                if t + 1 < NBLK:
                    magnitudes(t + 1)

            steps = [0]

            def step(ins):
                steps[0] += 1
                ins.then_inc(route, 1)
                dve.wait_ge(route, steps[0])

            dve.wait_ge(gate_ready, NBLK)
            dve.wait_ge(idft_done, NBLK)
            dve.wait_ge(h2_out, 16 * NBLK)
            dve.wait_ge(tp2_done, KD * NBLK)
            dve.wait_ge(iota_in, 16)
            for t in range(TILES):
                ins = V.max(best[:, t, :], gates[:, t, :])
            step(ins)
            for t in range(TILES):
                ins = V.max_index(best_i[:, t, :], best[:, t, :], gates[:, t, :])
            step(ins)
            V.tensor_tensor(pw_tmp[:, 0, :], best[:, :, 1], best[:, :, 0], ALU.subtract).then_inc(w_sub, 1)
            step(V.tensor_copy(pick[:].rearrange("p (k t) -> p k t", k=TOP_K),
                               best_i[:, :, 0:TOP_K].rearrange("p t k -> p k t")))
            step(V.tensor_tensor(onehot, pick[:].unsqueeze(2).to_broadcast([P, PCOLS, EXPERTS]),
                                 iota_sb[:, 0:EXPERTS].unsqueeze(1).to_broadcast([P, PCOLS, EXPERTS]), ALU.is_equal))
            step(V.tensor_scalar(strict_f, iota_sb, pcol, None, ALU.is_gt))
            step(V.tensor_copy(tri_b[:, 0, :], strict_f))
            step(V.memset(tri_b[:, 1, :], 1.0))
            V.tensor_copy(onehot_b, onehot.rearrange("p c e -> p (c e)")).then_inc(cast_done, 1)
            dve.wait_ge(rank_mm, 1)
            step(V.tensor_copy(rank, ps[:, 0, :]))
            step(V.tensor_copy(tot.rearrange("p c e -> p (c e)"), ps[:, 1, :]))
            step(V.memset(cum[:, :, 0:1], 0.0))
            for e in range(EXPERTS):
                ins = V.tensor_tensor_scan(cum[:, e, 1:PCOLS + 1], tot[:, :, e], tot[:, :, e], 0.0,
                                           ALU.add, ALU.bypass)
            step(ins)
            step(V.tensor_scalar(small[:, 0, :].bitcast(I32), cum[:, :, PCOLS], float(P - 1), None, ALU.add))
            step(V.tensor_scalar(small[:, 1, :].bitcast(I32), small[:, 0, :].bitcast(I32), 7, None,
                                 ALU.logical_shift_right))
            step(V.tensor_copy(small[:, 2, :], small[:, 1, :].bitcast(I32)))
            step(V.tensor_tensor_scan(small[:, 3, :], small[:, 2, :], small[:, 2, :], 0.0, ALU.add, ALU.bypass))
            step(V.tensor_tensor(small[:, 4, :], small[:, 3, :], small[:, 2, :], ALU.subtract))
            step(V.tensor_scalar(small[:, 5, :], small[:, 4, :], float(P), None, ALU.mult))
            rank_v = rank.rearrange("p (c e) -> p c e", e=EXPERTS)
            step(V.tensor_tensor(rank_v, rank_v, cum[:, :, 0:PCOLS].rearrange("p e c -> p c e"), ALU.add))
            step(V.tensor_tensor(rank_v, rank_v, small[:, 5, :].unsqueeze(1).to_broadcast([P, PCOLS, EXPERTS]),
                                 ALU.add))
            step(V.tensor_tensor(rank_v, rank_v, onehot, ALU.mult))
            step(V.tensor_reduce(slot, rank_v, AX_X, ALU.add))
            step(V.tensor_copy(slot_i[:, 0, :], slot))
            step(V.tensor_scalar(slot_i[:, 1, :], slot_i[:, 0, :], 7, None, ALU.logical_shift_right))
            step(V.tensor_copy(slot_hl[:, 1, :], slot_i[:, 1, :]))
            step(V.scalar_tensor_tensor(out=slot_hl[:, 0, :], in0=slot_hl[:, 1, :], scalar=-float(P), in1=slot,
                                        op0=ALU.mult, op1=ALU.add))
            step(V.tensor_scalar(small[:, 6, 0:1], pcol, 1.0, None, ALU.add))
            for c in range(PCOLS):
                if c >= 2:
                    dve.wait_ge(perm_mm, c - 1)
                V.tensor_scalar(lo_hot[:, c % 2, :], iota_sb, slot_hl[:, 0, c:c + 1], None, ALU.is_equal)
                V.tensor_scalar(hi_hot[:, c % 2, 0, :], iota_sb[:, 0:MOE_TILES], slot_hl[:, 1, c:c + 1],
                                small[:, 6, 0:1], ALU.is_equal, ALU.mult).then_inc(hi_made, 1)
                V.tensor_scalar(hi_hot[:, c % 2, 1, :], iota_sb[:, 0:MOE_TILES], slot_hl[:, 1, c:c + 1],
                                float(c), ALU.is_equal, ALU.mult).then_inc(hi_made, 1)
            step(V.tensor_tensor(te_cmp, iota_sb[:, 0:MOE_TILES].unsqueeze(2).to_broadcast([P, MOE_TILES, EXPERTS]),
                                 small[:, 3, :].unsqueeze(1).to_broadcast([P, MOE_TILES, EXPERTS]), ALU.is_ge))
            step(V.tensor_reduce(perm[:, 3, :], te_cmp, AX_X, ALU.add))
            V.tensor_scalar(tile_expert, perm[:, 3, :], float(EXPERTS - 1), None, ALU.min).then_inc(tiles_ready, 1)
            dve.wait_ge(w_exp, 1)
            step(V.tensor_scalar(pw_tmp[:, 0, :], pw_tmp[:, 1, :], 1.0, None, ALU.add))
            step(V.reciprocal(pair_w[:, 0, :], pw_tmp[:, 0, :]))
            V.tensor_tensor(pair_w[:, 1, :], pair_w[:, 0, :], pw_tmp[:, 1, :], ALU.mult).then_inc(tiles_ready, 1)
            dve.wait_ge(perm_mm, PCOLS)
            step(V.tensor_copy(perm[:, 1, :], ps[:, 2, 0:MOE_TILES]))
            step(V.scalar_tensor_tensor(out=perm[:, 0, :], in0=ps[:, 2, MOE_TILES:2 * MOE_TILES], scalar=float(P),
                                        in1=perm[:, 1, :], op0=ALU.mult, op1=ALU.add))
            step(V.tensor_scalar(perm[:, 1, :], perm[:, 0, :], 0.0, float(PAIRS + 1), ALU.is_equal, ALU.mult))
            V.scalar_tensor_tensor(out=scatter_idx, in0=perm[:, 0, :], scalar=-1.0, in1=perm[:, 1, :],
                                   op0=ALU.add, op1=ALU.add).then_inc(tiles_ready, 1)
            step(V.tensor_scalar(perm[:, 2, :], perm[:, 0, :], float(TOKENS + 1), -float(TOKENS), ALU.is_ge, ALU.mult))
            step(V.scalar_tensor_tensor(out=perm[:, 1, :], in0=perm[:, 0, :], scalar=-1.0, in1=perm[:, 2, :],
                                        op0=ALU.add, op1=ALU.add))
            V.tensor_scalar(gather_idx, perm[:, 1, :], 0.0, None, ALU.max).then_inc(tiles_ready, 1)

            dve.wait_ge(tiles_ready, 4)
            dve.wait_ge(bias_in, 32)

            def expert(i):
                return dve.value_load(tile_expert[0:1, bass.ds(i, 1)], min_val=0, max_val=EXPERTS - 1)

            def biased(i, s):
                e = expert(i)
                dve.wait_ge(up_done, i + 1)
                V.scalar_tensor_tensor(out=gv[:, s].rearrange("p a f -> p (a f)"),
                                       in0=ps[:, 4 + 2 * s:6 + 2 * s, :].rearrange("p a f -> p (a f)"),
                                       scalar=1.0 / (SX * SW), in1=b1_bc[:, bass.ds(e * (2 * HID), 2 * HID)],
                                       op0=ALU.mult, op1=ALU.add).then_inc(gv_ready, 1)
                dve.wait_ge(gv_ready, i + 1)
                V.tensor_scalar(gv[:, s, 0, :], gv[:, s, 0, :], LIMIT, None, ALU.min).then_inc(clip_done, 1)

            def rows_out(i, s):
                e = expert(i)
                dve.wait_ge(down_done, i + 1)
                V.scalar_tensor_tensor(out=y_sb[:, s, :], in0=ps[:, 2 + s, 0:D], scalar=1.0 / (SH * SW),
                                       in1=b2_bc[:, bass.ds(e * D, D)], op0=ALU.mult, op1=ALU.add).then_inc(y_ready, 1)

            def turn(i, s, more, out_wait):
                dve.wait_ge(sig_ready, i + 1)
                V.tensor_tensor(gv[:, s, 0, :], gv[:, s, 0, :], sig[:, s, :], ALU.mult).then_inc(gsig_ready, 1)
                dve.wait_ge(gsig_ready, i + 1)
                dve.wait_ge(vclip_done, i + 1)
                V.scalar_tensor_tensor(out=gv[:, s, 0, :], in0=gv[:, s, 1, :], scalar=1.0, in1=gv[:, s, 0, :],
                                       op0=ALU.add, op1=ALU.mult).then_inc(glu_ready, 1)
                if more:
                    biased(i + 1, 1 - s)
                dve.wait_ge(hid_hi, i + 1)
                V.scalar_tensor_tensor(out=hid[:, s, LO, :], in0=gv[:, s, 0, :], scalar=SH, in1=hid[:, s, HI, :],
                                       op0=ALU.mult, op1=ALU.subtract).then_inc(hid_ready, 1)
                if out_wait is not None:
                    if out_wait is not False:
                        dve.wait_ge(scattered[1 - s], out_wait)
                    rows_out(i - 1, 1 - s)

            biased(0, 0)
            turn(0, 0, True, None)
            turn(1, 1, True, False)
            turn(2, 0, True, False)
            turn(3, 1, True, 16)
            with dve.Fori(2, LOOP_END // 2) as n:
                turn(2 * n, 0, True, 16 * (n - 1))
                turn(2 * n + 1, 1, True, 16 * n)
            turn(LOOP_END, 0, True, 16 * (LOOP_END // 2 - 1))
            turn(LOOP_END + 1, 1, True, 16 * (LOOP_END // 2))
            turn(LOOP_END + 2, 0, False, 16 * (LOOP_END // 2))
            dve.wait_ge(scattered[0], 16 * (LOOP_END // 2 + 1))
            rows_out(MOE_TILES - 1, 0)

            for t in range(NBLK):
                s = t % 2
                for j in range(TPB):
                    n = t * TPB + j
                    dve.wait_ge(d_w1, n + 1)
                    V.scalar_tensor_tensor(out=d_y[:, s, 0, j, :], in0=d_y[:, s, 1, j, :],
                                           scalar=pair_w[:, 1, n:n + 1], in1=d_y[:, s, 0, j, :],
                                           op0=ALU.mult, op1=ALU.add).then_inc(d_w2, 1)
                dve.wait_ge(d_w2, TPB * (t + 1))
                V.tensor_tensor(d_y[:, s, 0], d_y[:, s, 0], gb_bc[:, t // 2, :].unsqueeze(1).to_broadcast([P, TPB, D]),
                                ALU.mult).then_inc(d_gb, 1)
                dve.wait_ge(d_gb, t + 1)
                if t == 0:
                    dve.wait_ge(x2_in, 16)
                V.tensor_tensor(d_x[:, t], d_y[:, s, 0], d_x[:, t], ALU.add).then_inc(d_ready, 1)

        @block.gpsimd
        def _(pool):
            G = nc.gpsimd
            def low_weights(n):
                pool.wait_ge(w_hi, n + 1)
                hi, lo = parts_of(n)
                G.tensor_tensor(lo, w_stage[:, n % 2, :], hi, ALU.subtract).then_inc(w_lo, 1)

            def low_rows(t):
                pool.wait_ge(h2_hi, t + 1)
                G.tensor_tensor(h2_parts[:, :, LO, :], x2, h2_parts[:, :, HI, :], ALU.subtract).then_inc(h2_lo, 1)

            pool.wait_ge(mod_ready, 11)
            for t in range(NBLK):
                s, b = t % 2, t // 2
                if s == 0:
                    if b >= 2:
                        pool.wait_ge(idft_done, 2 * (b - 1))
                    for r in range(2):
                        ins = G.tensor_tensor(idft_ga[:, b % 2, r, :], idft_sb[:, r, :], mod_bc[:, b, 0, :], ALU.mult)
                    ins.then_inc(ga_ready, 1)
                pool.wait_ge(rq_ready, t + 1)
                for r in range(2):
                    ins = G.tensor_tensor(z[:, s, QRY, r, :], z[:, s, QRY, r, :], mag[:, s, QRY, :], ALU.mult)
                ins.then_inc(uq_ready, 1)
                pool.wait_ge(uq_ready, t + 1)
                pool.wait_ge(scan_ready, 2 * (t + 1))
                for a in range(2):
                    for r in range(2):
                        ins = G.tensor_tensor(prod[:, a, r, :], s_run[:, s, a, :], z[:, s, QRY, r, :], ALU.mult)
                    ins.then_inc(x1_ready, 1)
                low_weights(2 * t)
                if t >= 1:
                    low_rows(t - 1)
                low_weights(2 * t + 1)
            low_rows(NBLK - 1)
            for n in range(2 * NBLK, W_CHUNKS):
                low_weights(n)

            def wait_turn(signal, value):
                pool.wait_ge(signal, value)
                pool.sem_inc(pool_turn, 1)

            def gather(i, s):
                G.tensor_copy(gather_now[:, s:s + 1], gather_idx[:, bass.ds(i, 1)]).then_inc(gather_set, 1)
                wait_turn(gather_set, i + 1)
                G.indirect_dma_start(out=xg[:, s, :], out_offset=None, in_=h_scratch,
                                     in_offset=bass.IndirectOffsetOnAxis(ap=gather_now[:, s:s + 1], axis=0)
                                     ).then_inc(gathered[s], 16)

            def scatter(i, s):
                wait_turn(y_ready, i + 1)
                G.tensor_copy(scatter_now[:, s:s + 1], scatter_idx[:, bass.ds(i, 1)]).then_inc(scatter_set, 1)
                wait_turn(scatter_set, i + 1)
                G.indirect_dma_start(out=y_scratch,
                                     out_offset=bass.IndirectOffsetOnAxis(ap=scatter_now[:, s:s + 1], axis=0),
                                     in_=y_sb[:, s, :], in_offset=None, bounds_check=PAIRS - 1,
                                     oob_is_err=False).then_inc(scattered[s], 16)

            def clip(i, s):
                wait_turn(gv_ready, i + 1)
                G.tensor_scalar(gv[:, s, 1, :], gv[:, s, 1, :], LIMIT, -LIMIT, ALU.min, ALU.max).then_inc(vclip_done, 1)

            def turn(i, s, more_rows, more, out_rows):
                if more_rows:
                    wait_turn(xg_tp, i + 2)
                    gather(i + 3, 1 - s)
                if more:
                    clip(i + 1, 1 - s)
                if out_rows:
                    scatter(i - 1, 1 - s)

            pool.wait_ge(tiles_ready, 4)
            gather(0, 0)
            gather(1, 1)
            clip(0, 0)
            wait_turn(xg_tp, 1)
            gather(2, 0)
            turn(0, 0, True, True, False)
            turn(1, 1, True, True, True)
            with pool.Fori(1, LOOP_END // 2) as n:
                for s in range(2):
                    turn(2 * n + s, s, True, True, True)
            turn(LOOP_END, 0, False, True, True)
            turn(LOOP_END + 1, 1, False, True, True)
            turn(LOOP_END + 2, 0, False, False, True)
            scatter(MOE_TILES - 1, 0)


def constants():
    f32 = np.float32
    e, k = np.arange(D), np.arange(P)
    turn = 2.0 * np.pi * ((e[:, None] * k[None, :]) % D) / D
    alt = np.where(e % 2 == 0, 1.0, -1.0)
    dft = np.concatenate([np.cos(turn), -np.sin(turn), alt[:, None]], axis=1).astype(f32)
    inv_re = np.cos(turn).T * np.where(k == 0, 1.0, 2.0)[:, None] / D
    inv_im = -np.sin(turn).T * 2.0 / D
    inv_im[0] = alt / D
    idft = np.stack([inv_re, inv_im], axis=1).astype(f32)
    i = np.arange(P)
    tri = np.zeros((P, 4, P), f32)
    tri[:, 0] = i[:, None] <= i[None, :]
    tri[:, 1] = 1.0
    tri[:, 3] = alt[:P, None]
    iota = np.concatenate([np.broadcast_to(i, (P, P)), i[:, None]], axis=1).astype(f32)
    return {"dft": dft.reshape(KD, P, -1).transpose(1, 0, 2), "idft": idft, "ident": np.eye(P, dtype=f32),
            "tri": tri, "iota": iota}


def kernel(L0_attn_x, L0_attn_Wq, L0_attn_bq, L0_attn_Wk, L0_attn_bk, L0_attn_Wv, L0_attn_bv, L0_ffn_gate_w,
           L0_ffn_dense_1_w, L0_ffn_dense_1_b, L0_ffn_dense_2_w, L0_ffn_dense_2_b, L0_c, L0_wmod):
    import concourse.bacc as bacc
    from concourse.bass_utils import run_bass_kernel_spmd

    def rows(a):
        a = np.asarray(a)
        return a.reshape(-1, P, a.shape[-1]).transpose(1, 0, 2)

    w1 = np.asarray(L0_ffn_dense_1_w).reshape(EXPERTS, HID, 2, KD, P)
    w2 = np.asarray(L0_ffn_dense_2_w).reshape(EXPERTS, D, KF, P)
    arrays = {
        "x": np.asarray(L0_attn_x).reshape(TOKENS, D),
        "wqkv": np.stack([rows(w) for w in (L0_attn_Wk, L0_attn_Wv, L0_attn_Wq)], axis=1),
        "bqkv": np.stack([np.asarray(b).reshape(KD, P).T for b in (L0_attn_bk, L0_attn_bv, L0_attn_bq)], axis=2),
        "gate_w": rows(L0_ffn_gate_w),
        "w1": w1.transpose(4, 0, 3, 2, 1).reshape(P, -1),
        "b1": np.asarray(L0_ffn_dense_1_b).reshape(EXPERTS, HID, 2).transpose(0, 2, 1).reshape(-1),
        "w2": w2.transpose(3, 0, 2, 1).reshape(P, -1),
        "b2": np.asarray(L0_ffn_dense_2_b).reshape(-1),
        "c_t": rows(np.asarray(L0_c).T),
        "wmod": rows(L0_wmod),
        **constants(),
    }
    nc = bacc.Bacc("TRN2", target_bir_lowering=False, num_devices=1)
    feed, args = {}, {}
    for name, a in arrays.items():
        a = np.ascontiguousarray(a)
        feed[f"in_{name}"] = a
        args[name] = nc.dram_tensor(f"in_{name}", a.shape, mybir.dt.from_np(a.dtype), kind="ExternalInput").ap()
    out = nc.dram_tensor("out_rows", (TOKENS, D), F32, kind="ExternalOutput").ap()
    adaln_moe_kernel(nc, **args, out=out)
    r = run_bass_kernel_spmd(nc, [feed], core_ids=[0])
    return r.results[0]["out_rows"].reshape(BATCH, SEQ, D)
```

```python
from contextlib import ExitStack

import numpy as np

import concourse.bass as bass
from concourse import mybir

ALU = mybir.AluOpType
ACT = mybir.ActivationFunctionType
F32 = mybir.dt.float32
BF16 = mybir.dt.bfloat16
FP16 = mybir.dt.float16
I32 = mybir.dt.int32
U32 = mybir.dt.uint32
AX_X = mybir.AxisListType.X

P = 128
BATCH, SEQ, D = 4, 1024, 256
TOKENS = BATCH * SEQ
KD = D // P
EXPERTS, HID = 8, 512
KF = HID // P
TOP_K = 2
BLK = 512
NBLK = TOKENS // BLK
TPB = BLK // P
TILES = TOKENS // P
PAIRS = TOKENS * TOP_K
PCOLS = PAIRS // P
MOE_TILES = PAIRS // P + EXPERTS - 1
LOOP_END = MOE_TILES - 3
EPS_UNIT, EPS_LN = 1e-8, 1e-5
ALPHA, LIMIT = 1.702, 9.0
KEY, VAL, QRY = 0, 1, 2
SX, SW, SH = 8.0, 64.0, 16.0
HI, LO = 0, 1
SPLIT = ((HI, HI), (LO, HI), (HI, LO))
WCH = 1024
RE, IM = 0, 1


def psum_plan():
    items = []
    for t in range(-1, NBLK + 2):
        if t + 1 < NBLK:
            items += [("z", t + 1, i) for i in range(6)] + [("ny", t + 1, 0)]
        if 0 <= t < NBLK:
            items.append(("pre", t, 0))
        if t >= 2:
            items.append(("gate", t - 2, 0))
        if 0 <= t < NBLK:
            items.append(("row", t, 0))
    return {item: n for n, item in enumerate(items)}, items


def adaln_moe_kernel(nc, x, wqkv, bqkv, gate_w, w1, b1, w2, b2, c_t, wmod, dft, idft, ident, tri, iota, out):
    place, order = psum_plan()
    ROT = 4
    x_scratch = nc.dram_tensor("x_scratch", (TOKENS, D), F32).ap()
    h_scratch = nc.dram_tensor("h_scratch", (TOKENS, 2 * D), FP16).ap()
    y_scratch = nc.dram_tensor("y_scratch", (PAIRS, D), F32).ap()

    x_blk = x.rearrange("(t j p) d -> t p j d", p=P, j=TPB)
    xs_blk = x_scratch.rearrange("(t j p) d -> t p j d", p=P, j=TPB)
    hs_blk = h_scratch.rearrange("(t j p) d -> t p j d", p=P, j=TPB)
    y_blk = y_scratch.rearrange("(k t j p) d -> k t p j d", p=P, j=TPB, k=TOP_K)
    out_blk = out.rearrange("(t j p) d -> t p j d", p=P, j=TPB)

    with ExitStack() as ctx:
        def sb(name, shape, dt=F32):
            return ctx.enter_context(nc.sbuf_tensor(name, shape, dt))

        def sem(name):
            return ctx.enter_context(nc.semaphore(name))

        def sems(name, n):
            return [sem(f"{name}{i}") for i in range(n)]

        w1_sb = sb("w1_sb", [P, 2, EXPERTS * KD * 2 * HID], FP16)
        w_stage = sb("w_stage", [P, 2, WCH])
        ident_sb = sb("ident_sb", [P, P])
        ident_h = sb("ident_h", [P, P], FP16)
        gb_bc = sb("gb_bc", [P, BATCH, D])
        gates = sb("gates", [P, TILES, EXPERTS])

        REGION = 33296
        region = sb("region", [P, REGION])
        cursor = [0]

        def carve(n):
            cursor[0] += n
            assert cursor[0] <= REGION, cursor
            return region[:, cursor[0] - n:cursor[0]]

        XS = 4
        x_sb = carve(XS * TPB * D).rearrange("p (s j d) -> p s j d", s=XS, j=TPB)
        n_sb = carve(TPB * D).rearrange("p (j d) -> p j d", j=TPB)
        h_t = carve(KD * BLK).rearrange("p (k n) -> p k n", k=KD)
        z_flat = carve(2 * 6 * BLK)
        z = z_flat.rearrange("p (s c r n) -> p s c r n", s=2, c=3, r=2)
        sq = carve(6 * BLK).rearrange("p (c r n) -> p c r n", c=3, r=2)
        m_flat = carve(2 * 3 * BLK)
        mag = m_flat.rearrange("p (s c n) -> p s c n", s=2, c=3)
        den = carve(BLK)
        rec = carve(BLK)
        uk = carve(2 * BLK).rearrange("p (r n) -> p r n", r=2)
        p_flat = carve(4 * BLK)
        prod = p_flat.rearrange("p (a r n) -> p a r n", a=2, r=2)
        s_flat = carve(4 * BLK)
        s_run = s_flat.rearrange("p (s r n) -> p s r n", s=2, r=2)
        x2 = carve(TPB * D).rearrange("p (j d) -> p j d", j=TPB)
        h2_parts = carve(TPB * D).bitcast(FP16).rearrange("p (j a d) -> p j a d", j=TPB, a=2)
        mod_bc = carve(BATCH * 3 * D).rearrange("p (b m d) -> p b m d", b=BATCH, m=3)
        NF = 2 * P + 1
        w_spec = carve(3 * KD * NF).rearrange("p (c k f) -> p c k f", c=3, k=KD)
        idft_sb = carve(2 * D).rearrange("p (r d) -> p r d", r=2)
        idft_ga = carve(2 * 2 * D).rearrange("p (s r d) -> p s r d", s=2, r=2)
        gate_h = carve(KD * EXPERTS).bitcast(FP16).rearrange("p (a k e) -> p a k e", a=2, k=KD)
        tri_sb = carve(2 * P).rearrange("p (a n) -> p a n", a=2)
        bias_f = carve(9)
        sca_t = carve(4 * BATCH).rearrange("p (w k b) -> p w k b", w=2, k=KD)
        stats = carve(2 * TPB * 6).rearrange("p (w j s) -> p w j s", w=2, j=TPB)
        mv = carve(2 * TPB * 2).rearrange("p (w j s) -> p w j s", w=2, j=TPB)
        mv1 = carve(2 * TPB * 2).rearrange("p (s j a) -> p s j a", s=2, j=TPB)
        rstd = carve(3 * TPB).rearrange("p (w j) -> p w j", w=3)
        ny = carve(3 * TPB).rearrange("p (j c) -> p j c", j=TPB)
        ny_abs = carve(3 * TPB).rearrange("p (j c) -> p j c", j=TPB)
        ny_unit = carve(3 * TPB).rearrange("p (j c) -> p j c", j=TPB)
        ny_kv = carve(TPB)
        ny_tot = carve(2 * (TPB + 1)).rearrange("p (s j) -> p s j", s=2)
        ny_pre = carve(TPB)
        ny_g = carve(TPB)
        wmod_sb = z_flat[:, 0:KD * 6 * D].rearrange("p (k n) -> p k n", k=KD)
        mod_tmp = s_flat[:, 0:BATCH * D].rearrange("p (b d) -> p b d", b=BATCH)
        wraw = m_flat[:, 0:3 * KD * D].rearrange("p (c k d) -> p c k d", c=3, k=KD)
        silu_rep = p_flat[:, 0:KD * BATCH * P].rearrange("p (k b m) -> p k b m", k=KD, b=BATCH)
        dft_sb = uk[:, :, :].rearrange("p r n -> p (r n)")[:, 0:KD * NF].rearrange("p (k f) -> p k f", k=KD)
        alt_rep = den[:, 0:P]
        bq_sb = rec[:, 0:KD * 3].rearrange("p (k c) -> p k c", k=KD)
        c_sb = rec[:, 16:16 + KD * BATCH].rearrange("p (k b) -> p k b", k=KD)
        c_sig = rec[:, 32:32 + KD * BATCH].rearrange("p (k b) -> p k b", k=KD)
        c_silu = rec[:, 48:48 + KD * BATCH].rearrange("p (k b) -> p k b", k=KD)
        gate_sb = rec[:, 64:64 + KD * EXPERTS].rearrange("p (k e) -> p k e", k=KD)

        cursor[0] = 0
        w2_sb = carve(EXPERTS * KF * D).bitcast(FP16).rearrange("p (a n) -> p a n", a=2)
        b1_bc = carve(EXPERTS * 2 * HID)
        b2_bc = carve(EXPERTS * D)
        xg = carve(2 * D).bitcast(FP16).rearrange("p (s d) -> p s d", s=2)
        xg_t = carve(2 * D).bitcast(FP16).rearrange("p (s n) -> p s n", s=2)
        gv = carve(2 * 2 * HID).rearrange("p (s a f) -> p s a f", s=2, a=2)
        sig = w_stage[:, 0, 0:2 * HID].rearrange("p (s f) -> p s f", s=2)
        hid = carve(2 * HID).bitcast(FP16).rearrange("p (s a f) -> p s a f", s=2, a=2)
        hid_t = carve(2 * HID).bitcast(FP16).rearrange("p (s n) -> p s n", s=2)
        y_sb = w_stage[:, 1, 0:2 * D].rearrange("p (s d) -> p s d", s=2)
        gather_idx = carve(MOE_TILES).bitcast(I32)
        scatter_idx = carve(MOE_TILES).bitcast(I32)
        tile_expert = carve(MOE_TILES).bitcast(I32)
        gather_now = carve(2).bitcast(I32)
        scatter_now = carve(2).bitcast(I32)
        pair_w = carve(PCOLS).rearrange("p (k t) -> p k t", k=TOP_K)
        x2_lo = cursor[0]
        GRP = 8
        d_x = carve(TILES * D).rearrange("p (t j d) -> p t j d", t=NBLK, j=TPB)
        cursor[0] = x2_lo
        best = carve(TILES * 8).rearrange("p (t e) -> p t e", e=8)
        best_i = carve(TILES * 8).bitcast(U32).rearrange("p (t e) -> p t e", e=8)
        pick = carve(PCOLS)
        onehot = carve(PCOLS * EXPERTS).rearrange("p (c e) -> p c e", e=EXPERTS)
        onehot_b = carve(PCOLS * EXPERTS // 2).bitcast(BF16)
        rank = carve(PCOLS * EXPERTS)
        tot = carve(PCOLS * EXPERTS).rearrange("p (c e) -> p c e", e=EXPERTS)
        cum = carve(EXPERTS * (PCOLS + 1)).rearrange("p (e c) -> p e c", e=EXPERTS)
        small = carve(16 * EXPERTS).rearrange("p (a e) -> p a e", e=EXPERTS)
        slot = carve(PCOLS)
        slot_i = carve(2 * PCOLS).bitcast(I32).rearrange("p (a c) -> p a c", a=2)
        slot_hl = carve(2 * PCOLS).rearrange("p (a c) -> p a c", a=2)
        tri_b = carve(P).bitcast(BF16).rearrange("p (a n) -> p a n", a=2)
        pw_tmp = carve(2 * TILES).rearrange("p (a t) -> p a t", a=2)
        lo_hot = carve(2 * GRP * P).rearrange("p (s c n) -> p s c n", s=2, c=GRP)
        hi_hot = carve(2 * GRP * MOE_TILES).rearrange("p (s c n) -> p s c n", s=2, c=GRP)
        pair_no = carve(PCOLS)
        te_cmp = carve(MOE_TILES * EXPERTS).rearrange("p (i e) -> p i e", e=EXPERTS)
        perm = carve(4 * MOE_TILES).rearrange("p (a i) -> p a i", a=4)
        strict_f = carve(P)
        iota_all = carve(P + 1)
        iota_sb = iota_all[:, 0:P]
        pcol = iota_all[:, P:P + 1]
        cursor[0] = 0
        d_y = carve(NBLK * TOP_K * TPB * D).rearrange("p (t k j d) -> p t k j d", t=NBLK, k=TOP_K, j=TPB)

        ps = ctx.enter_context(nc.psum_tensor("ps", [P, 8, 512], F32))
        TP, OUT, ROT0 = 0, 2, 4

        def rot(item):
            return ps[:, ROT0 + place[item] % ROT, :]

        const_in, wmod_in, wraw_in, w1_in, w2_in, bias_in = (sem(n) for n in (
            "const_in", "wmod_in", "wraw_in", "w1_in", "w2_in", "bias_in"))
        x_in = sems("x_in", XS)
        x2_out, h2_out = sem("x2_out"), sem("h2_out")
        (sig_done, silu_done, rep_done, pe_setup, act_setup, mod_mm, mod_copied, mod_ready, ga_ready,
         ln1_stats, ln1_agg, ln1_var, ln1_std, ln1_rstd, n_ready, tp_done, ht_ready, z_mm, z_ready, sq_ready,
         mag_ready, root_ready, eps_ready, den_ready, all_ready, rec_ready, rkv_ready, rq_ready, uk_ready,
         prod_ready, scan_ready, uq_ready, x1_ready, g_ready, nymm, ny_read, ny_absd, ny_rec, ny_unitd, ny_kvd,
         pre_mm, tot_read, ny_sum, ny_done, row_mm, row_ready, idft_done, x2_ready, ln2_stats,
         ln2_agg, ln2_var, ln2_std, ln2_rstd, h2_mid, h2_ready, tp2_done, h2t_ready, gate_mm, gate_ready) = (
            sem(n) for n in (
                "sig_done silu_done rep_done pe_setup act_setup mod_mm mod_copied mod_ready ga_ready "
                "ln1_stats ln1_agg ln1_var ln1_std ln1_rstd n_ready tp_done ht_ready z_mm z_ready sq_ready "
                "mag_ready root_ready eps_ready den_ready all_ready rec_ready rkv_ready rq_ready uk_ready "
                "prod_ready scan_ready uq_ready x1_ready g_ready nymm ny_read ny_absd ny_rec ny_unitd ny_kvd "
                "pre_mm tot_read ny_sum ny_done row_mm row_ready idft_done x2_ready ln2_stats "
                "ln2_agg ln2_var ln2_std ln2_rstd h2_mid h2_ready tp2_done h2t_ready gate_mm gate_ready").split())
        (route, cast_done, rank_mm, w_exp, hi_made, perm_mm, tiles_ready, w_sub) = (
            sem(n) for n in "route cast_done rank_mm w_exp hi_made perm_mm tiles_ready w_sub".split())
        w_in = sems("w_in", 2)
        iota_in = sem("iota_in")
        w_scaled, w_hi, w_lo, gate_split, h2_hi, h2_lo, hid_hi, x2_in = (sem(n) for n in (
            "w_scaled w_hi w_lo gate_split h2_hi h2_lo hid_hi x2_in").split())
        gathered = sems("gathered", 2)
        scattered = sems("scattered", 2)
        gather_set, scatter_set, pool_turn = sem("gather_set"), sem("scatter_set"), sem("pool_turn")
        (gsig_ready, vclip_done, xg_tp, xgt_ready, up_done, gv_ready, clip_done, sig_ready, glu_ready, hid_ready, hid_tp, hidt_ready,
         down_done, y_ready) = (sem(n) for n in (
            "gsig_ready vclip_done xg_tp xgt_ready up_done gv_ready clip_done sig_ready glu_ready hid_ready hid_tp hidt_ready "
            "down_done y_ready").split())
        d_in, d_out = sems("d_in", NBLK), sem("d_out")
        d_w1, d_w2, d_gb, d_ready = (sem(n) for n in "d_w1 d_w2 d_gb d_ready".split())

        block = ctx.enter_context(nc.Block())

        def bank_free(e, item):
            n = place[item] - ROT
            if n >= 0:
                kind, t, i = order[n]
                s, v = {"z": (z_ready, 6 * t + i + 1), "ny": (ny_read, t + 1), "pre": (ny_sum, 2 * t + 2),
                        "gate": (gate_ready, t + 1), "row": (row_ready, t + 1)}[kind]
                e.wait_ge(s, v)

        W1_CHUNKS = EXPERTS * KD * 2 * HID // WCH
        W_CHUNKS = W1_CHUNKS + EXPERTS * KF * D // WCH

        def load_weights(sp, n):
            if n >= 2:
                sp.wait_ge(w_hi, n - 1)
                sp.wait_ge(w_lo, n - 1)
            src = w1[:, n * WCH:(n + 1) * WCH] if n < W1_CHUNKS else w2[:, (n - W1_CHUNKS) * WCH:
                                                                         (n - W1_CHUNKS + 1) * WCH]
            sp.dma_start(w_stage[:, n % 2, :], src).then_inc(w_in[n % 2], 16)

        def parts_of(n):
            if n < W1_CHUNKS:
                return [w1_sb[:, a, n * WCH:(n + 1) * WCH] for a in (HI, LO)]
            return [w2_sb[:, a, (n - W1_CHUNKS) * WCH:(n - W1_CHUNKS + 1) * WCH] for a in (HI, LO)]

        @block.sync
        def _(sp):
            sp.dma_start(c_sb, c_t).then_inc(const_in, 16)
            sp.dma_start(dft_sb, dft[:, :, 0:NF]).then_inc(const_in, 16)
            sp.dma_start(alt_rep, tri[:, 3, :]).then_inc(const_in, 16)
            sp.dma_start(bq_sb, bqkv).then_inc(const_in, 16)
            sp.dma_start(ident_sb[:], ident).then_inc(const_in, 16)
            sp.dma_start(idft_sb, idft).then_inc(const_in, 16)
            sp.dma_start(gate_sb, gate_w).then_inc(const_in, 16)
            sp.dma_start(tri_sb, tri[:, 0:2, :]).then_inc(const_in, 16)
            sp.dma_start(wraw, wqkv).then_inc(wraw_in, 16)
            sp.dma_start(wmod_sb, wmod).then_inc(wmod_in, 16)
            for t in range(XS):
                sp.dma_start(x_sb[:, t], x_blk[t]).then_inc(x_in[t], 16)
            for n in range(2):
                load_weights(sp, n)
            for t in range(NBLK):
                sp.wait_ge(x2_ready, t + 1)
                sp.dma_start(xs_blk[t], x2).then_inc(x2_out, 16)
                if t + XS < NBLK:
                    sp.dma_start(x_sb[:, (t + XS) % XS], x_blk[t + XS]).then_inc(x_in[t % XS], 16)
                for n in (2 * t + 2, 2 * t + 3):
                    load_weights(sp, n)
                sp.wait_ge(h2_lo, t + 1)
                sp.dma_start(hs_blk[t], h2_parts.rearrange("p j a d -> p j (a d)")).then_inc(h2_out, 16)
            sp.wait_ge(gate_ready, NBLK)
            sp.wait_ge(x2_out, 16 * NBLK)
            sp.wait_ge(h2_out, 16 * NBLK)
            sp.wait_ge(tp2_done, KD * NBLK)
            sp.wait_ge(idft_done, NBLK)
            sp.dma_start(iota_all, iota).then_inc(iota_in, 16)
            for e in range(EXPERTS):
                if 2 * NBLK + 2 + e < W_CHUNKS:
                    load_weights(sp, 2 * NBLK + 2 + e)
                at = slice(e * 2 * HID, (e + 1) * 2 * HID)
                sp.dma_start(b1_bc[:, at], b1[at].partition_broadcast(P)).then_inc(bias_in, 16)
            sp.dma_start(b2_bc, b2.partition_broadcast(P)).then_inc(bias_in, 16)
            sp.wait_ge(tiles_ready, 4)
            for t in range(NBLK):
                sp.wait_ge(y_ready, MOE_TILES // NBLK * t + 1)
                sp.dma_start(d_x[:, t], xs_blk[t]).then_inc(x2_in, 16)
            sp.wait_ge(y_ready, MOE_TILES)
            for i in range(2):
                sp.wait_ge(scattered[i], 16 * ((MOE_TILES + 1 - i) // 2))
            for t in range(NBLK):
                for k in range(TOP_K):
                    sp.dma_start(d_y[:, t, k], y_blk[k, t]).then_inc(d_in[t], 16)
            for t in range(NBLK):
                sp.wait_ge(d_ready, t + 1)
                sp.dma_start(out_blk[t], d_x[:, t]).then_inc(d_out, 16)
            sp.wait_ge(d_out, 16 * NBLK)

        @block.tensor
        def _(pe):
            def transform_weights():
                pe.wait_ge(const_in, 128)
                pe.wait_ge(wraw_in, 16)
                for c in range(3):
                    for kd in range(KD):
                        for ke in range(KD):
                            mm = pe.matmul(ps[:, c * KD + kd, 0:NF], wraw[:, c, ke, kd * P:(kd + 1) * P],
                                           dft_sb[:, ke, :], start=(ke == 0), stop=(ke == KD - 1))
                        mm.then_inc(pe_setup, 1)
                for r in range(3):
                    for ke in range(KD):
                        lhs = dft_sb[:, ke, r * P:(r + 1) * P] if r < 2 else alt_rep
                        mm = pe.matmul(ps[:, 6, 3 * r:3 * r + 3], lhs, bq_sb[:, ke, :],
                                       start=(ke == 0), stop=(ke == KD - 1))
                mm.then_inc(pe_setup, 1)
                pe.wait_ge(wmod_in, 16)
                pe.wait_ge(silu_done, 1)
                for w in range(2):
                    for kd in range(KD):
                        for ke in range(KD):
                            at = w * D + kd * P
                            mm = pe.matmul(ps[:, 7, (w * KD + kd) * BATCH:(w * KD + kd + 1) * BATCH],
                                           wmod_sb[:, ke, at:at + P], c_silu[:, ke, :],
                                           start=(ke == 0), stop=(ke == KD - 1))
                mm.then_inc(pe_setup, 1)

            def broadcast_modulation():
                pe.wait_ge(rep_done, 1)
                for b in range(BATCH):
                    for half in range(2):
                        n = 2 * b + half
                        pe.wait_ge(act_setup, n + 1)
                        for ke in range(KD):
                            mm = pe.matmul(ps[:, n, :], silu_rep[:, ke, b, :],
                                           wmod_sb[:, ke, (2 + 2 * half) * D:(4 + 2 * half) * D],
                                           start=(ke == 0), stop=(ke == KD - 1))
                        mm.then_inc(mod_mm, 1)
                pe.wait_ge(mod_copied, 2 * BATCH)

            def transpose_rows(src, t, done):
                for k in range(KD):
                    for j in range(TPB):
                        mm = pe.transpose(ps[:, TP + k, j * P:(j + 1) * P], src[:, j, k * P:(k + 1) * P],
                                          ident_sb[:])
                    mm.then_inc(done, 1)

            def project(t):
                pe.wait_ge(n_ready, TPB * (t + 1))
                if t >= 1:
                    pe.wait_ge(ht_ready, KD * t)
                if t >= 4:
                    pe.wait_ge(h2t_ready, KD * (t - 3))
                transpose_rows(n_sb, t, tp_done)
                pe.wait_ge(ht_ready, KD * (t + 1))
                for i in range(6):
                    c, r = i // 2, i % 2
                    bank_free(pe, ("z", t, i))
                    for k in range(KD):
                        mm = pe.matmul(rot(("z", t, i)), w_spec[:, c, k, r * P:(r + 1) * P], h_t[:, k, :],
                                       start=(k == 0), stop=(k == KD - 1))
                    mm.then_inc(z_mm, 1)
                bank_free(pe, ("ny", t, 0))
                for j in range(TPB):
                    for k in range(KD):
                        mm = pe.matmul(rot(("ny", t, 0))[:, 3 * j:3 * j + 3], h_t[:, k, j * P:(j + 1) * P],
                                       w_spec[:, :, k, 2 * P], start=(k == 0), stop=(k == KD - 1))
                mm.then_inc(nymm, 1)

            def nyquist_sums(t):
                pe.wait_ge(ny_kvd, t + 1)
                bank_free(pe, ("pre", t, 0))
                pe.matmul(rot(("pre", t, 0))[:, 0:TPB], tri_sb[:, 0, :], ny_kv, start=True, stop=True)
                pe.matmul(rot(("pre", t, 0))[:, TPB:2 * TPB], tri_sb[:, 1, :], ny_kv, start=True,
                          stop=True).then_inc(pre_mm, 1)

            def gate_rows(t):
                pe.wait_ge(h2_lo, t + 1)
                pe.wait_ge(ht_ready, KD * min(t + 4, NBLK))
                for k in range(KD):
                    bank = ps[:, TP + k, :].bitcast(FP16)
                    for a in (HI, LO):
                        for j in range(TPB):
                            mm = pe.transpose(bank[:, a * BLK + j * P:a * BLK + (j + 1) * P],
                                              h2_parts[:, j, a, k * P:(k + 1) * P], ident_h[:])
                    mm.then_inc(tp2_done, 1)

            def gate(t):
                pe.wait_ge(h2t_ready, KD * (t + 1))
                bank_free(pe, ("gate", t, 0))
                for j in range(TPB):
                    n = 0
                    for k in range(KD):
                        cols = h_t[:, k, :].bitcast(FP16)
                        for xa, wa in SPLIT:
                            mm = pe.matmul(rot(("gate", t, 0))[:, j * EXPERTS:(j + 1) * EXPERTS],
                                           cols[:, xa * BLK + j * P:xa * BLK + (j + 1) * P], gate_h[:, wa, k, :],
                                           start=(n == 0), stop=(n == 3 * KD - 1))
                            n += 1
                mm.then_inc(gate_mm, 1)

            def nyquist_row(t):
                pe.wait_ge(ny_done, t + 1)
                bank_free(pe, ("row", t, 0))
                for j in range(TPB):
                    mm = pe.transpose(rot(("row", t, 0))[0:1, j * P:(j + 1) * P], ny_g[:, j:j + 1], ident_sb[:])
                mm.then_inc(row_mm, 1)

            def inverse(t):
                pe.wait_ge(row_ready, t + 1)
                pe.wait_ge(g_ready, 2 * (t + 1))
                pe.wait_ge(ga_ready, t // 2 + 1)
                if t >= 1:
                    pe.wait_ge(x2_ready, t)
                for j in range(TPB):
                    for r in range(2):
                        mm = pe.matmul(ps[:, OUT + j // 2, (j % 2) * D:(j % 2 + 1) * D],
                                       prod[:, 0, r, j * P:(j + 1) * P], idft_ga[:, (t // 2) % 2, r, :],
                                       start=(r == 0), stop=(r == 1))
                mm.then_inc(idft_done, 1)

            transform_weights()
            broadcast_modulation()
            for t in range(-1, NBLK + 2):
                if t + 1 < NBLK:
                    project(t + 1)
                if t >= 2:
                    gate_rows(t - 2)
                if 0 <= t < NBLK:
                    nyquist_sums(t)
                if t >= 2:
                    gate(t - 2)
                if 0 <= t < NBLK:
                    nyquist_row(t)
                    inverse(t)

            pe.wait_ge(cast_done, 1)
            pe.matmul(ps[:, 0, :], tri_b[:, 0, :], onehot_b, start=True, stop=True)
            pe.matmul(ps[:, 1, :], tri_b[:, 1, :], onehot_b, start=True, stop=True).then_inc(rank_mm, 1)
            for c in range(PCOLS):
                g = c // GRP % 2
                pe.wait_ge(hi_made, c + 1)
                pe.matmul(ps[:, 2, 0:MOE_TILES], lo_hot[:, g, c % GRP, :], hi_hot[:, g, c % GRP, :],
                          start=(c == 0), stop=(c == PCOLS - 1)).then_inc(perm_mm, 1)

            XT, HT, YB, GV = 0, 1, 2, 4

            def expert(i):
                return pe.value_load(tile_expert[0:1, bass.ds(i, 1)], min_val=0, max_val=EXPERTS - 1)

            def rows_in(s, wait):
                pe.wait_ge(gathered[s], wait)
                for q in range(2 * KD):
                    mm = pe.transpose(ps[:, XT, :].bitcast(FP16)[:, q * P:(q + 1) * P],
                                      xg[:, s, q * P:(q + 1) * P], ident_h[:])
                mm.then_inc(xg_tp, 1)

            def up(i, s, e, halves=(0, 1)):
                pe.wait_ge(xgt_ready, i + 1)
                for a in halves:
                    n = 0
                    for k in range(KD):
                        for wa in (HI, LO):
                            w = w1_sb[:, wa, bass.ds(e * (KD * 2 * HID) + (k * 2 + a) * HID, HID)]
                            for xa in (HI, LO)[:2 - wa]:
                                mm = pe.matmul(ps[:, GV + 2 * s + a, :],
                                               xg_t[:, s, (xa * KD + k) * P:(xa * KD + k + 1) * P], w,
                                               start=(n == 0), stop=(n == 3 * KD - 1))
                                n += 1
                if 1 in halves:
                    mm.then_inc(up_done, 1)

            def hidden_in(i, s):
                pe.wait_ge(hid_ready, i + 1)
                for q in range(2 * KF):
                    mm = pe.transpose(ps[:, HT, :].bitcast(FP16)[:, q * P:(q + 1) * P],
                                      hid[:, s, q // KF, (q % KF) * P:(q % KF + 1) * P], ident_h[:])
                mm.then_inc(hid_tp, 1)

            def down(i, s, e, chunks):
                pe.wait_ge(hidt_ready, i + 1)
                n = 3 * chunks[0]
                for k in chunks:
                    for wa in (HI, LO):
                        w = w2_sb[:, wa, bass.ds(e * (KF * D) + k * D, D)]
                        for xa in (HI, LO)[:2 - wa]:
                            mm = pe.matmul(ps[:, YB + s, 0:D],
                                           hid_t[:, s, (xa * KF + k) * P:(xa * KF + k + 1) * P], w,
                                           start=(n == 0), stop=(n == 3 * KF - 1))
                            n += 1
                if chunks[-1] == KF - 1:
                    mm.then_inc(down_done, 1)

            def turn(i, s, rows_wait, more=True, hidden=True, first=False):
                e = expert(i)
                if more and s == 1:
                    e_up = expert(i + 3)
                if rows_wait is not None:
                    pe.wait_ge(xgt_ready, i + 3)
                    rows_in(1 - s, rows_wait)
                if not first:
                    pe.wait_ge(y_ready, i - 1)
                down(i, s, e, range(KF // 2))
                if more and s == 0:
                    e_up = expert(i + 3)
                down(i, s, e, range(KF // 2, KF))
                if more:
                    pe.wait_ge(gv_ready, i + 2)
                    up(i + 3, 1 - s, e_up, (0,))
                if hidden:
                    hidden_in(i + 1, 1 - s)
                if more:
                    up(i + 3, 1 - s, e_up, (1,))

            pe.wait_ge(w_hi, W_CHUNKS)
            pe.wait_ge(w_lo, W_CHUNKS)
            pe.wait_ge(tiles_ready, 4)
            rows_in(0, 16)
            pe.wait_ge(xgt_ready, 1)
            rows_in(1, 16)
            up(0, 0, expert(0))
            pe.wait_ge(xgt_ready, 2)
            rows_in(0, 32)
            up(1, 1, expert(1))
            e2 = expert(2)
            pe.wait_ge(gv_ready, 1)
            up(2, 0, e2, (0,))
            hidden_in(0, 0)
            up(2, 0, e2, (1,))
            turn(0, 0, 32, first=True)
            turn(1, 1, 48, first=True)
            with pe.Fori(1, MOE_TILES // 2 - 1) as n:
                turn(2 * n, 0, 16 * (n + 2))
                turn(2 * n + 1, 1, 16 * (n + 3))
            turn(MOE_TILES - 3, 0, None, more=False)
            turn(MOE_TILES - 2, 1, None, more=False)
            turn(MOE_TILES - 1, 0, None, more=False, hidden=False)

        @block.scalar
        def _(act):
            act.wait_ge(const_in, 128)
            nc.scalar.activation(c_sig, c_sb, ACT.Sigmoid).then_inc(sig_done, 1)
            for n in range(6):
                act.wait_ge(pe_setup, n + 1)
                nc.scalar.activation(w_spec[:, n // KD, n % KD, :], ps[:, n, 0:NF], ACT.Copy).then_inc(act_setup, 1)
            act.wait_ge(pe_setup, 7)
            nc.scalar.activation(bias_f, ps[:, 6, 0:9], ACT.Copy).then_inc(act_setup, 1)
            act.wait_ge(pe_setup, 8)
            nc.scalar.activation(sca_t.rearrange("p w k b -> p (w k b)"), ps[:, 7, 0:4 * BATCH],
                                 ACT.Copy).then_inc(act_setup, 1)
            for b in range(BATCH):
                act.wait_ge(mod_mm, 2 * b + 1)
                nc.scalar.activation(mod_bc[:, b, 0:2, :], ps[:, 2 * b, :].rearrange("p (m d) -> p m d", m=2),
                                     ACT.Copy).then_inc(mod_copied, 1)
                act.wait_ge(mod_mm, 2 * b + 2)
                nc.scalar.activation(mod_bc[:, b, 2, :], ps[:, 2 * b + 1, 0:D], ACT.Copy)
                nc.scalar.activation(gb_bc[:, b, :], ps[:, 2 * b + 1, D:2 * D], ACT.Copy).then_inc(mod_copied, 1)

            def project(t):
                act.wait_ge(ln1_var, t + 1)
                nc.scalar.activation(rstd[:, t % 2, :], rstd[:, t % 2, :], ACT.Sqrt).then_inc(ln1_std, 1)

            def spectra(t):
                b = t // 2
                if t == 0:
                    act.wait_ge(mod_ready, 1)
                for k in range(KD):
                    act.wait_ge(tp_done, KD * t + k + 1)
                    if k == 0 and t >= 1:
                        act.wait_ge(nymm, t)
                    if k == 0 and t >= 4:
                        act.wait_ge(gate_mm, t - 3)
                    nc.scalar.activation(h_t[:, k, :], ps[:, TP + k, :], ACT.Identity,
                                         bias=sca_t[:, 0, k, b:b + 1],
                                         scale=sca_t[:, 1, k, b:b + 1]).then_inc(ht_ready, 1)

            def evacuate(t):
                if t >= 2:
                    act.wait_ge(uq_ready, t - 1)
                    act.wait_ge(prod_ready, 2 * (t - 1))
                for i in range(6):
                    c, r = i // 2, i % 2
                    act.wait_ge(z_mm, 6 * t + i + 1)
                    nc.scalar.activation(z[:, t % 2, c, r, :], rot(("z", t, i)), ACT.Identity,
                                         bias=bias_f[:, 3 * r + c:3 * r + c + 1]).then_inc(z_ready, 1)

            def squares(t):
                if t >= 1:
                    act.wait_ge(mag_ready, t)
                for c in range(3):
                    act.wait_ge(z_ready, 6 * t + 2 * c + 2)
                    nc.scalar.activation(sq[:, c], z[:, t % 2, c], ACT.Square).then_inc(sq_ready, 1)

            def std2(t):
                act.wait_ge(ln2_var, t + 1)
                nc.scalar.activation(rstd[:, 2, :], rstd[:, 2, :], ACT.Sqrt).then_inc(ln2_std, 1)

            def roots(t):
                act.wait_ge(mag_ready, t + 1)
                nc.scalar.activation(mag[:, t % 2], mag[:, t % 2], ACT.Sqrt).then_inc(root_ready, 1)

            def gate_rows(t):
                for k in range(KD):
                    act.wait_ge(tp2_done, KD * t + k + 1)
                    if k == 0:
                        act.wait_ge(nymm, min(t + 4, NBLK))
                    nc.scalar.activation(h_t[:, k, :].bitcast(FP16), ps[:, TP + k, :].bitcast(FP16),
                                         ACT.Copy).then_inc(h2t_ready, 1)

            def gate(t):
                act.wait_ge(gate_mm, t + 1)
                nc.scalar.activation(gates[:, t * TPB:(t + 1) * TPB, :],
                                     rot(("gate", t, 0))[:, 0:TPB * EXPERTS].rearrange("p (j e) -> p j e", j=TPB),
                                     ACT.Copy, scale=1.0 / (SX * SW)).then_inc(gate_ready, 1)

            def split_rows(t):
                act.wait_ge(h2_ready, TPB * (t + 1))
                if t >= 1:
                    act.wait_ge(h2_out, 16 * t)
                    act.wait_ge(tp2_done, KD * t)
                nc.scalar.activation(h2_parts[:, :, HI, :], x2, ACT.Copy).then_inc(h2_hi, 1)

            def split_weights(n):
                act.wait_ge(w_in[n % 2], 16 * (n // 2 + 1))
                nc.scalar.activation(w_stage[:, n % 2, :], w_stage[:, n % 2, :], ACT.Copy,
                                     scale=SW).then_inc(w_scaled, 1)
                act.wait_ge(w_scaled, n + 1)
                nc.scalar.activation(parts_of(n)[HI], w_stage[:, n % 2, :], ACT.Copy).then_inc(w_hi, 1)

            def nyquist_row(t):
                act.wait_ge(row_mm, t + 1)
                act.wait_ge(g_ready, 2 * (t + 1))
                nc.scalar.activation(prod[0:1, 0, IM, :], rot(("row", t, 0))[0:1, :], ACT.Copy).then_inc(row_ready, 1)

            project(0)
            project(1)
            for t in range(-1, NBLK + 2):
                if t + 1 < NBLK:
                    spectra(t + 1)
                    evacuate(t + 1)
                if t >= 2:
                    gate_rows(t - 2)
                if t + 1 < NBLK:
                    squares(t + 1)
                if t >= 2:
                    gate(t - 2)
                if 0 <= t < NBLK:
                    nyquist_row(t)
                if 1 <= t <= NBLK:
                    std2(t - 1)
                if t >= 0 and t + 2 < NBLK:
                    project(t + 2)
                if 0 <= t < NBLK:
                    split_weights(2 * t)
                    split_weights(2 * t + 1)
                if t + 1 < NBLK:
                    roots(t + 1)
                if 1 <= t <= NBLK:
                    split_rows(t - 1)

            for n in range(2 * NBLK, W_CHUNKS):
                split_weights(n)
            act.wait_ge(w_sub, 1)
            nc.scalar.activation(pw_tmp[:, 1, :], pw_tmp[:, 0, :], ACT.Exp).then_inc(w_exp, 1)

            def rows_in(i, s):
                act.wait_ge(xg_tp, i + 1)
                nc.scalar.activation(xg_t[:, s, :], ps[:, 0, :].bitcast(FP16)[:, 0:2 * D], ACT.Copy).then_inc(xgt_ready, 1)

            def sigmoid(i, s):
                act.wait_ge(clip_done, i + 1)
                nc.scalar.activation(sig[:, s, :], gv[:, s, 0, :], ACT.Sigmoid, scale=ALPHA).then_inc(sig_ready, 1)

            def turn(i, s, more_rows, more_gates):
                act.wait_ge(glu_ready, i + 1)
                if not isinstance(i, int) or i >= 2:
                    act.wait_ge(hid_tp, i - 1)
                nc.scalar.activation(hid[:, s, HI, :], gv[:, s, 0, :], ACT.Copy, scale=SH).then_inc(hid_hi, 1)
                if more_rows:
                    rows_in(i + 2, s)
                if more_gates:
                    sigmoid(i + 1, 1 - s)
                act.wait_ge(hid_tp, i + 1)
                if not isinstance(i, int) or i >= 2:
                    act.wait_ge(down_done, i - 1)
                nc.scalar.activation(hid_t[:, s, :], ps[:, 1, :].bitcast(FP16), ACT.Copy).then_inc(hidt_ready, 1)

            rows_in(0, 0)
            rows_in(1, 1)
            sigmoid(0, 0)
            for s in range(2):
                turn(s, s, True, True)
            with act.Fori(1, LOOP_END // 2) as n:
                for s in range(2):
                    turn(2 * n + s, s, True, True)
            turn(LOOP_END, 0, True, True)
            turn(LOOP_END + 1, 1, False, True)
            turn(LOOP_END + 2, 0, False, False)

            for t in range(NBLK):
                act.wait_ge(d_in[t], 16 * TOP_K)
                for j in range(TPB):
                    nc.scalar.activation(d_y[:, t, 0, j, :], d_y[:, t, 0, j, :], ACT.Copy,
                                         scale=pair_w[:, 0, t * TPB + j:t * TPB + j + 1]).then_inc(d_w1, 1)

        @block.vector
        def _(dve):
            V = nc.vector
            dve.wait_ge(sig_done, 1)
            V.tensor_tensor(c_silu, c_sb, c_sig, ALU.mult).then_inc(silu_done, 1)
            dve.wait_ge(silu_done, 1)
            V.tensor_copy(silu_rep, c_silu.unsqueeze(3).to_broadcast([P, KD, BATCH, P])).then_inc(rep_done, 1)
            V.tensor_copy(ident_h[:], ident_sb[:]).then_inc(gate_split, 1)
            V.tensor_scalar(gate_sb, gate_sb, SW, None, ALU.mult).then_inc(gate_split, 1)
            dve.wait_ge(gate_split, 2)
            V.tensor_copy(gate_h[:, HI], gate_sb).then_inc(gate_split, 1)
            dve.wait_ge(gate_split, 3)
            V.tensor_tensor(gate_h[:, LO], gate_sb, gate_h[:, HI], ALU.subtract).then_inc(gate_split, 1)
            dve.wait_ge(act_setup, 8)
            V.tensor_scalar(sca_t[:, 1], sca_t[:, 1], 1.0, None, ALU.add).then_inc(mod_ready, 1)

            def clamp_gain(g, n):
                V.tensor_scalar(mod_tmp, g, 0.0, 2.0, ALU.is_ge, ALU.mult).then_inc(mod_ready, 1)
                dve.wait_ge(mod_ready, n + 1)
                V.scalar_tensor_tensor(out=g, in0=g, scalar=-1.0, in1=g, op0=ALU.mult,
                                       op1=ALU.max).then_inc(mod_ready, 1)
                dve.wait_ge(mod_ready, n + 2)
                V.tensor_scalar(g, g, 0.25, None, ALU.max).then_inc(mod_ready, 1)
                dve.wait_ge(mod_ready, n + 3)
                V.scalar_tensor_tensor(out=g, in0=mod_tmp, scalar=-1.0, in1=g, op0=ALU.add,
                                       op1=ALU.mult).then_inc(mod_ready, 1)
                dve.wait_ge(mod_ready, n + 4)

            def modulation():
                dve.wait_ge(mod_copied, 2 * BATCH)
                clamp_gain(mod_bc[:, :, 0, :], 1)
                clamp_gain(gb_bc[:, :, :], 5)
                V.tensor_scalar(mod_bc[:, :, 2, :], mod_bc[:, :, 2, :], 1.0, SX, ALU.add, ALU.mult).then_inc(mod_ready, 1)
                V.tensor_scalar(mod_bc[:, :, 1, :], mod_bc[:, :, 1, :], SX, None, ALU.mult).then_inc(mod_ready, 1)

            def moments(src, w, t, s_stats, s_agg, s_var, mvt, sd):
                for j in range(TPB):
                    V.bn_stats(stats[:, w, j, :], src[:, j, :]).then_inc(s_stats, 1)
                dve.wait_ge(s_stats, TPB * (t + 1))
                for j in range(TPB):
                    V.bn_aggr(mvt[:, j, :], stats[:, w, j, :]).then_inc(s_agg, 1)
                dve.wait_ge(s_agg, TPB * (t + 1))
                V.tensor_scalar(sd, mvt[:, :, 1], EPS_LN, None, ALU.add).then_inc(s_var, 1)

            def ln1_moments(t):
                dve.wait_ge(x_in[t % XS], 16 * (t // XS + 1))
                moments(x_sb[:, t % XS], 0, t, ln1_stats, ln1_agg, ln1_var, mv1[:, t % 2], rstd[:, t % 2, :])

            def ln1_rows(t):
                dve.wait_ge(ln1_std, t + 1)
                V.reciprocal(rstd[:, t % 2, :], rstd[:, t % 2, :]).then_inc(ln1_rstd, 1)
                dve.wait_ge(ln1_rstd, t + 1)
                if t >= 1:
                    dve.wait_ge(tp_done, KD * t)
                for j in range(TPB):
                    V.tensor_scalar(n_sb[:, j, :], x_sb[:, t % XS, j, :], mv1[:, t % 2, j, 0:1],
                                    rstd[:, t % 2, j:j + 1], ALU.subtract, ALU.mult).then_inc(n_ready, 1)

            def nyquist_units(t):
                dve.wait_ge(nymm, t + 1)
                V.tensor_tensor(ny, rot(("ny", t, 0))[:, 0:3 * TPB].rearrange("p (j c) -> p j c", j=TPB),
                                bias_f[:, 6:9].unsqueeze(1).to_broadcast([P, TPB, 3]), ALU.add).then_inc(ny_read, 1)
                dve.wait_ge(ny_read, t + 1)
                V.scalar_tensor_tensor(out=ny_abs, in0=ny, scalar=-1.0, in1=ny, op0=ALU.mult,
                                       op1=ALU.max).then_inc(ny_absd, 1)
                dve.wait_ge(ny_absd, 2 * t + 1)
                V.tensor_scalar(ny_abs, ny_abs, EPS_UNIT, None, ALU.add).then_inc(ny_absd, 1)
                dve.wait_ge(ny_absd, 2 * t + 2)
                V.reciprocal(ny_abs, ny_abs).then_inc(ny_rec, 1)
                dve.wait_ge(ny_rec, t + 1)
                V.tensor_tensor(ny_unit, ny, ny_abs, ALU.mult).then_inc(ny_unitd, 1)
                dve.wait_ge(ny_unitd, t + 1)
                V.tensor_tensor(ny_kv, ny_unit[:, :, KEY], ny_unit[:, :, VAL], ALU.mult).then_inc(ny_kvd, 1)

            def nyquist_apply(t):
                dve.wait_ge(pre_mm, t + 1)
                if t % 2 == 0:
                    V.memset(ny_tot[:, 0, 0:1], 0.0).then_inc(tot_read, 1)
                else:
                    V.tensor_copy(ny_tot[:, 1, 0:1], ny_tot[:, 0, TPB:TPB + 1]).then_inc(tot_read, 1)
                V.tensor_copy(ny_pre, rot(("pre", t, 0))[:, 0:TPB]).then_inc(ny_sum, 1)
                dve.wait_ge(tot_read, 2 * t + 1)
                s = t % 2
                V.tensor_tensor_scan(ny_tot[:, s, 1:TPB + 1], rot(("pre", t, 0))[:, TPB:2 * TPB],
                                     ny_unit[:, :, QRY], ny_tot[:, s, 0:1], ALU.add, ALU.bypass).then_inc(tot_read, 1)
                dve.wait_ge(tot_read, 2 * t + 2)
                dve.wait_ge(ny_sum, 2 * t + 1)
                V.tensor_tensor(ny_pre, ny_pre, ny_tot[:, s, 0:TPB], ALU.add).then_inc(ny_sum, 1)
                dve.wait_ge(ny_sum, 2 * t + 2)
                V.tensor_tensor(ny_g, ny_pre, ny_unit[:, :, QRY], ALU.mult).then_inc(ny_done, 1)

            def bind(t):
                s = t % 2
                dve.wait_ge(root_ready, t + 1)
                V.tensor_scalar(mag[:, s], mag[:, s], EPS_UNIT, None, ALU.add).then_inc(eps_ready, 1)
                dve.wait_ge(eps_ready, t + 1)
                V.tensor_tensor(den, mag[:, s, KEY, :], mag[:, s, VAL, :], ALU.mult).then_inc(den_ready, 1)
                dve.wait_ge(den_ready, t + 1)
                V.tensor_tensor(rec, den, mag[:, s, QRY, :], ALU.mult).then_inc(all_ready, 1)
                dve.wait_ge(all_ready, t + 1)
                V.reciprocal(rec, rec).then_inc(rec_ready, 1)
                dve.wait_ge(rec_ready, t + 1)
                V.tensor_tensor(mag[:, s, KEY, :], rec, mag[:, s, QRY, :], ALU.mult).then_inc(rkv_ready, 1)
                dve.wait_ge(rkv_ready, t + 1)
                V.tensor_tensor(mag[:, s, QRY, :], rec, den, ALU.mult).then_inc(rq_ready, 1)
                V.tensor_tensor(uk, z[:, s, KEY], mag[:, s, KEY, :].unsqueeze(1).to_broadcast([P, 2, BLK]),
                                ALU.mult).then_inc(uk_ready, 1)
                dve.wait_ge(uk_ready, t + 1)
                if t >= 1:
                    dve.wait_ge(idft_done, t)
                for a in range(2):
                    V.tensor_tensor(prod[:, a], z[:, s, VAL], uk[:, a, :].unsqueeze(1).to_broadcast([P, 2, BLK]),
                                    ALU.mult).then_inc(prod_ready, 1)
                dve.wait_ge(prod_ready, 2 * t + 2)
                if t >= 2:
                    dve.wait_ge(x1_ready, 2 * (t - 1))
                first = t % 2 == 0
                V.tensor_tensor_scan(s_run[:, s, RE, :], prod[:, 0, RE, :], prod[:, 1, IM, :],
                                     0.0 if first else s_run[:, 1 - s, RE, BLK - 1:BLK],
                                     ALU.add, ALU.subtract).then_inc(scan_ready, 1)
                V.tensor_tensor_scan(s_run[:, s, IM, :], prod[:, 0, IM, :], prod[:, 1, RE, :],
                                     0.0 if first else s_run[:, 1 - s, IM, BLK - 1:BLK],
                                     ALU.add, ALU.add).then_inc(scan_ready, 1)

            def unbind(t):
                dve.wait_ge(x1_ready, 2 * (t + 1))
                V.tensor_tensor(prod[:, 0, RE, :], prod[:, 0, RE, :], prod[:, 1, IM, :], ALU.add).then_inc(g_ready, 1)
                V.tensor_tensor(prod[:, 0, IM, :], prod[:, 1, RE, :], prod[:, 0, IM, :], ALU.subtract).then_inc(g_ready, 1)

            def residual(t):
                dve.wait_ge(idft_done, t + 1)
                if t >= 1:
                    dve.wait_ge(h2_lo, t)
                V.tensor_tensor(x2, ps[:, OUT:OUT + 2, :].rearrange("p a (j d) -> p (a j) d", d=D),
                                x_sb[:, t % XS], ALU.add).then_inc(x2_ready, 1)
                dve.wait_ge(x2_ready, t + 1)
                moments(x2, 1, t, ln2_stats, ln2_agg, ln2_var, mv[:, 1], rstd[:, 2, :])

            def ln2_rows(t):
                b = t // 2
                dve.wait_ge(ln2_std, t + 1)
                V.reciprocal(rstd[:, 2, :], rstd[:, 2, :]).then_inc(ln2_rstd, 1)
                dve.wait_ge(x2_out, 16 * (t + 1))
                for j in range(TPB):
                    V.scalar_tensor_tensor(out=x2[:, j, :], in0=x2[:, j, :], scalar=mv[:, 1, j, 0:1],
                                           in1=mod_bc[:, b, 2, :], op0=ALU.subtract, op1=ALU.mult).then_inc(h2_mid, 1)
                dve.wait_ge(ln2_rstd, t + 1)
                for j in range(TPB):
                    dve.wait_ge(h2_mid, TPB * t + j + 1)
                    V.scalar_tensor_tensor(out=x2[:, j, :], in0=x2[:, j, :], scalar=rstd[:, 2, j:j + 1],
                                           in1=mod_bc[:, b, 1, :], op0=ALU.mult, op1=ALU.add).then_inc(h2_ready, 1)

            ln1_moments(0)
            ln1_moments(1)
            ln1_rows(0)
            modulation()
            for t in range(-1, NBLK + 1):
                if 0 <= t < NBLK:
                    nyquist_units(t)
                    bind(t)
                if t >= 1:
                    residual(t - 1)
                if t >= 0 and t + 2 < NBLK:
                    ln1_moments(t + 2)
                if 0 <= t < NBLK:
                    nyquist_apply(t)
                    unbind(t)
                if t == -1:
                    ln1_rows(1)
                if t >= 0 and t + 2 < NBLK:
                    ln1_rows(t + 2)
                if t >= 1:
                    if t == 1:
                        dve.wait_ge(mod_ready, 11)
                    ln2_rows(t - 1)

            steps = [0]

            def step(ins):
                steps[0] += 1
                ins.then_inc(route, 1)
                dve.wait_ge(route, steps[0])

            dve.wait_ge(gate_ready, NBLK)
            dve.wait_ge(idft_done, NBLK)
            dve.wait_ge(h2_out, 16 * NBLK)
            dve.wait_ge(tp2_done, KD * NBLK)
            dve.wait_ge(iota_in, 16)
            for t in range(TILES):
                ins = V.max(best[:, t, :], gates[:, t, :])
            step(ins)
            for t in range(TILES):
                ins = V.max_index(best_i[:, t, :], best[:, t, :], gates[:, t, :])
            step(ins)
            V.tensor_tensor(pw_tmp[:, 0, :], best[:, :, 1], best[:, :, 0], ALU.subtract).then_inc(w_sub, 1)
            step(V.tensor_copy(pick[:].rearrange("p (k t) -> p k t", k=TOP_K),
                               best_i[:, :, 0:TOP_K].rearrange("p t k -> p k t")))
            step(V.tensor_tensor(onehot, pick[:].unsqueeze(2).to_broadcast([P, PCOLS, EXPERTS]),
                                 iota_sb[:, 0:EXPERTS].unsqueeze(1).to_broadcast([P, PCOLS, EXPERTS]), ALU.is_equal))
            step(V.tensor_scalar(strict_f, iota_sb, pcol, None, ALU.is_gt))
            step(V.tensor_copy(tri_b[:, 0, :], strict_f))
            step(V.memset(tri_b[:, 1, :], 1.0))
            V.tensor_copy(onehot_b, onehot.rearrange("p c e -> p (c e)")).then_inc(cast_done, 1)
            dve.wait_ge(rank_mm, 1)
            step(V.tensor_copy(rank, ps[:, 0, :]))
            step(V.tensor_copy(tot.rearrange("p c e -> p (c e)"), ps[:, 1, :]))
            step(V.memset(cum[:, :, 0:1], 0.0))
            for e in range(EXPERTS):
                ins = V.tensor_tensor_scan(cum[:, e, 1:PCOLS + 1], tot[:, :, e], tot[:, :, e], 0.0,
                                           ALU.add, ALU.bypass)
            step(ins)
            step(V.tensor_scalar(small[:, 0, :].bitcast(I32), cum[:, :, PCOLS], float(P - 1), None, ALU.add))
            step(V.tensor_scalar(small[:, 1, :].bitcast(I32), small[:, 0, :].bitcast(I32), 7, None,
                                 ALU.logical_shift_right))
            step(V.tensor_copy(small[:, 2, :], small[:, 1, :].bitcast(I32)))
            step(V.tensor_tensor_scan(small[:, 3, :], small[:, 2, :], small[:, 2, :], 0.0, ALU.add, ALU.bypass))
            step(V.tensor_tensor(small[:, 4, :], small[:, 3, :], small[:, 2, :], ALU.subtract))
            step(V.tensor_scalar(small[:, 5, :], small[:, 4, :], float(P), None, ALU.mult))
            rank_v = rank.rearrange("p (c e) -> p c e", e=EXPERTS)
            step(V.tensor_tensor(rank_v, rank_v, cum[:, :, 0:PCOLS].rearrange("p e c -> p c e"), ALU.add))
            step(V.tensor_tensor(rank_v, rank_v, small[:, 5, :].unsqueeze(1).to_broadcast([P, PCOLS, EXPERTS]),
                                 ALU.add))
            step(V.tensor_tensor(rank_v, rank_v, onehot, ALU.mult))
            step(V.tensor_reduce(slot, rank_v, AX_X, ALU.add))
            step(V.tensor_copy(slot_i[:, 0, :], slot))
            step(V.tensor_scalar(slot_i[:, 1, :], slot_i[:, 0, :], 7, None, ALU.logical_shift_right))
            step(V.tensor_copy(slot_hl[:, 1, :], slot_i[:, 1, :]))
            step(V.scalar_tensor_tensor(out=slot_hl[:, 0, :], in0=slot_hl[:, 1, :], scalar=-float(P), in1=slot,
                                        op0=ALU.mult, op1=ALU.add))
            step(V.tensor_scalar(small[:, 6, 0:1], pcol, 1.0, None, ALU.add))
            step(V.tensor_scalar(pair_no, iota_sb[:, 0:PCOLS], float(P), None, ALU.mult))
            step(V.tensor_scalar(pair_no, pair_no, small[:, 6, 0:1], None, ALU.add))
            for c in range(PCOLS):
                g = c // GRP % 2
                if c % GRP == 0:
                    if c >= 2 * GRP:
                        dve.wait_ge(perm_mm, c - GRP)
                    V.tensor_tensor(lo_hot[:, g], iota_sb.unsqueeze(1).to_broadcast([P, GRP, P]),
                                    slot_hl[:, 0, c:c + GRP].unsqueeze(2).to_broadcast([P, GRP, P]), ALU.is_equal)
                V.tensor_scalar(hi_hot[:, g, c % GRP, :], iota_sb[:, 0:MOE_TILES], slot_hl[:, 1, c:c + 1],
                                pair_no[:, c:c + 1], ALU.is_equal, ALU.mult).then_inc(hi_made, 1)
            step(V.tensor_tensor(te_cmp, iota_sb[:, 0:MOE_TILES].unsqueeze(2).to_broadcast([P, MOE_TILES, EXPERTS]),
                                 small[:, 3, :].unsqueeze(1).to_broadcast([P, MOE_TILES, EXPERTS]), ALU.is_ge))
            step(V.tensor_reduce(perm[:, 3, :], te_cmp, AX_X, ALU.add))
            V.tensor_scalar(tile_expert, perm[:, 3, :], float(EXPERTS - 1), None, ALU.min).then_inc(tiles_ready, 1)
            dve.wait_ge(w_exp, 1)
            step(V.tensor_scalar(pw_tmp[:, 0, :], pw_tmp[:, 1, :], 1.0, None, ALU.add))
            step(V.reciprocal(pair_w[:, 0, :], pw_tmp[:, 0, :]))
            V.tensor_tensor(pair_w[:, 1, :], pair_w[:, 0, :], pw_tmp[:, 1, :], ALU.mult).then_inc(tiles_ready, 1)
            dve.wait_ge(perm_mm, PCOLS)
            step(V.tensor_copy(perm[:, 0, :], ps[:, 2, 0:MOE_TILES]))
            step(V.tensor_scalar(perm[:, 1, :], perm[:, 0, :], 0.0, float(PAIRS + 1), ALU.is_equal, ALU.mult))
            V.scalar_tensor_tensor(out=scatter_idx, in0=perm[:, 0, :], scalar=-1.0, in1=perm[:, 1, :],
                                   op0=ALU.add, op1=ALU.add).then_inc(tiles_ready, 1)
            step(V.tensor_scalar(perm[:, 2, :], perm[:, 0, :], float(TOKENS + 1), -float(TOKENS), ALU.is_ge, ALU.mult))
            step(V.scalar_tensor_tensor(out=perm[:, 1, :], in0=perm[:, 0, :], scalar=-1.0, in1=perm[:, 2, :],
                                        op0=ALU.add, op1=ALU.add))
            V.tensor_scalar(gather_idx, perm[:, 1, :], 0.0, None, ALU.max).then_inc(tiles_ready, 1)

            dve.wait_ge(tiles_ready, 4)
            dve.wait_ge(bias_in, 16 * (EXPERTS + 1))

            def expert(i):
                return dve.value_load(tile_expert[0:1, bass.ds(i, 1)], min_val=0, max_val=EXPERTS - 1)

            def biased(i, s):
                e = expert(i)
                dve.wait_ge(up_done, i + 1)
                V.scalar_tensor_tensor(out=gv[:, s].rearrange("p a f -> p (a f)"),
                                       in0=ps[:, 4 + 2 * s:6 + 2 * s, :].rearrange("p a f -> p (a f)"),
                                       scalar=1.0 / (SX * SW), in1=b1_bc[:, bass.ds(e * (2 * HID), 2 * HID)],
                                       op0=ALU.mult, op1=ALU.add).then_inc(gv_ready, 1)
                dve.wait_ge(gv_ready, i + 1)
                V.tensor_scalar(gv[:, s, 0, :], gv[:, s, 0, :], LIMIT, None, ALU.min).then_inc(clip_done, 1)
                V.tensor_scalar(gv[:, s, 1, :], gv[:, s, 1, :], LIMIT, -LIMIT, ALU.min, ALU.max).then_inc(vclip_done, 1)

            def rows_out(i, s):
                e = expert(i)
                dve.wait_ge(down_done, i + 1)
                V.scalar_tensor_tensor(out=y_sb[:, s, :], in0=ps[:, 2 + s, 0:D], scalar=1.0 / (SH * SW),
                                       in1=b2_bc[:, bass.ds(e * D, D)], op0=ALU.mult, op1=ALU.add).then_inc(y_ready, 1)

            def turn(i, s, more, out_wait):
                dve.wait_ge(sig_ready, i + 1)
                V.tensor_tensor(gv[:, s, 0, :], gv[:, s, 0, :], sig[:, s, :], ALU.mult).then_inc(gsig_ready, 1)
                dve.wait_ge(gsig_ready, i + 1)
                dve.wait_ge(vclip_done, i + 1)
                V.scalar_tensor_tensor(out=gv[:, s, 0, :], in0=gv[:, s, 1, :], scalar=1.0, in1=gv[:, s, 0, :],
                                       op0=ALU.add, op1=ALU.mult).then_inc(glu_ready, 1)
                if more:
                    biased(i + 1, 1 - s)
                dve.wait_ge(hid_hi, i + 1)
                V.scalar_tensor_tensor(out=hid[:, s, LO, :], in0=gv[:, s, 0, :], scalar=SH, in1=hid[:, s, HI, :],
                                       op0=ALU.mult, op1=ALU.subtract).then_inc(hid_ready, 1)
                if out_wait is not None:
                    if out_wait is not False:
                        dve.wait_ge(scattered[1 - s], out_wait)
                    rows_out(i - 1, 1 - s)

            biased(0, 0)
            turn(0, 0, True, None)
            turn(1, 1, True, False)
            turn(2, 0, True, False)
            turn(3, 1, True, 16)
            with dve.Fori(2, LOOP_END // 2) as n:
                turn(2 * n, 0, True, 16 * (n - 1))
                turn(2 * n + 1, 1, True, 16 * n)
            turn(LOOP_END, 0, True, 16 * (LOOP_END // 2 - 1))
            turn(LOOP_END + 1, 1, True, 16 * (LOOP_END // 2))
            turn(LOOP_END + 2, 0, False, 16 * (LOOP_END // 2))
            dve.wait_ge(scattered[0], 16 * (LOOP_END // 2 + 1))
            rows_out(MOE_TILES - 1, 0)

            for t in range(NBLK):
                for j in range(TPB):
                    n = t * TPB + j
                    dve.wait_ge(d_w1, n + 1)
                    V.scalar_tensor_tensor(out=d_y[:, t, 0, j, :], in0=d_y[:, t, 1, j, :],
                                           scalar=pair_w[:, 1, n:n + 1], in1=d_y[:, t, 0, j, :],
                                           op0=ALU.mult, op1=ALU.add).then_inc(d_w2, 1)
                dve.wait_ge(d_w2, TPB * (t + 1))
                V.tensor_tensor(d_y[:, t, 0], d_y[:, t, 0], gb_bc[:, t // 2, :].unsqueeze(1).to_broadcast([P, TPB, D]),
                                ALU.mult).then_inc(d_gb, 1)
                dve.wait_ge(d_gb, t + 1)
                if t == 0:
                    dve.wait_ge(x2_in, 16 * NBLK)
                V.tensor_tensor(d_x[:, t], d_y[:, t, 0], d_x[:, t], ALU.add).then_inc(d_ready, 1)

        @block.gpsimd
        def _(pool):
            G = nc.gpsimd
            def low_weights(n):
                pool.wait_ge(w_hi, n + 1)
                hi, lo = parts_of(n)
                G.tensor_tensor(lo, w_stage[:, n % 2, :], hi, ALU.subtract).then_inc(w_lo, 1)

            def magnitudes(t):
                pool.wait_ge(sq_ready, 3 * (t + 1))
                G.tensor_tensor(mag[:, t % 2], sq[:, :, RE, :], sq[:, :, IM, :], ALU.add).then_inc(mag_ready, 1)

            def low_rows(t):
                pool.wait_ge(h2_hi, t + 1)
                G.tensor_tensor(h2_parts[:, :, LO, :], x2, h2_parts[:, :, HI, :], ALU.subtract).then_inc(h2_lo, 1)

            magnitudes(0)
            pool.wait_ge(mod_ready, 11)
            for t in range(NBLK):
                s, b = t % 2, t // 2
                if s == 0:
                    if b >= 2:
                        pool.wait_ge(idft_done, 2 * (b - 1))
                    for r in range(2):
                        ins = G.tensor_tensor(idft_ga[:, b % 2, r, :], idft_sb[:, r, :], mod_bc[:, b, 0, :], ALU.mult)
                    ins.then_inc(ga_ready, 1)
                pool.wait_ge(rq_ready, t + 1)
                for r in range(2):
                    ins = G.tensor_tensor(z[:, s, QRY, r, :], z[:, s, QRY, r, :], mag[:, s, QRY, :], ALU.mult)
                ins.then_inc(uq_ready, 1)
                pool.wait_ge(uq_ready, t + 1)
                pool.wait_ge(scan_ready, 2 * (t + 1))
                for a in range(2):
                    for r in range(2):
                        ins = G.tensor_tensor(prod[:, a, r, :], s_run[:, s, a, :], z[:, s, QRY, r, :], ALU.mult)
                    ins.then_inc(x1_ready, 1)
                if t + 1 < NBLK:
                    magnitudes(t + 1)
                low_weights(2 * t)
                low_weights(2 * t + 1)
                if t >= 1:
                    low_rows(t - 1)
            low_rows(NBLK - 1)
            for n in range(2 * NBLK, W_CHUNKS):
                low_weights(n)

            def wait_turn(signal, value):
                pool.wait_ge(signal, value)
                pool.sem_inc(pool_turn, 1)

            def gather(i, s):
                G.tensor_copy(gather_now[:, s:s + 1], gather_idx[:, bass.ds(i, 1)]).then_inc(gather_set, 1)
                wait_turn(gather_set, i + 1)
                G.indirect_dma_start(out=xg[:, s, :], out_offset=None, in_=h_scratch,
                                     in_offset=bass.IndirectOffsetOnAxis(ap=gather_now[:, s:s + 1], axis=0)
                                     ).then_inc(gathered[s], 16)

            def scatter(i, s):
                wait_turn(y_ready, i + 1)
                G.tensor_copy(scatter_now[:, s:s + 1], scatter_idx[:, bass.ds(i, 1)]).then_inc(scatter_set, 1)
                wait_turn(scatter_set, i + 1)
                G.indirect_dma_start(out=y_scratch,
                                     out_offset=bass.IndirectOffsetOnAxis(ap=scatter_now[:, s:s + 1], axis=0),
                                     in_=y_sb[:, s, :], in_offset=None, bounds_check=PAIRS - 1,
                                     oob_is_err=False).then_inc(scattered[s], 16)

            def next_rows(i, s):
                wait_turn(xg_tp, i - 1)
                gather(i, s)

            pool.wait_ge(tiles_ready, 4)
            gather(0, 0)
            gather(1, 1)
            next_rows(2, 0)
            next_rows(3, 1)
            for i in range(4, 6):
                next_rows(i, i % 2)
            with pool.Fori(1, MOE_TILES // 2 - 2) as n:
                for s in range(2):
                    scatter(2 * n + s - 2, s)
                    next_rows(2 * n + s + 4, s)
            for m in range(MOE_TILES - 5, MOE_TILES):
                scatter(m - 2, m % 2)
                if m + 4 < MOE_TILES:
                    next_rows(m + 4, m % 2)
            scatter(MOE_TILES - 2, 1)
            scatter(MOE_TILES - 1, 0)


def constants():
    f32 = np.float32
    e, k = np.arange(D), np.arange(P)
    turn = 2.0 * np.pi * ((e[:, None] * k[None, :]) % D) / D
    alt = np.where(e % 2 == 0, 1.0, -1.0)
    dft = np.concatenate([np.cos(turn), -np.sin(turn), alt[:, None]], axis=1).astype(f32)
    inv_re = np.cos(turn).T * np.where(k == 0, 1.0, 2.0)[:, None] / D
    inv_im = -np.sin(turn).T * 2.0 / D
    inv_im[0] = alt / D
    idft = np.stack([inv_re, inv_im], axis=1).astype(f32)
    i = np.arange(P)
    tri = np.zeros((P, 4, P), f32)
    tri[:, 0] = i[:, None] <= i[None, :]
    tri[:, 1] = 1.0
    tri[:, 3] = alt[:P, None]
    iota = np.concatenate([np.broadcast_to(i, (P, P)), i[:, None]], axis=1).astype(f32)
    return {"dft": dft.reshape(KD, P, -1).transpose(1, 0, 2), "idft": idft, "ident": np.eye(P, dtype=f32),
            "tri": tri, "iota": iota}


def kernel(L0_attn_x, L0_attn_Wq, L0_attn_bq, L0_attn_Wk, L0_attn_bk, L0_attn_Wv, L0_attn_bv, L0_ffn_gate_w,
           L0_ffn_dense_1_w, L0_ffn_dense_1_b, L0_ffn_dense_2_w, L0_ffn_dense_2_b, L0_c, L0_wmod):
    import concourse.bacc as bacc
    from concourse.bass_utils import run_bass_kernel_spmd

    def rows(a):
        a = np.asarray(a)
        return a.reshape(-1, P, a.shape[-1]).transpose(1, 0, 2)

    w1 = np.asarray(L0_ffn_dense_1_w).reshape(EXPERTS, HID, 2, KD, P)
    w2 = np.asarray(L0_ffn_dense_2_w).reshape(EXPERTS, D, KF, P)
    arrays = {
        "x": np.asarray(L0_attn_x).reshape(TOKENS, D),
        "wqkv": np.stack([rows(w) for w in (L0_attn_Wk, L0_attn_Wv, L0_attn_Wq)], axis=1),
        "bqkv": np.stack([np.asarray(b).reshape(KD, P).T for b in (L0_attn_bk, L0_attn_bv, L0_attn_bq)], axis=2),
        "gate_w": rows(L0_ffn_gate_w),
        "w1": w1.transpose(4, 0, 3, 2, 1).reshape(P, -1),
        "b1": np.asarray(L0_ffn_dense_1_b).reshape(EXPERTS, HID, 2).transpose(0, 2, 1).reshape(-1),
        "w2": w2.transpose(3, 0, 2, 1).reshape(P, -1),
        "b2": np.asarray(L0_ffn_dense_2_b).reshape(-1),
        "c_t": rows(np.asarray(L0_c).T),
        "wmod": rows(L0_wmod),
        **constants(),
    }
    nc = bacc.Bacc("TRN2", target_bir_lowering=False, num_devices=1)
    feed, args = {}, {}
    for name, a in arrays.items():
        a = np.ascontiguousarray(a)
        feed[f"in_{name}"] = a
        args[name] = nc.dram_tensor(f"in_{name}", a.shape, mybir.dt.from_np(a.dtype), kind="ExternalInput").ap()
    out = nc.dram_tensor("out_rows", (TOKENS, D), F32, kind="ExternalOutput").ap()
    adaln_moe_kernel(nc, **args, out=out)
    r = run_bass_kernel_spmd(nc, [feed], core_ids=[0])
    return r.results[0]["out_rows"].reshape(BATCH, SEQ, D)
```
